# Optimizing a Trainium2 kernel written in Bass

```python
import numpy as np
import jax
import jax.numpy as jnp

def _softmax(x, axis=-1):
    return jax.nn.softmax(x, axis=axis)

def _gelu(x):
    return jax.nn.gelu(x, approximate=True)

def _silu(x):
    return jax.nn.silu(x)

def _sigmoid(x):
    return jax.nn.sigmoid(x)

def _layernorm(x, axis=-1, eps=1e-05):
    m = jnp.mean(x, axis=axis, keepdims=True)
    v = jnp.var(x, axis=axis, keepdims=True)
    return (x - m) / jnp.sqrt(v + eps)

def _scatter_add(tgt, idx, src, axis=0):
    return tgt.at[idx].add(src)

def _segment_sum(src, seg, n):
    return jax.ops.segment_sum(src, seg, n)
kernel_name = 'mk_adaln_d1_jaxref_r4_9f3fa3'

def setup_inputs(seed: int=0):
    np.random.seed(seed)
    _w = jnp.asarray

    def _L0_attn_setup():
        import jax, jax.numpy as jnp
        import numpy as np
        DIM = 256
        HID = 1024
        NUM_HEADS = 4
        WINDOW = 128
        NUM_PM = 64
        NEG = -1e+30

        def _swa(x_in, wq, wk, wv, wo):
            B, S, D = x_in.shape
            h, dh = (NUM_HEADS, D // NUM_HEADS)
            q = (x_in @ wq.T).reshape(B, S, h, dh).transpose(0, 2, 1, 3)
            k = (x_in @ wk.T).reshape(B, S, h, dh).transpose(0, 2, 1, 3)
            v = (x_in @ wv.T).reshape(B, S, h, dh).transpose(0, 2, 1, 3)
            i = jnp.arange(S)[:, None]
            j = jnp.arange(S)[None, :]
            mask = (j <= i) & (j > i - WINDOW)
            logits = jnp.einsum('bhqd,bhkd->bhqk', q, k) / np.sqrt(dh).astype(np.float32)
            logits = jnp.where(mask, logits, NEG)
            attn = jax.nn.softmax(logits, axis=-1)
            out = jnp.einsum('bhqk,bhkd->bhqd', attn, v)
            out = out.transpose(0, 2, 1, 3).reshape(B, S, D)
            return out @ wo.T

        def _mlp(w1, b1, w2, b2, x):
            return jax.nn.silu(x @ w1.T + b1) @ w2.T + b2
        key = jax.random.key(seed)
        ks = jax.random.split(key, 12)
        B, S = (2, 512)
        sc = 0.02
        n = lambda k, shape, s=sc: jax.random.normal(k, shape, jnp.float32) * s
        return {'x': n(ks[0], (B, S, DIM), 1.0), 'mem': n(ks[1], (NUM_PM, DIM), 1.0), 'wq': n(ks[2], (DIM, DIM)), 'wk': n(ks[3], (DIM, DIM)), 'wv': n(ks[4], (DIM, DIM)), 'wo': n(ks[5], (DIM, DIM)), 'w1': n(ks[6], (HID, DIM)), 'b1': jnp.zeros((HID,), jnp.float32), 'w2': n(ks[7], (DIM, HID)), 'b2': jnp.zeros((DIM,), jnp.float32), 'lin1': n(ks[8], (DIM, DIM)), 'lin2': n(ks[9], (DIM, DIM)), 'alpha': jnp.float32(0.0001), 'theta': jnp.float32(0.0001)}
    _L0_attn_in = _L0_attn_setup()

    def _L0_ffn_setup():
        import jax, jax.numpy as jnp
        import numpy as np
        TOPK = 8
        NUM_EXPERTS = 64
        FFN = 768
        CAPACITY = 160

        def _swiglu(x, w1, w2):
            h = x @ w1.T
            x1, x2 = jnp.split(h, 2, axis=-1)
            return x1 * jax.nn.silu(x2) @ w2.T
        key = jax.random.key(seed)
        ks = jax.random.split(key, 6)
        B, S, H = (1, 128, 256)
        scale = 0.02
        return {'hidden_states': jax.random.normal(ks[0], (B, S, H), jnp.float32), 'wg': jax.random.normal(ks[1], (NUM_EXPERTS, H), jnp.float32) * scale, 'shared_w1': jax.random.normal(ks[2], (2 * FFN, H), jnp.float32) * scale, 'shared_w2': jax.random.normal(ks[3], (H, FFN), jnp.float32) * scale, 'expert_w1': jax.random.normal(ks[4], (NUM_EXPERTS, 2 * FFN, H), jnp.float32) * scale, 'expert_w2': jax.random.normal(ks[5], (NUM_EXPERTS, H, FFN), jnp.float32) * scale}
    _L0_ffn_in = _L0_ffn_setup()
    _L0_c = _w((lambda *s: np.random.randn(*s).astype(np.float32) * 0.05)(1, 256))
    _L0_wmod = _w((lambda *s: np.random.randn(*s).astype(np.float32) * 0.05)(256, 6 * 256) * 256 ** (-0.5))
    _d = {'L0_attn_x': _L0_attn_in['x'], 'L0_attn_mem': _L0_attn_in['mem'], 'L0_attn_wq': _L0_attn_in['wq'], 'L0_attn_wk': _L0_attn_in['wk'], 'L0_attn_wv': _L0_attn_in['wv'], 'L0_attn_wo': _L0_attn_in['wo'], 'L0_attn_w1': _L0_attn_in['w1'], 'L0_attn_b1': _L0_attn_in['b1'], 'L0_attn_w2': _L0_attn_in['w2'], 'L0_attn_b2': _L0_attn_in['b2'], 'L0_attn_lin1': _L0_attn_in['lin1'], 'L0_attn_lin2': _L0_attn_in['lin2'], 'L0_attn_alpha': _L0_attn_in['alpha'], 'L0_attn_theta': _L0_attn_in['theta'], 'L0_ffn_wg': _L0_ffn_in['wg'], 'L0_ffn_shared_w1': _L0_ffn_in['shared_w1'], 'L0_ffn_shared_w2': _L0_ffn_in['shared_w2'], 'L0_ffn_expert_w1': _L0_ffn_in['expert_w1'], 'L0_ffn_expert_w2': _L0_ffn_in['expert_w2'], 'L0_c': _L0_c, 'L0_wmod': _L0_wmod}
    _x0 = _d['L0_attn_x']
    _d['L0_attn_x'] = jax.random.normal(jax.random.fold_in(jax.random.key(seed), 1), (1, 4096, 256), dtype=_x0.dtype)
    del _x0
    return _d

def reference(L0_attn_x, L0_attn_mem, L0_attn_wq, L0_attn_wk, L0_attn_wv, L0_attn_wo, L0_attn_w1, L0_attn_b1, L0_attn_w2, L0_attn_b2, L0_attn_lin1, L0_attn_lin2, L0_attn_alpha, L0_attn_theta, L0_ffn_wg, L0_ffn_shared_w1, L0_ffn_shared_w2, L0_ffn_expert_w1, L0_ffn_expert_w2, L0_c, L0_wmod):

    def _L0_attn_ref(x, mem, wq, wk, wv, wo, w1, b1, w2, b2, lin1, lin2, alpha, theta):
        import jax, jax.numpy as jnp
        import numpy as np
        DIM = 256
        HID = 1024
        NUM_HEADS = 4
        WINDOW = 128
        NUM_PM = 64
        NEG = -1e+30

        def _swa(x_in, wq, wk, wv, wo):
            B, S, D = x_in.shape
            h, dh = (NUM_HEADS, D // NUM_HEADS)
            q = (x_in @ wq.T).reshape(B, S, h, dh).transpose(0, 2, 1, 3)
            k = (x_in @ wk.T).reshape(B, S, h, dh).transpose(0, 2, 1, 3)
            v = (x_in @ wv.T).reshape(B, S, h, dh).transpose(0, 2, 1, 3)
            i = jnp.arange(S)[:, None]
            j = jnp.arange(S)[None, :]
            mask = (j <= i) & (j > i - WINDOW)
            logits = jnp.einsum('bhqd,bhkd->bhqk', q, k) / np.sqrt(dh).astype(np.float32)
            logits = jnp.where(mask, logits, NEG)
            attn = jax.nn.softmax(logits, axis=-1)
            out = jnp.einsum('bhqk,bhkd->bhqd', attn, v)
            out = out.transpose(0, 2, 1, 3).reshape(B, S, D)
            return out @ wo.T

        def _mlp(w1, b1, w2, b2, x):
            return jax.nn.silu(x @ w1.T + b1) @ w2.T + b2
        B, S, D = x.shape
        pm = jnp.broadcast_to(mem[None], (B, NUM_PM, D))
        x_in = jnp.concatenate([pm, x], axis=1)
        out_swa = _swa(x_in, wq, wk, wv, wo)
        k_flat = x_in.reshape(-1, D)
        v_flat = out_swa.reshape(-1, D)

        def loss_fn(params):
            pred = _mlp(*params, k_flat)
            return 0.5 * jnp.sum((pred - v_flat) ** 2)
        grads = jax.grad(loss_fn)((w1, b1, w2, b2))
        upd = jax.tree_util.tree_map(lambda p, g: (1.0 - alpha) * p - theta * g, (w1, b1, w2, b2), grads)
        out_mem = _mlp(*upd, k_flat).reshape(x_in.shape)
        g1 = jax.nn.sigmoid(out_swa @ lin1.T)
        g2 = jax.nn.sigmoid(out_mem @ lin2.T)
        out_merged = g1 * out_swa + g2 * out_mem
        return out_merged[:, NUM_PM:, :]

    def _L0_ffn_ref(hidden_states, wg, shared_w1, shared_w2, expert_w1, expert_w2):
        import jax, jax.numpy as jnp
        import numpy as np
        TOPK = 8
        NUM_EXPERTS = 64
        FFN = 768
        CAPACITY = 160

        def _swiglu(x, w1, w2):
            h = x @ w1.T
            x1, x2 = jnp.split(h, 2, axis=-1)
            return x1 * jax.nn.silu(x2) @ w2.T
        B, S, H = hidden_states.shape
        T = B * S
        x = hidden_states.reshape(T, H)
        shared_out = _swiglu(x, shared_w1, shared_w2)
        logits = x.astype(jnp.float32) @ wg.T
        gates = jax.nn.softmax(logits, axis=-1)
        w_topk, idx_topk = jax.lax.top_k(gates, TOPK)
        denom = jnp.maximum(w_topk.sum(-1, keepdims=True), jnp.finfo(jnp.float32).eps)
        w_topk = w_topk / denom
        A = T * TOPK
        flat_e = idx_topk.reshape(A)
        flat_w = w_topk.reshape(A)
        flat_t = jnp.repeat(jnp.arange(T), TOPK)
        order = jnp.argsort(flat_e)
        se, st, sw = (flat_e[order], flat_t[order], flat_w[order])
        counts = jnp.zeros(NUM_EXPERTS, jnp.int32).at[flat_e].add(1)
        starts = jnp.cumsum(counts) - counts
        rank = jnp.arange(A) - starts[se]
        valid = rank < CAPACITY
        buf = jnp.zeros((NUM_EXPERTS, CAPACITY, H), x.dtype).at[se, rank].set(x[st], mode='drop')
        h = jnp.einsum('ech,efh->ecf', buf, expert_w1)
        x1, x2 = jnp.split(h, 2, axis=-1)
        out = jnp.einsum('ecf,ehf->ech', x1 * jax.nn.silu(x2), expert_w2)
        y = out[se, jnp.clip(rank, 0, CAPACITY - 1)]
        y = jnp.where(valid[:, None], y * sw[:, None].astype(y.dtype), 0.0)
        combined = jnp.zeros((T, H), x.dtype).at[st].add(y)
        return (shared_out + combined).reshape(B, S, H)
    x = L0_attn_x
    mod = (_silu(L0_c) @ L0_wmod).reshape(L0_c.shape[0], 6, 1, -1)
    sa, ca, ga, sb, cb, gb = (mod[:, 0], mod[:, 1], mod[:, 2], mod[:, 3], mod[:, 4], mod[:, 5])
    ga = (2 * (ga >= 0) - 1) * jnp.maximum(jnp.abs(ga), 0.25)
    gb = (2 * (gb >= 0) - 1) * jnp.maximum(jnp.abs(gb), 0.25)
    h = _layernorm(x, axis=-1) * (1 + ca) + sa
    x = x + ga * _L0_attn_ref(h, L0_attn_mem, L0_attn_wq, L0_attn_wk, L0_attn_wv, L0_attn_wo, L0_attn_w1, L0_attn_b1, L0_attn_w2, L0_attn_b2, L0_attn_lin1, L0_attn_lin2, L0_attn_alpha, L0_attn_theta)
    h = _layernorm(x, axis=-1) * (1 + cb) + sb
    x = x + gb * _L0_ffn_ref(h, L0_ffn_wg, L0_ffn_shared_w1, L0_ffn_shared_w2, L0_ffn_expert_w1, L0_ffn_expert_w2)
    return x

_drawn_inputs = setup_inputs


def setup_inputs(seed=0):
    import zlib

    import numpy as np

    out = dict(_drawn_inputs(seed))
    spreads = {'L0_attn_b1': (0.0, 0.523), 'L0_attn_b2': (0.0, 0.724)}
    factors = {'L0_attn_mem': 8.0,
     'L0_attn_wq': 8.0,
     'L0_attn_wk': 8.0,
     'L0_attn_wv': 8.0,
     'L0_attn_wo': 8.0,
     'L0_attn_w1': 4.804,
     'L0_attn_w2': 4.613,
     'L0_attn_lin1': 64.0,
     'L0_attn_lin2': 8.0,
     'L0_ffn_wg': 64.0,
     'L0_ffn_shared_w1': 40.708,
     'L0_ffn_shared_w2': 41.822,
     'L0_ffn_expert_w1': 64.0,
     'L0_ffn_expert_w2': 64.0,
     'L0_c': 3.033,
     'L0_wmod': 3.056}
    for name, (base, spread) in spreads.items():
        noise = np.random.default_rng([zlib.crc32(name.encode()), seed]).standard_normal(out[name].shape)
        drawn = base * np.exp(spread * noise) if base else spread * noise
        out[name] = jnp.asarray(drawn.astype(out[name].dtype))
    for name, factor in factors.items():
        out[name] = (out[name] * factor).astype(out[name].dtype)
    return out
```

```python
from contextlib import ExitStack

import concourse.bass as bass
from concourse import mybir

F32 = mybir.dt.float32
BF16 = mybir.dt.bfloat16
I32 = mybir.dt.int32
U32 = mybir.dt.uint32
ALU = mybir.AluOpType
ACT = mybir.ActivationFunctionType
AX = mybir.AxisListType.X

P = 128
D = 256
DC = D // P
HID = 1024
HC = HID // P
HEADS = 4
DH = D // HEADS
MEM = 64
TOKENS = 4096
TILES = TOKENS // P
CH = 512
TPC = CH // P
CHUNKS = TOKENS // CH
E = 64
TOPK = 8
FFN = 768
FC = FFN // P
CAP = 160
CAP_B = CAP - P
ROW = D + 2
NEG = -1e30
EPS = 1e-5
F32_EPS = 1.1920929e-07
OFF_LIST = 20000
HEAD_AT = [0, 2, 1, 3]


def wait_past(engine, sem, value):
    if isinstance(value, int) and value <= 0:
        return
    engine.wait_ge(sem, value)


def wait_apart(engine, sem, value, passed):
    engine.wait_ge(sem, value)
    engine.sem_inc(passed, 1)


def flat(a):
    names = "abcd"[:len(a.shape) - 1]
    return a.rearrange(f"p {' '.join(names)} -> p ({' '.join(names)})")


class Sems:

    def __init__(self, nc, prefix):
        self.nc, self.prefix, self.made = nc, prefix, {}

    def __call__(self, name):
        if name not in self.made:
            self.made[name] = self.nc.alloc_semaphore(self.prefix + name)
        return self.made[name]

    def clear(self):
        self.nc.clear_and_free_semaphores(list(self.made.values()))
        self.nc.all_engine_barrier()


RSQRT_STEPS = 3
RSQRT_OPS = 3 + 3 * RSQRT_STEPS


def inverse_sqrt(dve, done, calls, y, var, t):
    ops = [
        lambda: dve.tensor_scalar(var, var, EPS, None, ALU.add),
        lambda: dve.tensor_scalar(t.bitcast(I32), var.bitcast(I32), 1, None, ALU.logical_shift_right),
        lambda: dve.tensor_scalar(y.bitcast(I32), t.bitcast(I32), -1.0, float(0x5F3759DF), ALU.mult, ALU.add),
    ] + [
        lambda: dve.tensor_tensor(t, y, y, ALU.mult),
        lambda: dve.scalar_tensor_tensor(out=t, in0=t, scalar=-0.5, in1=var, op0=ALU.mult, op1=ALU.mult),
        lambda: dve.scalar_tensor_tensor(out=y, in0=t, scalar=1.5, in1=y, op0=ALU.add, op1=ALU.mult),
    ] * RSQRT_STEPS
    for k, op in enumerate(ops):
        op().then_inc(done, 1)
        dve.wait_ge(done, calls * RSQRT_OPS + k + 1)


def shared_buffers(nc, ctx):
    def sb(name, shape, dt=F32):
        return ctx.enter_context(nc.sbuf_tensor(name, shape, dt))
    return {
        "xT_all": sb("xT_all", [P, DC, TOKENS]),
        "swaT_all": sb("swaT_all", [P, DC, TOKENS]),
        "w1T": sb("w1T", [P, DC, HID]),
        "w2T": sb("w2T", [P, HC, D]),
        "b1c": sb("b1c", [P, HC]),
        "b2c": sb("b2c", [P, DC]),
        "mod": sb("mod", [P, 6, D]),
        "ident": sb("ident", [P, P]),
    }


def memory_stage(nc, T, buf, psum, S):
    with ExitStack() as ctx:
        def sb(name, shape, dt=F32):
            return ctx.enter_context(nc.sbuf_tensor("a_" + name, shape, dt))

        xT_all, swaT_all, w1T, w2T = buf["xT_all"], buf["swaT_all"], buf["w1T"], buf["w2T"]
        mod, ident, b1c, b2c = buf["mod"], buf["ident"], buf["b1c"], buf["b2c"]
        wqkv = sb("wqkv", [P, 3, DC, D])
        woT = sb("woT", [P, DC, D])
        w2n = sb("w2n", [P, DC, HID])
        b1row = sb("b1row", [P, HID])
        alpha = sb("alpha", [P, 1])
        theta = sb("theta", [P, 1])
        keep = sb("keep", [P, 1])
        step = sb("step", [P, 1])
        cond = sb("cond", [P, DC])
        cond_s = sb("cond_s", [P, DC])
        cond_w = sb("cond_w", [P, DC, P])
        wmod = sb("wmod", [P, DC, 6 * D])
        ones = sb("ones", [P, P])
        clamp = sb("clamp", [P, 2, D])
        masks = sb("masks", [P, 4, 2 * P])
        fill = sb("fill", [P, ROW])
        slot_id = sb("slot_id", [P, 2], I32)
        dW1T = sb("dW1T", [P, DC, HID])
        dW2 = sb("dW2", [P, DC, HID])
        dz_sum = sb("dz_sum", [P, HID])
        db1 = sb("db1", [P, HC])
        e_part = sb("e_part", [P, DC])
        db2 = sb("db2", [P, DC])
        x_in = [sb(f"x_in{p}", [P, D]) for p in range(2)]
        stats = sb("stats", [P, 6])
        moments = sb("moments", [P, 2])
        rstd = sb("rstd", [P, 1])
        half = sb("half", [P, 1])
        xn = sb("xn", [P, D])
        xm = [sb(f"xm{p}", [P, D]) for p in range(2)]
        xT = sb("xT", [P, DC, P])
        qT = sb("qT", [P, DC, P])
        kT = sb("kT", [P, DC, 2, P])
        v = sb("v", [P, 2, D])
        logit = sb("logit", [P, HEADS, 2 * P])
        peak = sb("peak", [P, HEADS])
        npeak = sb("npeak", [P, HEADS])
        psums = sb("psums", [P, HEADS])
        prec = sb("prec", [P, HEADS])
        prob = sb("prob", [P, HEADS, 2 * P])
        probT = sb("probT", [P, HEADS, 2, P])
        oT = sb("oT", [P, DC, P])
        swaT = sb("swaT", [P, DC, P])
        zb = sb("zb", [P, HID])
        sg = sb("sg", [P, HID])
        h = [sb(f"h{p}", [P, HID]) for p in range(2)]
        hs = sb("hs", [P, HID])
        gp = sb("gp", [P, HID])
        hT = sb("hT", [P, HC, P])
        eT = sb("eT", [P, DC, P])
        e = sb("e", [P, D])
        dz = sb("dz", [P, HID])

        def bank(b, n=CH):
            return psum[b][:, 0:n]

        def mm(out, lhsT, rhs, first, last):
            return nc.tensor.matmul(out, lhsT, rhs, start=first, stop=last, skip_group_check=True)

        LAST = TILES

        def tiles(eng, body, tail=None):
            body(0, 0)
            body(1, 1)
            body(2, 0)
            with eng.Fori(1, TILES // 2) as i:
                body(i * 2 + 1, 1)
                body(i * 2 + 2, 0)
            if tail:
                tail()

        x_rows = T["x"]
        block = ctx.enter_context(nc.Block())

        @block.sync
        def _(sp):
            sp.dma_start(cond[:], T["c"]).then_inc(S("cond_in"), 16)
            sp.dma_start(wmod[:], T["wmod"]).then_inc(S("wmod_in"), 16)
            sp.dma_start(x_in[0][P - MEM:P, :], T["mem"]).then_inc(S("mem_in"), 16)
            sp.dma_start(x_in[1][:], x_rows[0:P, :]).then_inc(S("x_in1"), 16)
            sp.dma_start(wqkv[:], T["wqkvT"]).then_inc(S("wqkv_in"), 16)
            sp.dma_start(w1T[:], T["w1T"]).then_inc(S("w1_in"), 16)
            sp.dma_start(b1row[:], T["b1row"]).then_inc(S("b1row_in"), 16)
            sp.dma_start(w2T[:], T["w2T"]).then_inc(S("w2T_in"), 16)
            sp.dma_start(woT[:], T["woT"]).then_inc(S("wo_in"), 16)
            sp.dma_start(b2c[:], T["b2c"]).then_inc(S("small_in"), 16)
            sp.dma_start(b1c[:], T["b1c"]).then_inc(S("small_in"), 16)
            sp.dma_start(alpha[:], T["alpha"]).then_inc(S("small_in"), 16)
            sp.dma_start(theta[:], T["theta"]).then_inc(S("small_in"), 16)
            sp.dma_start(w2n[:], T["w2n"]).then_inc(S("w2n_in"), 16)

            def load(n, p, m):
                wait_past(sp, S("xn"), n - 2)
                sp.dma_start(x_in[p][:], x_rows[bass.ds(m * P, P), :]).then_inc(S(f"x_in{p}"), 16)

            sp.wait_ge(S("xm"), 1)
            load(2, 0, 1)
            with sp.Fori(1, TILES // 2) as i:
                load(i * 2 + 1, 1, i * 2)
                load(i * 2 + 2, 0, i * 2 + 1)
            sp.wait_ge(S("fill"), 1)
            slots = T["slots"].rearrange("(e r) d -> r e d", e=E)
            fill_b = fill[:, :].unsqueeze(1).to_broadcast([P, E, ROW])
            sp.dma_start(slots[0:P], fill_b).then_inc(S("slots_out"), 16)
            sp.dma_start(T["out"][TOKENS:TOKENS + P, :], fill[:, 0:D]).then_inc(S("spare_out"), 16)
            sp.dma_start(T["out"][TOKENS + P:TOKENS + CAP, :], fill[0:CAP_B, 0:D]).then_inc(S("spare_out"), 16)
            sp.wait_ge(S("slots_out"), 16)
            sp.wait_ge(S("spare_out"), 32)
            sp.wait_ge(S("fill"), 2)
            sp.dma_start(slots[P:CAP], fill_b[0:CAP_B]).then_inc(S("slots_out"), 16)
            sp.wait_ge(S("slots_out"), 32)

        @block.gpsimd
        def _(pool):
            pool.memset(ident[:], 0.0)
            pool.memset(ones[:], 1.0).then_inc(S("ones"), 1)
            pool.memset(x_in[0][0:P - MEM, :], 0.0)
            pool.memset(kT[:, :, 1, :], 0.0)
            pool.memset(v[:, 1, :], 0.0).then_inc(S("kv_zero"), 1)
            pool.memset(dz_sum[:], 0.0)
            pool.memset(fill[:], 0.0)
            pool.memset(masks[:], 0.0).then_inc(S("zeroed"), 1)
            pool.wait_ge(S("zeroed"), 1)
            pool.affine_select(out=ident[:], in_=ident[:], compare_op=ALU.not_equal, fill=1.0, base=0,
                               pattern=[[-1, P]], channel_multiplier=1).then_inc(S("ident"), 1)
            for m, own in ((0, 0), (1, 1), (2, 0), (3, 1)):
                prev = 1 - own
                a = masks[:, m, own * P:(own + 1) * P]
                pool.affine_select(out=a, in_=a, compare_op=ALU.is_ge, fill=NEG, base=0,
                                   pattern=[[-1, P]], channel_multiplier=1)
                b = masks[:, m, prev * P:(prev + 1) * P]
                pool.affine_select(out=b, in_=b, compare_op=ALU.is_gt, fill=NEG, base=0,
                                   pattern=[[1, P]], channel_multiplier=-1).then_inc(S("banded"), 1)
            pool.wait_ge(S("banded"), 4)
            pool.memset(masks[:, 0, P:2 * P], NEG)
            pool.memset(masks[:, 0, 0:P - MEM], NEG)
            pool.memset(masks[:, 1, 0:P - MEM], NEG).then_inc(S("masks"), 1)
            pool.iota(slot_id[:, 0:1], pattern=[[0, 1]], base=TOKENS, channel_multiplier=1)
            pool.iota(slot_id[:, 1:2], pattern=[[0, 1]], base=TOKENS + P, channel_multiplier=1).then_inc(S("slot_id"), 1)
            pool.wait_ge(S("slot_id"), 1)
            pool.tensor_copy(fill[:, D + 1:D + 2].bitcast(I32), slot_id[:, 0:1]).then_inc(S("fill"), 1)
            pool.wait_ge(S("mem_in"), 16)
            pool.tensor_copy(xm[0][:], x_in[0][:]).then_inc(S("xm"), 1)

            def modulate(n, p):
                pool.wait_ge(S("xn"), n)
                wait_past(pool, S("dW_mm"), 8 * n - 8)
                pool.tensor_tensor(xm[p][:], xn[:], mod[:, 1, :], ALU.mult).then_inc(S("xm_scaled"), 1)
                pool.wait_ge(S("xm_scaled"), n)
                pool.tensor_tensor(xm[p][:], xm[p][:], mod[:, 0, :], ALU.add).then_inc(S("xm"), 1)

            pool.wait_ge(S("mod"), 1)

            def body(n, p, m=None):
                if not isinstance(n, int) or n >= 1:
                    wait_apart(pool, S("xT"), n + 1, S("passed_pool"))
                    pool.tensor_copy(xT_all[:, :, bass.ds((n - 1) * P, P)], xT[:]).then_inc(S("xT_kept"), 1)
                    pool.wait_ge(S("dz"), 2 * n)
                    wait_past(pool, S("dz_sum"), n - 1)
                    pool.tensor_tensor(dz_sum[:], dz_sum[:], dz[:], ALU.add).then_inc(S("dz_sum"), 1)
                pool.wait_ge(S("prec"), n + 1)
                pool.tensor_tensor(prob[:], prob[:], prec[:].unsqueeze(2).to_broadcast([P, HEADS, 2 * P]),
                                   ALU.mult).then_inc(S("prob"), 1)
                pool.wait_ge(S("sg"), n + 1)
                wait_past(pool, S("dW_mm"), 8 * n - 8)
                pool.tensor_tensor(h[p][:], zb[:], sg[:], ALU.mult).then_inc(S("h"), 1)
                pool.wait_ge(S("h"), n + 1)
                pool.tensor_tensor(hs[:], h[p][:], sg[:], ALU.mult).then_inc(S("hs"), 1)
                wait_past(pool, S("dz"), 2 * n)
                pool.tensor_tensor(gp[:], h[p][:], sg[:], ALU.add).then_inc(S("gp_sum"), 1)
                pool.wait_ge(S("gp_sum"), n + 1)
                pool.wait_ge(S("hs"), n + 1)
                pool.tensor_tensor(gp[:], gp[:], hs[:], ALU.subtract).then_inc(S("gp"), 1)

            def keep_swa(n):
                if not isinstance(n, int) or n >= 1:
                    wait_apart(pool, S("swaT"), n + 1, S("passed_pool"))
                    pool.tensor_copy(swaT_all[:, :, bass.ds((n - 1) * P, P)], swaT[:]).then_inc(S("swaT_kept"), 1)

            def with_next(n, p):
                body(n, p)
                modulate(n + 1, 1 - p)
                keep_swa(n)

            with_next(0, 0)
            with_next(1, 1)
            with_next(2, 0)
            with pool.Fori(1, TILES // 2 - 1) as i:
                with_next(i * 2 + 1, 1)
                with_next(i * 2 + 2, 0)
            with_next(LAST - 1, 1)
            body(LAST, 0)
            keep_swa(LAST)
            pool.wait_ge(S("dz"), 2 * LAST + 2)
            pool.wait_ge(S("dz_sum"), LAST)
            pool.tensor_tensor(dz_sum[:], dz_sum[:], dz[:], ALU.add).then_inc(S("dz_sum"), 1)
            pool.wait_ge(S("slots_out"), 16)
            pool.wait_ge(S("spare_out"), 32)
            pool.tensor_copy(fill[:, D + 1:D + 2].bitcast(I32), slot_id[:, 1:2]).then_inc(S("fill"), 1)

        @block.scalar
        def _(act):
            act.wait_ge(S("cond_in"), 16)
            act.activation(cond_s[:], cond[:], ACT.Sigmoid).then_inc(S("cond_s"), 1)

            def body(n, p):
                act.wait_ge(S("xT_mm"), n + 1)
                wait_past(act, S("z_mm"), 2 * n)
                wait_past(act, S("xT_kept"), n - 1)
                act.copy(flat(xT[:]), bank(0, D)).then_inc(S("xT"), 1)
                act.wait_ge(S("v_mm"), n + 1)
                wait_past(act, S("o_mm"), n)
                if isinstance(n, int) and n == 0:
                    act.wait_ge(S("kv_zero"), 1)
                act.copy(v[:, p, :], bank(2, D)).then_inc(S("v"), 1)
                if not isinstance(n, int) or n >= 1:
                    e_rows(n - 1)
                for s in range(HEADS):
                    act.wait_ge(S("npeak"), n + 1)
                    wait_past(act, S("probT_mm"), 2 * n)
                    ins = act.activation(prob[:, s, :], logit[:, s, :], ACT.Exp, bias=npeak[:, s:s + 1],
                                         accum_out=psums[:, s:s + 1])
                ins.then_inc(S("prob_exp"), 1)
                act.wait_ge(S("zb"), 2 * n + 2)
                wait_past(act, S("gp"), n)
                act.activation(sg[:], zb[:], ACT.Sigmoid).then_inc(S("sg"), 1)
                act.wait_ge(S("probT_mm"), 2 * n + 2)
                wait_past(act, S("o_mm"), n)
                act.copy(flat(probT[:, 2:4, :, :]), bank(3)).then_inc(S("probT_hi"), 1)
                for g in range(2):
                    act.wait_ge(S("hT_mm"), 2 * n + g + 1)
                    wait_past(act, S("pred_mm"), n)
                    act.copy(flat(hT[:, 4 * g:4 * g + 4, :]), bank(4 + g)).then_inc(S("hT"), 1)
                act.wait_ge(S("pred_mm"), n + 1)
                wait_past(act, S("eT"), n)
                wait_past(act, S("swaT_kept"), n - 1)
                act.copy(flat(swaT[:]), bank(7, D)).then_inc(S("swaT"), 1)

            def e_rows(m):
                act.wait_ge(S("e_mm"), m + 1)
                wait_past(act, S("dW_mm"), 8 * m)
                act.copy(e[:], bank(3, D)).then_inc(S("e"), 1)

            tiles(act, body, lambda: e_rows(LAST))

        @block.vector
        def _(dve):
            dve.memset(dW1T[:], 0.0)
            dve.memset(dW2[:], 0.0)
            dve.memset(db2[:], 0.0).then_inc(S("d_zero"), 1)
            dve.wait_ge(S("cond_s"), 1)
            dve.tensor_tensor(cond_s[:], cond_s[:], cond[:], ALU.mult).then_inc(S("cond_silu"), 1)
            dve.wait_ge(S("cond_silu"), 1)
            dve.wait_ge(S("ones"), 1)
            for k in range(DC):
                ins = dve.tensor_scalar(cond_w[:, k, :], ones[:], cond_s[:, k:k + 1], None, ALU.mult)
            ins.then_inc(S("cond_w"), 1)
            dve.wait_ge(S("mod_mm"), 1)
            for j in range(3):
                ins = dve.tensor_copy(flat(mod[:, 2 * j:2 * j + 2, :]), bank(j))
            ins.then_inc(S("mod_copied"), 1)
            dve.wait_ge(S("mod_copied"), 1)
            for j in (1, 4):
                dve.tensor_scalar(mod[:, j, :], mod[:, j, :], 1.0, None, ALU.add)
            for j, g in enumerate((2, 5)):
                dve.scalar_tensor_tensor(out=clamp[:, j, :], in0=mod[:, g, :], scalar=-1.0, in1=mod[:, g, :],
                                         op0=ALU.mult, op1=ALU.max).then_inc(S("clamped"), 1)
                dve.wait_ge(S("clamped"), 3 * j + 1)
                dve.tensor_scalar(clamp[:, j, :], clamp[:, j, :], 0.25, None, ALU.max)
                dve.tensor_scalar(mod[:, g, :], mod[:, g, :], 0.0, 2.0, ALU.is_ge, ALU.mult).then_inc(S("clamped"), 1)
                dve.wait_ge(S("clamped"), 3 * j + 2)
                dve.scalar_tensor_tensor(out=mod[:, g, :], in0=mod[:, g, :], scalar=-1.0, in1=clamp[:, j, :],
                                         op0=ALU.add, op1=ALU.mult).then_inc(S("clamped"), 1)
            dve.wait_ge(S("clamped"), 6)
            dve.memset(peak[:], 0.0).then_inc(S("mod"), 1)
            dve.wait_ge(S("mod"), 1)
            dve.wait_ge(S("small_in"), 64)
            dve.tensor_scalar(keep[:], alpha[:], -1.0, 1.0, ALU.mult, ALU.add)
            dve.tensor_scalar(step[:], theta[:], -1.0, None, ALU.mult).then_inc(S("rates"), 1)
            dve.wait_ge(S("b1row_in"), 16)
            dve.wait_ge(S("masks"), 1)

            def normalise(n, p, loads):
                dve.wait_ge(S(f"x_in{p}"), loads * 16)
                dve.bn_stats(stats[:], x_in[p][:]).then_inc(S("stats"), 1)
                wait_apart(dve, S("stats"), n, S("passed_dve"))
                dve.bn_aggr(moments[:], stats[:]).then_inc(S("moments"), 1)
                dve.wait_ge(S("moments"), n)
                inverse_sqrt(dve, S("rstd"), n - 1, rstd[:], moments[:, 1:2], half[:])
                wait_past(dve, S("xm_scaled"), n - 1)
                dve.tensor_scalar(xn[:], x_in[p][:], moments[:, 0:1], rstd[:, 0:1], ALU.subtract, ALU.mult)\
                   .then_inc(S("xn"), 1)

            def grad_z(m):
                dve.wait_ge(S("gp"), m + 1)
                wait_past(dve, S("dW_mm"), 8 * m)
                wait_past(dve, S("dz_sum"), m)
                for g in range(2):
                    dve.wait_ge(S("dh_mm"), 2 * m + g + 1)
                    dve.tensor_tensor(dz[:, g * CH:(g + 1) * CH], bank(4 + g), gp[:, g * CH:(g + 1) * CH],
                                      ALU.mult).then_inc(S("dz"), 1)

            def gather_dW(m):
                for j in range(8):
                    into = dW1T if j < 4 else dW2
                    part = into[:, (j % 4) // 2, (j % 2) * CH:(j % 2 + 1) * CH]
                    dve.wait_ge(S("dW_mm"), 8 * m + j + 1)
                    wait_past(dve, S("dW"), 8 * m + j - 7)
                    dve.tensor_tensor(part, part, bank((2 + j) % 8), ALU.add).then_inc(S("dW"), 1)

            def body(n, p, mask, loads):
                dve.wait_ge(S("qk_mm"), n + 1)
                wait_past(dve, S("s_mm"), 2 * n)
                dve.tensor_copy(flat(qT[:]), bank(1, D))
                if isinstance(n, int) and n == 0:
                    dve.wait_ge(S("kv_zero"), 1)
                dve.tensor_copy(kT[:, :, p, :], psum[1][:, D:2 * D].rearrange("p (c t) -> p c t", c=DC))\
                   .then_inc(S("qk"), 1)
                if not isinstance(n, int) or n >= 1:
                    grad_z(n - 1)
                for s in range(HEADS):
                    wait_past(dve, S("prob_exp"), n)
                    wait_apart(dve, S("s_mm"), 2 * n + s // 2 + 1, S("passed_dve"))
                    ins = dve.tensor_tensor_reduce(
                        out=logit[:, s, :], in0=psum[6 + s // 2][:, (s % 2) * D:(s % 2 + 1) * D], in1=masks[:, mask, :],
                        scale=float(DH) ** -0.5, scalar=-3e38, op0=ALU.add, op1=ALU.max, accum_out=peak[:, s:s + 1])
                    if s % 2:
                        ins.then_inc(S("peak"), 1)
                dve.wait_ge(S("peak"), 2 * n + 2)
                dve.tensor_scalar(npeak[:], peak[:], -1.0, None, ALU.mult).then_inc(S("npeak"), 1)
                for g in range(2):
                    dve.wait_ge(S("z_mm"), 2 * n + g + 1)
                    wait_past(dve, S("h"), n)
                    dve.tensor_tensor(zb[:, g * CH:(g + 1) * CH], bank(g), b1row[:, g * CH:(g + 1) * CH], ALU.add)\
                       .then_inc(S("zb"), 1)
                dve.wait_ge(S("prob_exp"), n + 1)
                wait_past(dve, S("prob"), n)
                dve.reciprocal(prec[:], psums[:]).then_inc(S("prec"), 1)
                if loads is not None:
                    normalise(n + 1, 1 - p, loads)
                if not isinstance(n, int) or n >= 1:
                    if isinstance(n, int) and n == 1:
                        dve.wait_ge(S("d_zero"), 1)
                    gather_dW(n - 1)
                dve.wait_ge(S("probT_mm"), 2 * n + 1)
                wait_past(dve, S("o_mm"), n)
                dve.tensor_copy(flat(probT[:, 0:2, :, :]), bank(2)).then_inc(S("probT_lo"), 1)
                dve.wait_ge(S("o_mm"), n + 1)
                wait_past(dve, S("swa_mm"), n)
                dve.tensor_copy(flat(oT[:]), bank(6, D)).then_inc(S("oT"), 1)
                dve.wait_ge(S("pred_mm"), n + 1)
                dve.wait_ge(S("swaT"), n + 1)
                wait_past(dve, S("dh_mm"), 2 * n)
                wait_past(dve, S("e_part"), n)
                for k in range(DC):
                    ins = dve.scalar_tensor_tensor(out=eT[:, k, :], in0=psum[7][:, D + k * P:D + (k + 1) * P],
                                                   scalar=b2c[:, k:k + 1], in1=swaT[:, k, :],
                                                   op0=ALU.add, op1=ALU.subtract)
                if isinstance(n, int) and n == 0:
                    ins.then_inc(S("e_raw"), 1)
                    dve.wait_ge(S("e_raw"), 1)
                    ins = dve.memset(eT[:, :, 0:P - MEM], 0.0)
                ins.then_inc(S("eT"), 1)
                dve.wait_ge(S("eT"), n + 1)
                wait_past(dve, S("db2"), n)
                dve.tensor_reduce(e_part[:], eT[:], AX, ALU.add).then_inc(S("e_part"), 1)
                dve.wait_ge(S("e_part"), n + 1)
                dve.tensor_tensor(db2[:], db2[:], e_part[:], ALU.add).then_inc(S("db2"), 1)

            body(0, 0, 0, 1)
            body(1, 1, 1, 1)
            body(2, 0, 2, 2)
            with dve.Fori(1, TILES // 2 - 1) as i:
                body(i * 2 + 1, 1, 3, i + 1)
                body(i * 2 + 2, 0, 2, i + 2)
            body(LAST - 1, 1, 3, TILES // 2)
            body(LAST, 0, 2, None)
            grad_z(LAST)
            gather_dW(LAST)
            dve.wait_ge(S("rates"), 1)
            dve.wait_ge(S("dW"), 8 * LAST + 8)
            dve.tensor_scalar(dW1T[:], dW1T[:], step[:, 0:1], None, ALU.mult)
            dve.tensor_scalar(dW2[:], dW2[:], step[:, 0:1], None, ALU.mult).then_inc(S("stepped"), 1)
            dve.wait_ge(S("stepped"), 1)
            dve.scalar_tensor_tensor(out=w2n[:], in0=w2n[:], scalar=keep[:, 0:1], in1=dW2[:],
                                     op0=ALU.mult, op1=ALU.add).then_inc(S("w2_new"), 1)
            dve.scalar_tensor_tensor(out=w1T[:], in0=w1T[:], scalar=keep[:, 0:1], in1=dW1T[:],
                                     op0=ALU.mult, op1=ALU.add)
            dve.wait_ge(S("db1_mm"), 1)
            dve.tensor_scalar(db1[:], bank(4, HC), step[:, 0:1], None, ALU.mult)
            dve.wait_ge(S("db2"), LAST + 1)
            dve.tensor_scalar(db2[:], db2[:], step[:, 0:1], None, ALU.mult).then_inc(S("stepped"), 1)
            dve.wait_ge(S("stepped"), 2)
            dve.scalar_tensor_tensor(out=b1c[:], in0=b1c[:], scalar=keep[:, 0:1], in1=db1[:],
                                     op0=ALU.mult, op1=ALU.add)
            dve.scalar_tensor_tensor(out=b2c[:], in0=b2c[:], scalar=keep[:, 0:1], in1=db2[:],
                                     op0=ALU.mult, op1=ALU.add).then_inc(S("b_new"), 1)
            for g in range(4):
                dve.wait_ge(S("w2T_mm"), g + 1)
                dve.tensor_copy(flat(w2T[:, 2 * g:2 * g + 2, :]), bank(g)).then_inc(S("w2T_new"), 1)
            dve.wait_ge(S("w2T_new"), 4)

        @block.tensor
        def _(pe):
            pe.wait_ge(S("cond_w"), 1)
            pe.wait_ge(S("wmod_in"), 16)
            for j in range(3):
                for k in range(DC):
                    ins = mm(bank(j), cond_w[:, k, :], wmod[:, k, j * CH:(j + 1) * CH], k == 0, k == DC - 1)
            ins.then_inc(S("mod_mm"), 1)
            pe.wait_ge(S("mod_copied"), 1)
            pe.wait_ge(S("ident"), 1)

            def turn(out, src):
                return nc.tensor.transpose(out, src, ident[:])

            def backward(m):
                pe.wait_ge(S("eT"), m + 1)
                pe.wait_ge(S("probT_hi"), m + 1)
                for k in range(DC):
                    ins = turn(psum[3][:, k * P:(k + 1) * P], eT[:, k, :])
                ins.then_inc(S("e_mm"), 1)
                if isinstance(m, int) and m == 0:
                    pe.wait_ge(S("w2n_in"), 16)
                for g in range(2):
                    pe.wait_ge(S("hT"), 2 * m + g + 1)
                    for k in range(DC):
                        ins = mm(bank(4 + g), eT[:, k, :], w2n[:, k, g * CH:(g + 1) * CH], k == 0, k == DC - 1)
                    ins.then_inc(S("dh_mm"), 1)

            def gradient(m, p, tail=False):
                n = m + 1
                pe.wait_ge(S("dz"), 2 * m + 2)
                for j in range(4):
                    if j == 0:
                        pe.wait_ge(S("probT_lo" if tail else "v"), m + 1 if tail else n + 1)
                    if j == 1:
                        pe.wait_ge(S("e"), m + 1)
                    mm(bank((2 + j) % 8), xm[p][:, (j // 2) * P:(j // 2 + 1) * P], dz[:, (j % 2) * CH:(j % 2 + 1) * CH],
                       True, True).then_inc(S("dW_mm"), 1)
                for j in range(4, 8):
                    if tail:
                        if j == 4:
                            pe.wait_ge(S("oT"), m + 1)
                        if j == 5:
                            pe.wait_ge(S("eT"), m + 1)
                    elif j < 6:
                        pe.wait_ge(S("peak"), 2 * n + j - 3)
                    else:
                        pe.wait_ge(S("zb"), 2 * n + j - 5)
                    g = j - 4
                    mm(bank((2 + j) % 8), e[:, (g // 2) * P:(g // 2 + 1) * P], h[p][:, (g % 2) * CH:(g % 2 + 1) * CH],
                       True, True).then_inc(S("dW_mm"), 1)

            def body(n, p):
                first = isinstance(n, int) and n == 0
                pe.wait_ge(S("xm"), n + 1)
                wait_past(pe, S("dW"), 8 * n - 9)
                for k in range(DC):
                    ins = turn(psum[0][:, k * P:(k + 1) * P], xm[p][:, k * P:(k + 1) * P])
                ins.then_inc(S("xT_mm"), 1)
                if first:
                    pe.wait_ge(S("wqkv_in"), 16)
                pe.wait_ge(S("xT"), n + 1)
                wait_past(pe, S("dW"), 8 * n - 8)
                for j in range(4):
                    for k in range(DC):
                        ins = mm(psum[1][:, j * P:(j + 1) * P], wqkv[:, j // 2, k, (j % 2) * P:(j % 2 + 1) * P],
                                 xT[:, k, :], k == 0, k == DC - 1)
                ins.then_inc(S("qk_mm"), 1)
                wait_past(pe, S("probT_lo"), n)
                for k in range(DC):
                    ins = mm(bank(2, D), xT[:, k, :], wqkv[:, 2, k, :], k == 0, k == DC - 1)
                ins.then_inc(S("v_mm"), 1)
                if not first:
                    backward(n - 1)
                pe.wait_ge(S("qk"), n + 1)
                wait_past(pe, S("oT"), n)
                wait_past(pe, S("eT"), n)
                for b in range(2):
                    for c in range(DC):
                        ins = mm(psum[6 + b][:, c * D:(c + 1) * D], qT[b * DH:(b + 1) * DH, c, :],
                                 kT[b * DH:(b + 1) * DH, c, :, :], True, True)
                    ins.then_inc(S("s_mm"), 1)
                if first:
                    pe.wait_ge(S("w1_in"), 16)
                for g in range(2):
                    for k in range(DC):
                        ins = mm(bank(g), xT[:, k, :], w1T[:, k, g * CH:(g + 1) * CH], k == 0, k == DC - 1)
                    ins.then_inc(S("z_mm"), 1)
                if not first:
                    gradient(n - 1, 1 - p)
                pe.wait_ge(S("prob"), n + 1)
                for g in range(2):
                    wait_past(pe, S("dW"), 8 * n - 7 + g)
                    if first:
                        pe.wait_ge(S("v"), 1)
                    for b in range(4):
                        ins = turn(psum[2 + g][:, b * P:(b + 1) * P],
                                   prob[:, 2 * g + b // 2, (b % 2) * P:(b % 2 + 1) * P])
                    ins.then_inc(S("probT_mm"), 1)
                pe.wait_ge(S("h"), n + 1)
                for g in range(2):
                    wait_past(pe, S("dW"), 8 * n - 5 + g)
                    for b in range(4):
                        ins = turn(psum[4 + g][:, b * P:(b + 1) * P], h[p][:, (4 * g + b) * P:(4 * g + b + 1) * P])
                    ins.then_inc(S("hT_mm"), 1)
                pe.wait_ge(S("probT_lo"), n + 1)
                pe.wait_ge(S("probT_hi"), n + 1)
                pe.wait_ge(S("v"), n + 1)
                wait_past(pe, S("dW"), 8 * n - 3)
                for s in range(HEADS):
                    hd = HEAD_AT[s]
                    for t in range(2):
                        ins = mm(psum[6][(hd % 2) * DH:(hd % 2 + 1) * DH, (hd // 2) * P:(hd // 2 + 1) * P],
                                 v[:, t, hd * DH:(hd + 1) * DH], probT[:, s, t, :], t == 0, t == 1)
                ins.then_inc(S("o_mm"), 1)
                if first:
                    pe.wait_ge(S("wo_in"), 16)
                    pe.wait_ge(S("w2T_in"), 16)
                pe.wait_ge(S("oT"), n + 1)
                wait_past(pe, S("dW"), 8 * n - 2)
                for m in range(DC):
                    for k in range(DC):
                        ins = mm(psum[7][:, m * P:(m + 1) * P], woT[:, k, m * P:(m + 1) * P], oT[:, k, :],
                                 k == 0, k == DC - 1)
                ins.then_inc(S("swa_mm"), 1)
                pe.wait_ge(S("hT"), 2 * n + 2)
                for m in range(DC):
                    for k in range(HC):
                        ins = mm(psum[7][:, D + m * P:D + (m + 1) * P], w2T[:, k, m * P:(m + 1) * P], hT[:, k, :],
                                 k == 0, k == HC - 1)
                ins.then_inc(S("pred_mm"), 1)

            def tail():
                backward(LAST)
                gradient(LAST, 0, tail=True)
                pe.wait_ge(S("dz_sum"), LAST + 1)
                pe.wait_ge(S("dW"), 8 * LAST + 3)
                for j in range(HC):
                    ins = mm(psum[4][:, j:j + 1], dz_sum[:, j * P:(j + 1) * P], ones[:, 0:1], True, True)
                ins.then_inc(S("db1_mm"), 1)
                pe.wait_ge(S("w2_new"), 1)
                pe.wait_ge(S("dW"), 8 * LAST + 8)
                for g in range(4):
                    for b in range(4):
                        j, k = 2 * g + b // 2, b % 2
                        ins = turn(psum[g][:, b * P:(b + 1) * P], w2n[:, k, j * P:(j + 1) * P])
                    ins.then_inc(S("w2T_mm"), 1)

            tiles(pe, body, tail)


def token_stage(nc, T, buf, psum, S):
    with ExitStack() as ctx:
        def sb(name, shape, dt=F32):
            return ctx.enter_context(nc.sbuf_tensor("b_" + name, shape, dt))

        xT_all, swaT_all, w1T, w2T = buf["xT_all"], buf["swaT_all"], buf["w1T"], buf["w2T"]
        mod, ident, b1c, b2c = buf["mod"], buf["ident"], buf["b1c"], buf["b2c"]
        linT = sb("linT", [P, 2, DC, D])
        wgT = sb("wgT", [P, DC, E])
        s1T = sb("s1T", [P, DC, 2 * FFN])
        s2T = sb("s2T", [P, FC, D])
        before = sb("before", [P, P], BF16)
        every = sb("every", [P, P], BF16)
        slot_base = sb("slot_base", [P, E])
        token = sb("token", [P, TPC], I32)
        carry = sb("carry", [P, E])
        h2 = sb("h2", [P, HC, CH])
        om = sb("om", [P, DC, CH])
        g1 = sb("g1", [P, DC, CH])
        g2 = sb("g2", [P, DC, CH])
        x = sb("x", [P, TPC, D])
        x2 = sb("x2", [P, TPC, D])
        stats = sb("stats", [P, TPC, 6])
        moments = sb("moments", [P, TPC, 2])
        rstd = sb("rstd", [P, TPC])
        half = sb("half", [P, TPC])
        hm = sb("hm", [P, TPC, D])
        hT = sb("hT", [P, DC, CH])
        lg = sb("lg", [P, TPC, E])
        lmax = sb("lmax", [P, TPC])
        gate = sb("gate", [P, TPC, E])
        gsum = sb("gsum", [P, TPC])
        grec = sb("grec", [P, TPC])
        top = sb("top", [P, TPC, TOPK])
        rest = sb("rest", [P, TPC, E])
        chosen = sb("chosen", [P, TPC, E])
        chosen_b = sb("chosen_b", [P, TPC, E], BF16)
        wsum = sb("wsum", [P, TPC])
        wrec = sb("wrec", [P, TPC])
        rank = sb("rank", [P, TPC, E])
        fits = sb("fits", [P, TPC, E])
        slot = sb("slot", [P, TPC, E])
        slot8 = sb("slot8", [P, TPC, TOPK])
        off = sb("off", [P, TPC, TOPK])
        index = sb("index", [P, TPC, TOPK], U32)
        picked = sb("picked", [P, TOPK, E])
        w8 = sb("w8", [P, TPC, TOPK])
        row = sb("row", [P, 2, TOPK, ROW])
        sil = [sb(f"sil{p}", [P, CH]) for p in range(2)]
        gT = sb("gT", [P, FC, CH])
        base = sb("base", [P, TPC, D])

        def bank(b, n=CH):
            return psum[b][:, 0:n]

        def mm(out, lhsT, rhs, first, last):
            return nc.tensor.matmul(out, lhsT, rhs, start=first, stop=last, skip_group_check=True)

        def wide(a, n):
            return a.unsqueeze(2).to_broadcast([P, TPC, n])

        def rows_of(a):
            return a.unsqueeze(1).to_broadcast([P, TPC, D])

        def chunk(c):
            return bass.ds(c * CH, CH)


        x_rows = T["x"].rearrange("(c t p) d -> p (c t) d", p=P, t=TPC)
        out_rows = T["out"][0:TOKENS, :].rearrange("(c t p) d -> p (c t) d", p=P, t=TPC)
        BANK_Z = range(8)
        BANK_SH = [2, 3, 4, 5, 6, 7, 0, 1, 2, 3, 4, 5]

        block = ctx.enter_context(nc.Block())

        @block.sync
        def _(sp):
            sp.dma_start(linT[:], T["linT"]).then_inc(S("lin_in"), 16)
            sp.dma_start(wgT[:], T["wgT"]).then_inc(S("wg_in"), 16)
            sp.dma_start(s1T[:], T["s1T"]).then_inc(S("s1_in"), 16)
            sp.dma_start(s2T[:], T["s2T"]).then_inc(S("s2_in"), 16)

            def load(c):
                wait_past(sp, S("x2"), c)
                sp.dma_start(x[:], x_rows[:, bass.ds(c * TPC, TPC), :]).then_inc(S("x_in"), 16)

            def store(c):
                sp.wait_ge(S("base"), 2 * c)
                sp.dma_start(out_rows[:, bass.ds((c - 1) * TPC, TPC), :], base[:]).then_inc(S("base_out"), 16)

            load(0)
            with sp.Fori(1, CHUNKS) as c:
                load(c)
                store(c)
            store(CHUNKS)
            sp.wait_ge(S("base_out"), 16 * CHUNKS)

        @block.gpsimd
        def _(pool):
            pool.memset(before[:], 1.0)
            pool.memset(every[:], 1.0)
            pool.memset(carry[:], 0.0).then_inc(S("set"), 1)
            pool.wait_ge(S("set"), 1)
            pool.affine_select(out=before[:], in_=before[:], compare_op=ALU.is_gt, fill=0.0, base=0,
                               pattern=[[1, P]], channel_multiplier=-1)
            pool.iota(slot_base[:], pattern=[[CAP, E]], base=1, channel_multiplier=0,
                      allow_small_or_imprecise_dtypes=True)
            pool.iota(token[:], pattern=[[P, TPC]], base=0, channel_multiplier=1).then_inc(S("route_const"), 1)

            def scatter(c):
                pool.wait_ge(S("index"), c)
                for t in range(TPC):
                    wait_apart(pool, S("row_part"), (c - 1) * TPC + t + 1, S("passed_pool"))
                    pool.tensor_copy(row[:, t % 2, :, D + 1:D + 2].bitcast(I32),
                                     token[:, t:t + 1].unsqueeze(1).to_broadcast([P, TOPK, 1])).then_inc(S("row"), 1)
                    wait_apart(pool, S("row"), (c - 1) * TPC + t + 1, S("passed_pool"))
                    for k in range(TOPK):
                        pool.indirect_dma_start(
                            out=T["slots"], out_offset=bass.IndirectOffsetOnAxis(ap=index[:, t, k:k + 1], axis=0),
                            in_=row[:, t % 2, k, :], in_offset=None,
                            bounds_check=last_slot, oob_is_err=False).then_inc(S(f"row_out{t % 2}"), 16)
                pool.tensor_scalar(token[:], token[:], float(CH), None, ALU.add).then_inc(S("token"), 1)
                pool.wait_ge(S("token"), c)

            last_slot = pool.to_reg(E * CAP - 1)
            scatter(1)
            with pool.Fori(2, CHUNKS + 1) as c:
                scatter(c)
            pool.wait_ge(S("row_out0"), CHUNKS * TPC // 2 * TOPK * 16)
            pool.wait_ge(S("row_out1"), CHUNKS * TPC // 2 * TOPK * 16)

        @block.scalar
        def _(act):
            def late(c):
                for g in range(2):
                    act.wait_ge(S("hT_mm"), 2 * c - 1 + g)
                    act.copy(hT[:, :, g * D:(g + 1) * D],
                             bank(g).rearrange("p (k t) -> p k t", k=DC)).then_inc(S("hT"), 1)
                act.wait_ge(S("lg"), c)
                act.activation(gate[:], lg[:], ACT.Exp).then_inc(S("gate_exp"), 1)

            def late_rows(c):
                for t in range(TPC):
                    act.wait_ge(S("w8"), (c - 1) * TPC + t + 1)
                    wait_past(act, S(f"row_out{t % 2}"), ((c - 1) * 2 + t // 2) * TOPK * 16)
                    act.copy(row[:, t % 2, :, 0:D], hm[:, t, :].unsqueeze(1).to_broadcast([P, TOPK, D]))
                    act.copy(row[:, t % 2, :, D:D + 1], w8[:, t, :].unsqueeze(2)).then_inc(S("row_part"), 1)

            def late_silu(c):
                for j in range(FC):
                    act.wait_ge(S("sh_mm"), (c - 1) * 2 * FC + 2 * j + 1)
                    wait_past(act, S("gT"), (c - 1) * FC + max(j - 1, 0))
                    act.activation(sil[j % 2][:], bank(BANK_SH[2 * j]), ACT.Silu).then_inc(S("sil"), 1)

            def body(c, after):
                for j in range(HC):
                    act.wait_ge(S("z_mm"), c * HC + j + 1)
                    wait_past(act, S("om_mm"), 2 * c)
                    act.activation(h2[:, j, :], bank(BANK_Z[j]), ACT.Silu, bias=b1c[:, j:j + 1]).then_inc(S("h2"), 1)
                if after:
                    late(c)
                for g, (dst, banks) in enumerate(((g1, (5, 6)), (g2, (7, 0)))):
                    for m in range(DC):
                        act.wait_ge(S("lin_mm"), c * 4 + 2 * g + m + 1)
                        wait_past(act, S("mT_mm"), 2 * c)
                        act.activation(dst[:, m, :], bank(banks[m]), ACT.Sigmoid).then_inc(S("gated"), 1)
                if after:
                    late_silu(c)
                    late_rows(c)

            body(0, False)
            body(1, True)
            with act.Fori(2, CHUNKS) as c:
                body(c, True)
            late(CHUNKS)
            late_silu(CHUNKS)
            late_rows(CHUNKS)

        @block.vector
        def _(dve):
            dve.wait_ge(S("route_const"), 1)

            def route(c):
                lp = bank(2, TPC * E).rearrange("p (t e) -> p t e", t=TPC)
                dve.wait_ge(S("gate_mm"), c)
                dve.tensor_reduce(lmax[:], lp, AX, ALU.max).then_inc(S("lmax"), 1)
                dve.wait_ge(S("lmax"), c)
                dve.tensor_tensor(lg[:], lp, wide(lmax[:], E), ALU.subtract).then_inc(S("lg"), 1)
                dve.wait_ge(S("gate_exp"), c)
                dve.tensor_reduce(gsum[:], gate[:], AX, ALU.add).then_inc(S("gsum"), 1)
                dve.wait_ge(S("gsum"), c)
                dve.reciprocal(grec[:], gsum[:]).then_inc(S("grec"), 1)
                dve.wait_ge(S("grec"), c)
                dve.tensor_tensor(gate[:], gate[:], wide(grec[:], E), ALU.mult).then_inc(S("gate"), 1)
                wait_apart(dve, S("gate"), c, S("passed_dve"))
                for t in range(TPC):
                    ins = dve.max(top[:, t, :], gate[:, t, :])
                ins.then_inc(S("top"), 1)
                wait_apart(dve, S("top"), c, S("passed_dve"))
                for t in range(TPC):
                    dve.match_replace(out=rest[:, t, :], in_to_replace=top[:, t, :], in_values=gate[:, t, :],
                                      imm_value=-1.0)
                dve.tensor_reduce(wsum[:], top[:], AX, ALU.add).then_inc(S("rest"), 1)
                dve.wait_ge(S("rest"), c)
                dve.tensor_scalar(wsum[:], wsum[:], F32_EPS, None, ALU.max)
                dve.tensor_scalar(chosen_b[:], rest[:], 0.0, None, ALU.is_lt)
                dve.tensor_scalar(chosen[:], rest[:], 0.0, None, ALU.is_lt).then_inc(S("chosen"), 1)
                dve.wait_ge(S("chosen"), c)
                dve.reciprocal(wrec[:], wsum[:]).then_inc(S("wrec"), 1)
                dve.wait_ge(S("wrec"), c)
                dve.tensor_tensor(gate[:], gate[:], wide(wrec[:], E), ALU.mult).then_inc(S("weight"), 1)

            def slots_of(c):
                dve.wait_ge(S("rank_mm"), c)
                for t in range(TPC):
                    wait_past(dve, S("carry"), (c - 1) * TPC + t)
                    dve.tensor_tensor(rank[:, t, :], psum[1][:, D + t * E:D + (t + 1) * E], carry[:], ALU.add)\
                       .then_inc(S("rank"), 1)
                    dve.wait_ge(S("rank"), (c - 1) * TPC + t + 1)
                    dve.tensor_tensor(carry[:], carry[:], psum[1][:, t * E:(t + 1) * E], ALU.add)\
                       .then_inc(S("carry"), 1)
                dve.scalar_tensor_tensor(out=fits[:], in0=rank[:], scalar=float(CAP), in1=chosen[:],
                                         op0=ALU.is_lt, op1=ALU.mult)
                dve.tensor_tensor(slot[:], rank[:], slot_base[:].unsqueeze(1).to_broadcast([P, TPC, E]), ALU.add)\
                   .then_inc(S("fits"), 1)
                dve.wait_ge(S("fits"), c)
                dve.tensor_tensor(slot[:], slot[:], fits[:], ALU.mult).then_inc(S("slot"), 1)
                wait_apart(dve, S("slot"), c, S("passed_dve"))
                for t in range(TPC):
                    ins = dve.max(slot8[:, t, :], slot[:, t, :])
                ins.then_inc(S("slot8"), 1)
                dve.wait_ge(S("slot8"), c)
                dve.tensor_scalar(off[:], slot8[:], 1.0, float(OFF_LIST), ALU.is_lt, ALU.mult).then_inc(S("off"), 1)
                dve.wait_ge(S("off"), c)
                wait_past(dve, S("row_out0"), (c - 1) * 2 * TOPK * 16)
                wait_past(dve, S("row_out1"), (c - 1) * 2 * TOPK * 16)
                dve.scalar_tensor_tensor(out=index[:], in0=slot8[:], scalar=-1.0, in1=off[:], op0=ALU.add,
                                         op1=ALU.add).then_inc(S("index"), 1)
                dve.wait_ge(S("weight"), c)
                wait_past(dve, S("row_part"), (c - 1) * TPC)
                for t in range(TPC):
                    wait_past(dve, S("w8"), (c - 1) * TPC + t)
                    for k in range(TOPK):
                        ins = dve.scalar_tensor_tensor(out=picked[:, k, :], in0=slot[:, t, :],
                                                       scalar=slot8[:, t, k:k + 1], in1=gate[:, t, :],
                                                       op0=ALU.is_equal, op1=ALU.mult, accum_out=w8[:, t, k:k + 1])
                    ins.then_inc(S("w8"), 1)

            def merge(c):
                dve.wait_ge(S("gated"), 4 * c + 2)
                dve.tensor_tensor(g1[:], g1[:], swaT_all[:, :, chunk(c)], ALU.mult)
                dve.wait_ge(S("gated"), 4 * c + 4)
                dve.tensor_tensor(g2[:], g2[:], om[:], ALU.mult).then_inc(S("parts"), 1)
                dve.wait_ge(S("parts"), c + 1)
                dve.tensor_tensor(g1[:], g1[:], g2[:], ALU.add).then_inc(S("merged"), 1)

            def shared(c):
                for j in range(FC):
                    dve.wait_ge(S("sil"), (c - 1) * FC + j + 1)
                    dve.wait_ge(S("sh_mm"), (c - 1) * 2 * FC + 2 * j + 2)
                    wait_past(dve, S("so_mm"), (c - 1) * 2)
                    dve.tensor_tensor(gT[:, j, :], bank(BANK_SH[2 * j + 1]), sil[j % 2][:], ALU.mult)\
                       .then_inc(S("gT"), 1)

            def base_rows(c):
                for g in range(2):
                    dve.wait_ge(S("so_mm"), 2 * c - 1 + g)
                    wait_past(dve, S("base_out"), (c - 1) * 16)
                    dve.tensor_tensor(base[:, 2 * g:2 * g + 2, :], bank(6 + g).rearrange("p (t d) -> p t d", t=2),
                                      mod[:, 5, :].unsqueeze(1).to_broadcast([P, 2, D]), ALU.mult)\
                       .then_inc(S("base_raw"), 1)
                    dve.wait_ge(S("base_raw"), 2 * c - 1 + g)
                    dve.tensor_tensor(base[:, 2 * g:2 * g + 2, :], base[:, 2 * g:2 * g + 2, :],
                                      x2[:, 2 * g:2 * g + 2, :], ALU.add).then_inc(S("base"), 1)

            def residual(c):
                dve.wait_ge(S("x_in"), 16 * (c + 1))
                for g in range(2):
                    dve.wait_ge(S("mT_mm"), 2 * c + g + 1)
                    if g == 0:
                        wait_past(dve, S("base"), 2 * c)
                    dve.tensor_tensor(x2[:, 2 * g:2 * g + 2, :], bank(2 + g).rearrange("p (t d) -> p t d", t=2),
                                      mod[:, 2, :].unsqueeze(1).to_broadcast([P, 2, D]), ALU.mult)\
                       .then_inc(S("x2_raw"), 1)
                dve.wait_ge(S("x2_raw"), 2 * c + 2)
                dve.tensor_tensor(x2[:], x2[:], x[:], ALU.add).then_inc(S("x2"), 1)
                dve.wait_ge(S("x2"), c + 1)
                for t in range(TPC):
                    ins = dve.bn_stats(stats[:, t, :], x2[:, t, :])
                ins.then_inc(S("stats"), 1)
                wait_apart(dve, S("stats"), c + 1, S("passed_dve"))
                for t in range(TPC):
                    ins = dve.bn_aggr(moments[:, t, :], stats[:, t, :])
                ins.then_inc(S("moments"), 1)
                dve.wait_ge(S("moments"), c + 1)
                inverse_sqrt(dve, S("rstd"), c, rstd[:], moments[:, :, 1], half[:])
                wait_past(dve, S("hT_mm"), 2 * c)
                wait_past(dve, S("row_part"), c * TPC)
                for t in range(TPC):
                    ins = dve.tensor_scalar(hm[:, t, :], x2[:, t, :], moments[:, t, 0:1], rstd[:, t:t + 1],
                                            ALU.subtract, ALU.mult)
                ins.then_inc(S("hn"), 1)
                dve.wait_ge(S("hn"), c + 1)
                dve.tensor_tensor(hm[:], hm[:], rows_of(mod[:, 4, :]), ALU.mult).then_inc(S("hscaled"), 1)
                dve.wait_ge(S("hscaled"), c + 1)
                dve.tensor_tensor(hm[:], hm[:], rows_of(mod[:, 3, :]), ALU.add).then_inc(S("hm"), 1)

            def body(c, after):
                if after:
                    route(c)
                for m in range(DC):
                    dve.wait_ge(S("om_mm"), 2 * c + m + 1)
                    wait_past(dve, S("parts"), c)
                    dve.tensor_scalar(om[:, m, :], bank(3 + m), b2c[:, m:m + 1], None, ALU.add).then_inc(S("om"), 1)
                if after:
                    slots_of(c)
                merge(c)
                if after:
                    shared(c)
                    base_rows(c)
                residual(c)

            body(0, False)
            body(1, True)
            with dve.Fori(2, CHUNKS) as c:
                body(c, True)
            route(CHUNKS)
            slots_of(CHUNKS)
            shared(CHUNKS)
            base_rows(CHUNKS)

        @block.tensor
        def _(pe):
            def turn(out, src):
                return nc.tensor.transpose(out, src, ident[:])

            def gates(c):
                pe.wait_ge(S("hm"), c)
                for g in range(2):
                    for b in range(4):
                        k, t = b // 2, 2 * g + b % 2
                        ins = turn(psum[g][:, b * P:(b + 1) * P], hm[:, t, k * P:(k + 1) * P])
                    ins.then_inc(S("hT_mm"), 1)
                pe.wait_ge(S("hT"), 2 * c)
                for t in range(TPC):
                    for k in range(DC):
                        ins = mm(psum[2][:, t * E:(t + 1) * E], hT[:, k, t * P:(t + 1) * P], wgT[:, k, :],
                                 k == 0, k == DC - 1)
                ins.then_inc(S("gate_mm"), 1)

            def ranks(c):
                pe.wait_ge(S("chosen"), c)
                flat = chosen_b[:].rearrange("p t e -> p (t e)")
                mm(psum[1][:, 0:TPC * E], every[:], flat, True, True)
                mm(psum[1][:, D:D + TPC * E], before[:], flat, True, True).then_inc(S("rank_mm"), 1)

            def shared(c, tail):
                for i in range(2 * FC):
                    j, part = i // 2, i % 2
                    if i == 0:
                        pe.wait_ge(S("lg"), c)
                    if not tail:
                        if i == 1:
                            pe.wait_ge(S("om"), 2 * c + 2)
                        if i in (3, 4, 5, 6):
                            pe.wait_ge(S("gated"), 4 * c + i - 2)
                    if i == 7:
                        pe.wait_ge(S("carry"), c * TPC)
                    if i >= 8:
                        pe.wait_ge(S("gT"), (c - 1) * FC + (i - 8) // 2 + 1)
                    col = (FC + j if part == 0 else j) * P
                    for k in range(DC):
                        ins = mm(bank(BANK_SH[i]), s1T[:, k, col:col + P], hT[:, k, :], k == 0, k == DC - 1)
                    ins.then_inc(S("sh_mm"), 1)
                pe.wait_ge(S("gT"), c * FC)
                for g in range(2):
                    for t in range(2):
                        for k in range(FC):
                            ins = mm(psum[6 + g][:, t * D:(t + 1) * D], gT[:, k, (2 * g + t) * P:(2 * g + t + 1) * P],
                                     s2T[:, k, :], k == 0, k == FC - 1)
                    ins.then_inc(S("so_mm"), 1)

            def body(c, after):
                for j in range(HC):
                    if j in (2, 3):
                        wait_past(pe, S("x2_raw"), 2 * c - 3 + j)
                    if j == 6 and after:
                        wait_past(pe, S("base_raw"), 2 * c - 2)
                    for k in range(DC):
                        ins = mm(bank(BANK_Z[j]), w1T[:, k, j * P:(j + 1) * P], xT_all[:, k, chunk(c)],
                                 k == 0, k == DC - 1)
                    ins.then_inc(S("z_mm"), 1)
                pe.wait_ge(S("h2"), c * HC + 3)
                if after:
                    gates(c)
                pe.wait_ge(S("h2"), (c + 1) * HC)
                for m in range(DC):
                    for k in range(HC):
                        ins = mm(bank(3 + m), w2T[:, k, m * P:(m + 1) * P], h2[:, k, :], k == 0, k == HC - 1)
                    ins.then_inc(S("om_mm"), 1)
                for m in range(DC):
                    for k in range(DC):
                        ins = mm(bank(5 + m), linT[:, 0, k, m * P:(m + 1) * P], swaT_all[:, k, chunk(c)],
                                 k == 0, k == DC - 1)
                    ins.then_inc(S("lin_mm"), 1)
                pe.wait_ge(S("om"), 2 * c + 2)
                for m in range(DC):
                    for k in range(DC):
                        ins = mm(bank((7, 0)[m]), linT[:, 1, k, m * P:(m + 1) * P], om[:, k, :], k == 0, k == DC - 1)
                    ins.then_inc(S("lin_mm"), 1)
                if after:
                    ranks(c)
                    shared(c, False)
                pe.wait_ge(S("merged"), c + 1)
                for g in range(2):
                    for b in range(4):
                        t, k = 2 * g + b // 2, b % 2
                        ins = turn(psum[2 + g][:, b * P:(b + 1) * P], g1[:, k, t * P:(t + 1) * P])
                    ins.then_inc(S("mT_mm"), 1)

            pe.wait_ge(S("lin_in"), 16)
            pe.wait_ge(S("wg_in"), 16)
            pe.wait_ge(S("s1_in"), 16)
            pe.wait_ge(S("s2_in"), 16)
            body(0, False)
            body(1, True)
            with pe.Fori(2, CHUNKS) as c:
                body(c, True)
            gates(CHUNKS)
            ranks(CHUNKS)
            shared(CHUNKS, True)


def expert_stage(nc, T, buf, psum, S):
    with ExitStack() as ctx:
        def sb(name, shape, dt=F32):
            return ctx.enter_context(nc.sbuf_tensor("c_" + name, shape, dt))

        mod, ident = buf["mod"], buf["ident"]
        w1 = [sb(f"w1_{p}", [P, DC, 2 * FFN]) for p in range(2)]
        w2 = [sb(f"w2_{p}", [P, FC, D]) for p in range(2)]
        xa = [sb(f"xa{q}", [P, ROW]) for q in range(4)]
        xb = [sb(f"xb{q}", [CAP_B, ROW]) for q in range(4)]
        xT = [sb(f"xT{p}", [P, DC, CAP]) for p in range(2)]
        sil = sb("sil", [P, FC, CAP])
        gT = [sb(f"gT{p}", [P, FC, CAP]) for p in range(2)]
        yT = sb("yT", [P, DC, CAP])
        ya = sb("ya", [P, D])
        yb = sb("yb", [CAP_B, D])
        H = FC // 2
        Y_BANK = (5, 7)

        def mm(out, lhsT, rhs, first, last):
            return nc.tensor.matmul(out, lhsT, rhs, start=first, stop=last, skip_group_check=True)

        def experts(eng, step):
            for n in range(4):
                step(n, n, 1, n // 2 + 1)
            with eng.Fori(1, E // 4) as i:
                for q in range(4):
                    step(i * 4 + q, q, i + 1, i * 2 + q // 2 + 1)

        block = ctx.enter_context(nc.Block())

        @block.sync
        def _(sp):
            def load_w2(n, p):
                wait_past(sp, S("y_mm"), n - 1)
                sp.dma_start(w2[p][:], T["e2T"][bass.ds(n, 1)].rearrange("a p k f -> p (a k) f"))\
                  .then_inc(S(f"w2_in{p}"), 16)

            def step(n, q, rows_in, weights_in):
                p = q % 2
                wait_past(sp, S("added"), (n - 3) * 32)
                sp.dma_start(xa[q][:], T["slots"][bass.ds(n * CAP, P), :]).then_inc(S(f"x_in{q}"), 16)
                sp.dma_start(xb[q][:], T["slots"][bass.ds(n * CAP + P, CAP_B), :]).then_inc(S(f"x_in{q}"), 16)
                wait_past(sp, S("h_mm"), (n - 1) * 4)
                sp.dma_start(w1[p][:], T["e1T"][bass.ds(n, 1)].rearrange("a p k f -> p (a k) f"))\
                  .then_inc(S(f"w1_in{p}"), 16)
                if not isinstance(n, int) or n >= 1:
                    load_w2(n - 1, 1 - p)

            experts(sp, step)
            load_w2(E - 1, 1)

        @block.scalar
        def _(act):
            def y_cols(n):
                for m in range(DC):
                    act.wait_ge(S("y_mm"), n + 1)
                    wait_past(act, S("yR_mm"), n)
                    ins = act.copy(yT[:, m, :], psum[Y_BANK[m]][:, 0:CAP])
                ins.then_inc(S("yT"), 1)

            def step(n, q, rows_in, weights_in):
                p = q % 2
                act.wait_ge(S("xT_mm"), n + 1)
                wait_past(act, S("h_mm"), (n - 1) * 4)
                act.copy(flat(xT[p][:]), psum[0][:, 0:DC * CAP]).then_inc(S("xT"), 1)
                if not isinstance(n, int) or n >= 1:
                    y_cols(n - 1)
                for g in range(2):
                    act.wait_ge(S("h_mm"), 4 * n + 2 * g + 1)
                    wait_past(act, S("gT"), 2 * n - 1 + g)
                    act.activation(flat(sil[:, g * H:(g + 1) * H, :]), psum[1 + 2 * g][:, 0:H * CAP], ACT.Silu)\
                       .then_inc(S("sil"), 1)

            experts(act, step)
            y_cols(E - 1)

        @block.vector
        def _(dve):
            def y_rows(n, q):
                dve.wait_ge(S("yR_mm"), n + 1)
                wait_past(dve, S("added"), n * 32)
                dve.scalar_tensor_tensor(out=ya[:], in0=psum[6][:, 0:D], scalar=xa[q][:, D:D + 1], in1=mod[:, 5, :],
                                         op0=ALU.mult, op1=ALU.mult)
                dve.scalar_tensor_tensor(out=yb[:], in0=psum[6][0:CAP_B, D:2 * D], scalar=xb[q][:, D:D + 1],
                                         in1=mod[0:CAP_B, 5, :], op0=ALU.mult, op1=ALU.mult).then_inc(S("y"), 1)

            def step(n, q, rows_in, weights_in):
                p = q % 2
                for g in range(2):
                    dve.wait_ge(S("sil"), 2 * n + g + 1)
                    dve.wait_ge(S("h_mm"), 4 * n + 2 * g + 2)
                    wait_past(dve, S("y_mm"), n - 1)
                    dve.tensor_tensor(flat(gT[p][:, g * H:(g + 1) * H, :]), psum[2 + 2 * g][:, 0:H * CAP],
                                      flat(sil[:, g * H:(g + 1) * H, :]), ALU.mult).then_inc(S("gT"), 1)
                if not isinstance(n, int) or n >= 1:
                    y_rows(n - 1, (q - 1) % 4)

            experts(dve, step)
            y_rows(E - 1, 3)

        @block.gpsimd
        def _(pool):
            last_row = pool.to_reg(TOKENS + CAP - 1)

            def step(n, q, rows_in, weights_in):
                wait_past(pool, S("added"), n * 32)
                wait_apart(pool, S("y"), n + 1, S("passed_pool"))
                for y, x in ((ya, xa[q]), (yb, xb[q])):
                    pool.indirect_dma_start(
                        out=T["out"], out_offset=bass.IndirectOffsetOnAxis(ap=x[:, D + 1:D + 2].bitcast(U32), axis=0),
                        in_=y[:], in_offset=None, bounds_check=last_row, oob_is_err=True,
                        compute_op=ALU.add).then_inc(S("added"), 16)

            experts(pool, step)
            pool.wait_ge(S("added"), E * 32)

        @block.tensor
        def _(pe):
            def turn_x(n, q, rows_in):
                pe.wait_ge(S(f"x_in{q}"), rows_in * 32)
                wait_past(pe, S("xT"), n)
                for k in range(DC):
                    nc.tensor.transpose(psum[0][:, k * CAP:k * CAP + P], xa[q][:, k * P:(k + 1) * P], ident[:])
                    ins = nc.tensor.transpose(psum[0][:, k * CAP + P:(k + 1) * CAP], xb[q][:, k * P:(k + 1) * P],
                                              ident[0:CAP_B, 0:CAP_B])
                ins.then_inc(S("xT_mm"), 1)

            def up(n, p, weights_in):
                pe.wait_ge(S(f"w1_in{p}"), weights_in * 16)
                pe.wait_ge(S("xT"), n + 1)
                for g in range(2):
                    for part in range(2):
                        wait_past(pe, S("sil" if part == 0 else "gT"), 2 * n - 1 + g)
                        for j in range(H):
                            col = ((FC if part == 0 else 0) + g * H + j) * P
                            for k in range(DC):
                                ins = mm(psum[1 + 2 * g + part][:, j * CAP:(j + 1) * CAP], w1[p][:, k, col:col + P],
                                         xT[p][:, k, :], k == 0, k == DC - 1)
                        ins.then_inc(S("h_mm"), 1)

            def down(n, p, weights_in):
                pe.wait_ge(S(f"w2_in{p}"), weights_in * 16)
                wait_past(pe, S("yT"), n)
                for g in range(2):
                    pe.wait_ge(S("gT"), 2 * n + g + 1)
                    for m in range(DC):
                        for k in range(g * H, (g + 1) * H):
                            ins = mm(psum[Y_BANK[m]][:, 0:CAP], w2[p][:, k, m * P:(m + 1) * P], gT[p][:, k, :],
                                     k == 0, k == FC - 1)
                ins.then_inc(S("y_mm"), 1)

            def turn_y(n):
                pe.wait_ge(S("yT"), n + 1)
                wait_past(pe, S("y"), n)
                for k in range(DC):
                    nc.tensor.transpose(psum[6][:, k * P:(k + 1) * P], yT[:, k, 0:P], ident[:])
                    ins = nc.tensor.transpose(psum[6][0:CAP_B, D + k * P:D + (k + 1) * P], yT[:, k, P:CAP], ident[:])
                ins.then_inc(S("yR_mm"), 1)

            def step(n, q, rows_in, weights_in):
                p = q % 2
                late = not isinstance(n, int) or n >= 1
                turn_x(n, q, rows_in)
                if late:
                    down(n - 1, 1 - p, weights_in - (1 - p))
                up(n, p, weights_in)
                if late:
                    turn_y(n - 1)

            experts(pe, step)
            down(E - 1, 1, E // 2)
            turn_y(E - 1)


def build(nc, T):
    with ExitStack() as ctx:
        buf = shared_buffers(nc, ctx)
        psum = [ctx.enter_context(nc.psum_tensor(f"bank{b}", [P, CH], F32)) for b in range(8)]
        for stage, prefix in ((memory_stage, "a_"), (token_stage, "b_"), (expert_stage, "c_")):
            sems = Sems(nc, prefix)
            stage(nc, T, buf, psum, sems)
            sems.clear()


def kernel(**inputs):
    import numpy as np
    import concourse.bacc as bacc
    from concourse.bass_utils import run_bass_kernel_spmd

    a = {k: np.asarray(v) for k, v in inputs.items()}

    def split(w):
        k, n = w.shape
        return np.ascontiguousarray(w.reshape(k // P, P, n).transpose(1, 0, 2))

    w = {k[len("L0_"):]: v for k, v in a.items()}
    e1, e2 = w["ffn_expert_w1"], w["ffn_expert_w2"]
    arrays = {
        "x": w["attn_x"].reshape(TOKENS, D),
        "mem": w["attn_mem"],
        "wqkvT": np.ascontiguousarray(np.stack([split(w["attn_wq"].T), split(w["attn_wk"].T),
                                                split(w["attn_wv"].T)], axis=1)),
        "woT": split(w["attn_wo"].T),
        "w1T": split(w["attn_w1"].T),
        "w2T": split(w["attn_w2"].T),
        "w2n": split(w["attn_w2"]),
        "b1row": np.ascontiguousarray(np.broadcast_to(w["attn_b1"][None, :], (P, HID))),
        "b1c": np.ascontiguousarray(w["attn_b1"].reshape(HC, P).T),
        "b2c": np.ascontiguousarray(w["attn_b2"].reshape(DC, P).T),
        "alpha": np.ascontiguousarray(np.broadcast_to(w["attn_alpha"].reshape(1, 1), (P, 1))),
        "theta": np.ascontiguousarray(np.broadcast_to(w["attn_theta"].reshape(1, 1), (P, 1))),
        "linT": np.ascontiguousarray(np.stack([split(w["attn_lin1"].T), split(w["attn_lin2"].T)], axis=1)),
        "wgT": split(w["ffn_wg"].T),
        "s1T": split(w["ffn_shared_w1"].T),
        "s2T": split(w["ffn_shared_w2"].T),
        "e1T": np.ascontiguousarray(e1.reshape(E, 2 * FFN, DC, P).transpose(0, 3, 2, 1)),
        "e2T": np.ascontiguousarray(e2.reshape(E, D, FC, P).transpose(0, 3, 2, 1)),
        "c": np.ascontiguousarray(w["c"].reshape(DC, P).T),
        "wmod": split(w["wmod"]),
    }
    nc = bacc.Bacc("TRN2", target_bir_lowering=False, num_devices=1)
    T = {k: nc.dram_tensor("in_" + k, v.shape, mybir.dt.from_np(v.dtype), kind="ExternalInput").ap()
         for k, v in arrays.items()}
    T["out"] = nc.dram_tensor("out_rows", (TOKENS + CAP, D), F32, kind="ExternalOutput").ap()
    T["slots"] = nc.dram_tensor("slots", (E * CAP, ROW), F32, kind="Internal").ap()
    build(nc, T)
    r = run_bass_kernel_spmd(nc, [{"in_" + k: v for k, v in arrays.items()}], core_ids=[0])
    return r.results[0]["out_rows"][:TOKENS].reshape(1, TOKENS, D)
```

```python
from contextlib import ExitStack

import concourse.bass as bass
from concourse import mybir

F32 = mybir.dt.float32
F32R = mybir.dt.float32r
BF16 = mybir.dt.bfloat16
I32 = mybir.dt.int32
U32 = mybir.dt.uint32
ALU = mybir.AluOpType
ACT = mybir.ActivationFunctionType
AX = mybir.AxisListType.X

P = 128
D = 256
DC = D // P
HID = 1024
HC = HID // P
HEADS = 4
DH = D // HEADS
MEM = 64
TOKENS = 4096
TILES = TOKENS // P
CH = 512
TPC = CH // P
CHUNKS = TOKENS // CH
E = 64
TOPK = 8
FFN = 768
FC = FFN // P
CAP = 160
CAP_B = CAP - P
ROW = D + 2
NEG = -1e30
EPS = 1e-5
F32_EPS = 1.1920929e-07
OFF_LIST = 20000
HEAD_AT = [0, 2, 1, 3]


def wait_past(engine, sem, value):
    if isinstance(value, int) and value <= 0:
        return
    engine.wait_ge(sem, value)


def wait_apart(engine, sem, value, passed):
    engine.wait_ge(sem, value)
    engine.sem_inc(passed, 1)


def flat(a):
    names = "abcd"[:len(a.shape) - 1]
    return a.rearrange(f"p {' '.join(names)} -> p ({' '.join(names)})")


def mm_split(nc, out, w, x, first, last):
    pairs = ((w[0], x[0]), (w[0], x[1]), (w[1], x[0]))
    for i, (a, b) in enumerate(pairs):
        ins = nc.tensor.matmul(out, a, b, start=first and i == 0, stop=last and i == 2, skip_group_check=True)
    return ins


class Sems:

    def __init__(self, nc, prefix):
        self.nc, self.prefix, self.made = nc, prefix, {}

    def __call__(self, name):
        if name not in self.made:
            self.made[name] = self.nc.alloc_semaphore(self.prefix + name)
        return self.made[name]

    def clear(self):
        self.nc.clear_and_free_semaphores(list(self.made.values()))
        self.nc.all_engine_barrier()


RSQRT_STEPS = 3
RSQRT_OPS = 3 + 3 * RSQRT_STEPS


def inverse_sqrt(dve, done, calls, y, var, t):
    ops = [
        lambda: dve.tensor_scalar(var, var, EPS, None, ALU.add),
        lambda: dve.tensor_scalar(t.bitcast(I32), var.bitcast(I32), 1, None, ALU.logical_shift_right),
        lambda: dve.tensor_scalar(y.bitcast(I32), t.bitcast(I32), -1.0, float(0x5F3759DF), ALU.mult, ALU.add),
    ] + [
        lambda: dve.tensor_tensor(t, y, y, ALU.mult),
        lambda: dve.scalar_tensor_tensor(out=t, in0=t, scalar=-0.5, in1=var, op0=ALU.mult, op1=ALU.mult),
        lambda: dve.scalar_tensor_tensor(out=y, in0=t, scalar=1.5, in1=y, op0=ALU.add, op1=ALU.mult),
    ] * RSQRT_STEPS
    for k, op in enumerate(ops):
        op().then_inc(done, 1)
        dve.wait_ge(done, calls * RSQRT_OPS + k + 1)


def shared_buffers(nc, ctx, inner):
    def sb(where, name, shape, dt=F32):
        return where.enter_context(nc.sbuf_tensor(name, shape, dt))
    return {
        "mod": sb(ctx, "mod", [P, 6, D]),
        "ident": sb(ctx, "ident", [P, P]),
        "w1T": [sb(inner, f"w1T_{part}", [P, DC, HID], F32R) for part in ("high", "low")],
        "w2T": [sb(inner, f"w2T_{part}", [P, HC, D], F32R) for part in ("high", "low")],
        "b1c": sb(inner, "b1c", [P, HC]),
        "b2c": sb(inner, "b2c", [P, DC]),
    }


def cut(pair, *at):
    return tuple(t[at] for t in pair)


def memory_stage(nc, T, buf, psum, S):
    with ExitStack() as ctx:
        def sb(name, shape, dt=F32):
            return ctx.enter_context(nc.sbuf_tensor("a_" + name, shape, dt))

        def split(name, shape):
            return sb(name + "_high", shape, F32R), sb(name + "_low", shape, F32R)

        w1T, w2T, mod, ident, b1c, b2c = (buf[k] for k in ("w1T", "w2T", "mod", "ident", "b1c", "b2c"))
        wqk = sb("wqk", [P, 2, DC, D])
        wv = split("wv", [P, DC, D])
        woT = sb("woT", [P, DC, D])
        w2n = split("w2n", [P, DC, HID])
        b1row = sb("b1row", [P, HID])
        b2row = sb("b2row", [P, D])
        alpha = sb("alpha", [P, 1])
        theta = sb("theta", [P, 1])
        keep = sb("keep", [P, 1])
        step = sb("step", [P, 1])
        cond = sb("cond", [P, DC])
        cond_s = sb("cond_s", [P, DC])
        cond_w = sb("cond_w", [P, DC, P])
        ones = sb("ones", [P, P])
        clamp = sb("clamp", [P, 2, D])
        masks = sb("masks", [P, 4, 2 * P])
        fill = sb("fill", [P, ROW])
        slot_id = sb("slot_id", [P, 2], I32)
        dW1T = sb("dW1T", [P, DC, HID])
        dW2 = sb("dW2", [P, DC, HID])
        dz_sum = sb("dz_sum", [P, HID])
        e_sum = sb("e_sum", [P, D])
        db = sb("db", [P, HC + DC])
        x_pre = [sb(f"x_pre{p}", [P, TPC, D]) for p in range(2)]
        stats = sb("stats", [P, TILES, 6])
        moments = sb("moments", [P, TILES, 2])
        rstd = sb("rstd", [P, TILES])
        half = sb("half", [P, TILES])
        x_in = [sb(f"x_in{p}", [P, D]) for p in range(2)]
        xn = sb("xn", [P, D])
        xm = sb("xm", [P, D])
        xms = [split(f"xm{p}", [P, D]) for p in range(2)]
        xT = sb("xT", [P, DC, P])
        xTs = split("xT", [P, DC, P])
        qT = sb("qT", [P, DC, P])
        kT = sb("kT", [P, DC, 2, P])
        v = sb("v", [P, 2, D])
        logit = sb("logit", [P, HEADS, 2 * P])
        peak = sb("peak", [P, HEADS])
        npeak = sb("npeak", [P, HEADS])
        psums = sb("psums", [P, HEADS])
        prec = sb("prec", [P, HEADS])
        prob = sb("prob", [P, HEADS, 2 * P])
        probT = sb("probT", [P, HEADS, 2, P])
        oT = sb("oT", [P, DC, P])
        swa = sb("swa", [P, D])
        swaT = sb("swaT", [P, DC, P])
        zb = sb("zb", [P, HID])
        sg = sb("sg", [P, HID])
        h = sb("h", [P, HID])
        hsp = [split(f"h{p}", [P, HID]) for p in range(2)]
        gp = sb("gp", [P, HID])
        hT = split("hT", [P, HC, P])
        pred = sb("pred", [P, D])
        e = sb("e", [P, D])
        es = split("e", [P, D])
        eT = split("eT", [P, DC, P])
        dz = sb("dz", [P, HID])
        dzs = split("dz", [P, HID])
        wmod = [t[:].rearrange("p a b -> p (a b)").rearrange("p (k n) -> p k n", k=DC) for t in (logit, prob)]
        wmod.append(probT[:].rearrange("p a b c -> p (a b c)").rearrange("p (k n) -> p k n", k=DC))
        w2n_raw = sb("w2n_raw", [P, DC, HID])
        wv_raw = sb("wv_raw", [P, DC, D])

        def bank(b, n=CH):
            return psum[b][:, 0:n]

        def mm(out, lhsT, rhs, first, last):
            return nc.tensor.matmul(out, lhsT, rhs, start=first, stop=last, skip_group_check=True)

        LAST = TILES
        DW_BANK = (1, 2, 3, 4, 5, 6, 7, 0)

        def known(n, least):
            return not isinstance(n, int) or n >= least

        x_rows = T["x"]
        x_chunks = T["x"].rearrange("(c t p) d -> c p t d", p=P, t=TPC)
        block = ctx.enter_context(nc.Block())

        @block.sync
        def _(sp):
            sp.dma_start(cond[:], T["c"]).then_inc(S("cond_in"), 16)
            sp.dma_start(x_in[0][P - MEM:P, :], T["mem"]).then_inc(S("mem_in"), 16)
            for c in range(2):
                sp.dma_start(x_pre[c][:], x_chunks[c]).then_inc(S(f"x_pre{c}"), 16)
            for j in range(3):
                sp.dma_start(wmod[j], T["wmod"][:, :, j * CH:(j + 1) * CH]).then_inc(S("wmod_in"), 16)
            sp.dma_start(wqk[:], T["wqkT"]).then_inc(S("wqk_in"), 16)
            sp.dma_start(wv_raw[:], T["wvT"]).then_inc(S("wv_in"), 16)
            sp.dma_start(dW1T[:], T["w1T"]).then_inc(S("w1_in"), 16)
            sp.dma_start(b1row[:], T["b1row"]).then_inc(S("b1row_in"), 16)
            sp.dma_start(dW2[:].rearrange("p k n -> p (k n)"), T["w2T"].rearrange("p k n -> p (k n)"))\
              .then_inc(S("w2T_in"), 16)
            sp.dma_start(b2row[:], T["b2row"]).then_inc(S("b1row_in"), 16)
            sp.dma_start(woT[:], T["woT"]).then_inc(S("wo_in"), 16)
            sp.dma_start(w2n_raw[:], T["w2n"]).then_inc(S("w2n_in"), 16)
            sp.dma_start(x_in[1][:], x_rows[0:P, :]).then_inc(S("x_in1"), 16)
            for c in range(2, CHUNKS):
                sp.wait_ge(S("stats"), c - 1)
                sp.dma_start(x_pre[c % 2][:], x_chunks[c]).then_inc(S(f"x_pre{c % 2}"), 16)
            for name, into in (("b2c", b2c), ("b1c", b1c), ("alpha", alpha), ("theta", theta)):
                sp.dma_start(into[:], T[name]).then_inc(S("small_in"), 16)

            def step(n, p):
                sp.wait_ge(S("xn"), n) if known(n, 1) else sp.wait_ge(S("xm"), 1)
                sp.dma_start(x_in[p][:], x_rows[bass.ds((n + 1) * P, P), :]).then_inc(S(f"x_in{p}"), 16)
                keep_xT(n)
                keep_swaT(n - 1)

            def keep_xT(n):
                if known(n, 1):
                    sp.wait_ge(S("xT"), n + 1)
                    sp.dma_start(T["xT"][bass.ds((n - 1) * P, P), :], flat(xT[:])).then_inc(S("xT_out"), 16)

            def keep_swaT(n):
                if known(n, 1):
                    sp.wait_ge(S("swaT"), n + 1)
                    sp.dma_start(T["swaT"][bass.ds((n - 1) * P, P), :], flat(swaT[:])).then_inc(S("swaT_out"), 16)

            step(0, 0)
            step(1, 1)
            step(2, 0)
            with sp.Fori(1, TILES // 2 - 1) as i:
                step(i * 2 + 1, 1)
                step(i * 2 + 2, 0)
            for n in (LAST - 1, LAST):
                keep_xT(n)
                keep_swaT(n - 1)
            keep_swaT(LAST)
            sp.wait_ge(S("fill"), 1)
            slots = T["slots"].rearrange("(e r) d -> r e d", e=E)
            fill_b = fill[:, :].unsqueeze(1).to_broadcast([P, E, ROW])
            sp.dma_start(slots[0:P], fill_b).then_inc(S("slots_out"), 16)
            sp.dma_start(T["out"][TOKENS:TOKENS + P, :], fill[:, 0:D]).then_inc(S("spare_out"), 16)
            sp.dma_start(T["out"][TOKENS + P:TOKENS + CAP, :], fill[0:CAP_B, 0:D]).then_inc(S("spare_out"), 16)
            sp.wait_ge(S("slots_out"), 16)
            sp.wait_ge(S("spare_out"), 32)
            sp.wait_ge(S("fill"), 2)
            sp.dma_start(slots[P:CAP], fill_b[0:CAP_B]).then_inc(S("slots_out"), 16)
            sp.wait_ge(S("slots_out"), 32)
            sp.wait_ge(S("xT_out"), 16 * TILES)
            sp.wait_ge(S("swaT_out"), 16 * TILES)

        @block.gpsimd
        def _(pool):
            pool.memset(ident[:], 0.0)
            pool.memset(ones[:], 1.0).then_inc(S("ones"), 1)
            pool.memset(x_in[0][0:P - MEM, :], 0.0)
            pool.memset(kT[:, :, 1, :], 0.0)
            pool.memset(v[:, 1, :], 0.0).then_inc(S("kv_zero"), 1)
            pool.memset(dz_sum[:], 0.0)
            pool.memset(e_sum[:], 0.0)
            pool.memset(fill[:], 0.0)
            pool.memset(masks[:], 0.0).then_inc(S("zeroed"), 1)
            pool.wait_ge(S("zeroed"), 1)
            pool.affine_select(out=ident[:], in_=ident[:], compare_op=ALU.not_equal, fill=1.0, base=0,
                               pattern=[[-1, P]], channel_multiplier=1).then_inc(S("ident"), 1)
            for m, own in ((0, 0), (1, 1), (2, 0), (3, 1)):
                prev = 1 - own
                a = masks[:, m, own * P:(own + 1) * P]
                pool.affine_select(out=a, in_=a, compare_op=ALU.is_ge, fill=NEG, base=0,
                                   pattern=[[-1, P]], channel_multiplier=1)
                b = masks[:, m, prev * P:(prev + 1) * P]
                pool.affine_select(out=b, in_=b, compare_op=ALU.is_gt, fill=NEG, base=0,
                                   pattern=[[1, P]], channel_multiplier=-1).then_inc(S("banded"), 1)
            pool.wait_ge(S("banded"), 4)
            pool.memset(masks[:, 0, P:2 * P], NEG)
            pool.memset(masks[:, 0, 0:P - MEM], NEG)
            pool.memset(masks[:, 1, 0:P - MEM], NEG).then_inc(S("masks"), 1)
            pool.iota(slot_id[:, 0:1], pattern=[[0, 1]], base=TOKENS, channel_multiplier=1)
            pool.iota(slot_id[:, 1:2], pattern=[[0, 1]], base=TOKENS + P, channel_multiplier=1).then_inc(S("slot_id"), 1)
            pool.wait_ge(S("slot_id"), 1)
            pool.tensor_copy(fill[:, D + 1:D + 2].bitcast(I32), slot_id[:, 0:1]).then_inc(S("fill"), 1)
            pool.wait_ge(S("mem_in"), 16)
            pool.tensor_copy(xm[:], x_in[0][:]).then_inc(S("xm"), 1)

            def modulate(n):
                pool.wait_ge(S("xn"), n)
                pool.wait_ge(S("xT_mm"), n)
                pool.wait_ge(S("xm_low"), n)
                pool.tensor_tensor(xm[:], xn[:], mod[:, 1, :], ALU.mult).then_inc(S("xm_scaled"), 1)
                pool.wait_ge(S("xm_scaled"), n)
                pool.tensor_tensor(xm[:], xm[:], mod[:, 0, :], ALU.add).then_inc(S("xm"), 1)

            pool.wait_ge(S("mod"), 1)

            def sums(m):
                pool.wait_ge(S("dz"), 2 * m + 2)
                wait_past(pool, S("dz_sum"), m)
                pool.tensor_tensor(dz_sum[:], dz_sum[:], dz[:], ALU.add).then_inc(S("dz_sum"), 1)

            def body(n, more):
                pool.wait_ge(S("prec"), n + 1)
                pool.tensor_tensor(prob[:], prob[:], prec[:].unsqueeze(2).to_broadcast([P, HEADS, 2 * P]),
                                   ALU.mult).then_inc(S("prob"), 1)
                pool.wait_ge(S("sg"), n + 1)
                wait_past(pool, S("hT_mm"), 2 * n)
                wait_past(pool, S("h_low"), n)
                pool.tensor_tensor(h[:], zb[:], sg[:], ALU.mult).then_inc(S("h"), 1)
                if more:
                    modulate(n + 1)
                wait_past(pool, S("dz"), 2 * n)
                pool.wait_ge(S("h"), n + 1)
                pool.tensor_tensor(gp[:], h[:], sg[:], ALU.mult).then_inc(S("h_sg"), 1)
                pool.wait_ge(S("h_sg"), n + 1)
                pool.tensor_tensor(sg[:], h[:], sg[:], ALU.add).then_inc(S("h_plus"), 1)
                pool.wait_ge(S("h_plus"), n + 1)
                pool.tensor_tensor(gp[:], sg[:], gp[:], ALU.subtract).then_inc(S("gp"), 1)
                if known(n, 1):
                    sums(n - 1)
                pool.wait_ge(S("e"), n + 1)
                wait_past(pool, S("e_sum"), n)
                pool.tensor_tensor(e_sum[:], e_sum[:], e[:], ALU.add).then_inc(S("e_sum"), 1)

            body(0, True)
            body(1, True)
            body(2, True)
            with pool.Fori(1, TILES // 2 - 1) as i:
                body(i * 2 + 1, True)
                body(i * 2 + 2, True)
            body(LAST - 1, True)
            body(LAST, False)
            sums(LAST)
            pool.wait_ge(S("slots_out"), 16)
            pool.wait_ge(S("spare_out"), 32)
            pool.tensor_copy(fill[:, D + 1:D + 2].bitcast(I32), slot_id[:, 1:2]).then_inc(S("fill"), 1)

        @block.scalar
        def _(act):
            act.wait_ge(S("cond_in"), 16)
            act.activation(cond_s[:], cond[:], ACT.Sigmoid).then_inc(S("cond_s"), 1)
            for name, raw, high in (("wv", wv_raw, wv[0]), ("w1", dW1T, w1T[0]), ("w2T", dW2, w2T[0]),
                                    ("w2n", w2n_raw, w2n[0])):
                act.wait_ge(S(name + "_in"), 16)
                act.copy(flat(high[:]), flat(raw[:])).then_inc(S("w_high"), 1)

            def turned(n):
                act.wait_ge(S("xT_mm"), n + 1)
                wait_past(act, S("qk_mm"), n)
                wait_past(act, S("xT_out"), (n - 1) * 16)
                act.copy(flat(xT[:]), bank(6, D)).then_inc(S("xT"), 1)
                wait_past(act, S("z_mm"), 2 * n)
                act.copy(flat(xTs[0][:]), bank(6, D)).then_inc(S("xT_high"), 1)

            def error_high(m):
                act.wait_ge(S("e"), m + 1)
                wait_past(act, S("dW_mm"), 8 * m)
                act.copy(es[0][:], e[:]).then_inc(S("e_high"), 1)
                act.wait_ge(S("eT_mm"), m + 1)
                wait_past(act, S("dh_mm"), 2 * m)
                act.copy(flat(eT[0][:]), bank(2, D)).then_inc(S("eT_high"), 1)
                wait_past(act, S("swaT_out"), (m - 1) * 16)
                act.copy(flat(swaT[:]), psum[2][:, D:2 * D]).then_inc(S("swaT"), 1)

            def dz_high(m):
                wait_past(act, S("dW_mm"), 8 * m)
                for g in range(2):
                    act.wait_ge(S("dz"), 2 * m + g + 1)
                    act.copy(dzs[0][:, g * CH:(g + 1) * CH], dz[:, g * CH:(g + 1) * CH]).then_inc(S("dz_high"), 1)

            def body(n, p, more):
                act.wait_ge(S("v_mm"), n + 1)
                wait_past(act, S("o_mm"), n)
                if not known(n, 1):
                    act.wait_ge(S("kv_zero"), 1)
                act.copy(v[:, p, :], bank(1, D)).then_inc(S("v"), 1)
                if known(n, 1):
                    error_high(n - 1)
                act.wait_ge(S("npeak"), n + 1)
                wait_past(act, S("probT_mm"), 2 * n)
                for s in range(HEADS):
                    ins = act.activation(prob[:, s, :], logit[:, s, :], ACT.Exp, bias=npeak[:, s:s + 1],
                                         accum_out=psums[:, s:s + 1])
                ins.then_inc(S("prob_exp"), 1)
                act.wait_ge(S("zb"), 2 * n + 2)
                wait_past(act, S("gp"), n)
                act.activation(sg[:], zb[:], ACT.Sigmoid).then_inc(S("sg"), 1)
                if known(n, 1):
                    dz_high(n - 1)
                act.wait_ge(S("xm"), n + 1)
                wait_past(act, S("dW_mm"), 8 * n - 8)
                act.copy(xms[p][0][:], xm[:]).then_inc(S("xm_high"), 1)
                act.wait_ge(S("h"), n + 1)
                act.copy(hsp[p][0][:], h[:]).then_inc(S("h_high"), 1)
                act.wait_ge(S("probT_mm"), 2 * n + 2)
                wait_past(act, S("o_mm"), n)
                act.copy(flat(probT[:, 2:4, :, :]), bank(2)).then_inc(S("probT_hi"), 1)
                for g in range(2):
                    act.wait_ge(S("hT_mm"), 2 * n + g + 1)
                    wait_past(act, S("pred_mm"), n)
                    act.copy(flat(hT[0][:, 4 * g:4 * g + 4, :]), bank(3 + g)).then_inc(S("hT_high"), 1)
                if more:
                    turned(n + 1)
                act.wait_ge(S("swa_mm"), n + 1)
                wait_past(act, S("eT_mm"), n)
                wait_past(act, S("e"), n)
                act.copy(swa[:], psum[7][:, D:2 * D]).then_inc(S("swa"), 1)

            turned(0)
            body(0, 0, True)
            body(1, 1, True)
            body(2, 0, True)
            with act.Fori(1, TILES // 2 - 1) as i:
                body(i * 2 + 1, 1, True)
                body(i * 2 + 2, 0, True)
            body(LAST - 1, 1, True)
            body(LAST, 0, False)
            error_high(LAST)
            dz_high(LAST)
            act.wait_ge(S("w1_new"), 1)
            act.copy(flat(w1T[0][:]), flat(dW1T[:])).then_inc(S("w_high"), 1)
            for g in range(4):
                act.wait_ge(S("w2T_mm"), g + 1)
                act.copy(flat(w2T[0][:, 2 * g:2 * g + 2, :]), bank(g)).then_inc(S("w_high"), 1)

        @block.vector
        def _(dve):
            for c in range(CHUNKS):
                dve.wait_ge(S(f"x_pre{c % 2}"), 16 * (c // 2 + 1))
                for t in range(TPC):
                    ins = dve.bn_stats(stats[:, c * TPC + t, :], x_pre[c % 2][:, t, :])
                ins.then_inc(S("stats"), 1)
                if c == 0:
                    dve.wait_ge(S("cond_s"), 1)
                    dve.tensor_tensor(cond_s[:], cond_s[:], cond[:], ALU.mult).then_inc(S("cond_silu"), 1)
                    dve.wait_ge(S("cond_silu"), 1)
                    dve.wait_ge(S("ones"), 1)
                    for k in range(DC):
                        ins = dve.tensor_scalar(cond_w[:, k, :], ones[:], cond_s[:, k:k + 1], None, ALU.mult)
                    ins.then_inc(S("cond_w"), 1)
                if c == 1:
                    dve.wait_ge(S("w_high"), 1)
                    dve.tensor_tensor(flat(wv[1][:]), flat(wv_raw[:]), flat(wv[0][:]).bitcast(F32), ALU.subtract)\
                       .then_inc(S("w_low"), 1)
                if c == 2:
                    dve.wait_ge(S("mod_mm"), 1)
                    for j in range(3):
                        ins = dve.tensor_copy(flat(mod[:, 2 * j:2 * j + 2, :]), bank(j))
                    ins.then_inc(S("mod_copied"), 1)
            dve.wait_ge(S("stats"), CHUNKS)
            for t in range(TILES):
                ins = dve.bn_aggr(moments[:, t, :], stats[:, t, :])
            ins.then_inc(S("moments"), 1)
            dve.wait_ge(S("moments"), 1)
            inverse_sqrt(dve, S("rstd"), 0, rstd[:], moments[:, :, 1], half[:])
            dve.wait_ge(S("mod_copied"), 1)
            for j in (1, 4):
                dve.tensor_scalar(mod[:, j, :], mod[:, j, :], 1.0, None, ALU.add)
            for j, g in enumerate((2, 5)):
                dve.scalar_tensor_tensor(out=clamp[:, j, :], in0=mod[:, g, :], scalar=-1.0, in1=mod[:, g, :],
                                         op0=ALU.mult, op1=ALU.max).then_inc(S("clamped"), 1)
                dve.wait_ge(S("clamped"), 3 * j + 1)
                dve.tensor_scalar(clamp[:, j, :], clamp[:, j, :], 0.25, None, ALU.max)
                dve.tensor_scalar(mod[:, g, :], mod[:, g, :], 0.0, 2.0, ALU.is_ge, ALU.mult).then_inc(S("clamped"), 1)
                dve.wait_ge(S("clamped"), 3 * j + 2)
                dve.scalar_tensor_tensor(out=mod[:, g, :], in0=mod[:, g, :], scalar=-1.0, in1=clamp[:, j, :],
                                         op0=ALU.add, op1=ALU.mult).then_inc(S("clamped"), 1)
            dve.wait_ge(S("clamped"), 6)
            dve.memset(peak[:], 0.0).then_inc(S("mod"), 1)
            for i, (raw, pair) in enumerate(((dW1T, w1T), (dW2, w2T), (w2n_raw, w2n))):
                dve.wait_ge(S("w_high"), i + 2)
                dve.tensor_tensor(flat(pair[1][:]), flat(raw[:]), flat(pair[0][:]).bitcast(F32), ALU.subtract)\
                   .then_inc(S("w_low"), 1)
            dve.wait_ge(S("w_low"), 4)
            dve.memset(dW1T[:], 0.0)
            dve.memset(dW2[:], 0.0).then_inc(S("d_zero"), 1)
            dve.wait_ge(S("mod"), 1)
            dve.wait_ge(S("b1row_in"), 32)
            dve.wait_ge(S("masks"), 1)

            def normalise(n, p, loads):
                dve.wait_ge(S(f"x_in{p}"), loads * 16)
                wait_past(dve, S("xm_scaled"), n - 1)
                m = n - 1
                dve.tensor_scalar(xn[:], x_in[p][:], moments[:, bass.ds(m, 1), 0], rstd[:, bass.ds(m, 1)],
                                  ALU.subtract, ALU.mult).then_inc(S("xn"), 1)

            def turned_low(n):
                dve.wait_ge(S("xT_high"), n + 1)
                wait_past(dve, S("z_mm"), 2 * n)
                dve.tensor_tensor(flat(xTs[1][:]), bank(6, D), flat(xTs[0][:]).bitcast(F32), ALU.subtract)\
                   .then_inc(S("xT_low"), 1)

            def error_low(m):
                dve.wait_ge(S("e_high"), m + 1)
                wait_past(dve, S("dW_mm"), 8 * m)
                dve.tensor_tensor(es[1][:], e[:], es[0][:].bitcast(F32), ALU.subtract).then_inc(S("e_low"), 1)
                dve.wait_ge(S("eT_high"), m + 1)
                wait_past(dve, S("dh_mm"), 2 * m)
                dve.wait_ge(S("swaT"), m + 1)
                dve.tensor_tensor(flat(eT[1][:]), bank(2, D), flat(eT[0][:]).bitcast(F32), ALU.subtract)\
                   .then_inc(S("eT_low"), 1)

            def grad_z(m):
                dve.wait_ge(S("gp"), m + 1)
                wait_past(dve, S("dW_mm"), 8 * m)
                wait_past(dve, S("dz_sum"), m)
                for g in range(2):
                    dve.wait_ge(S("dh_mm"), 2 * m + g + 1)
                    dve.tensor_tensor(dz[:, g * CH:(g + 1) * CH], bank((7, 0)[g]), gp[:, g * CH:(g + 1) * CH],
                                      ALU.mult).then_inc(S("dz"), 1)
                for g in range(2):
                    dve.wait_ge(S("dz_high"), 2 * m + g + 1)
                    c = slice(g * CH, (g + 1) * CH)
                    dve.tensor_tensor(dzs[1][:, c], dz[:, c], dzs[0][:, c].bitcast(F32), ALU.subtract)\
                       .then_inc(S("dz_low"), 1)

            def gather_dW(m, js):
                for j in js:
                    into = dW2 if j < 4 else dW1T
                    part = into[:, (j % 4) // 2, (j % 2) * CH:(j % 2 + 1) * CH]
                    dve.wait_ge(S("dW_mm"), 8 * m + j + 1)
                    wait_past(dve, S("dW"), 8 * m + j - 7)
                    dve.tensor_tensor(part, part, bank(DW_BANK[j]), ALU.add).then_inc(S("dW"), 1)

            def body(n, p, mask, loads):
                dve.wait_ge(S("qk_mm"), n + 1)
                wait_past(dve, S("s_mm"), 2 * n)
                dve.tensor_copy(flat(qT[:]), bank(0, D))
                if not known(n, 1):
                    dve.wait_ge(S("kv_zero"), 1)
                dve.tensor_copy(kT[:, :, p, :], psum[0][:, D:2 * D].rearrange("p (c t) -> p c t", c=DC))\
                   .then_inc(S("qk"), 1)
                if known(n, 1):
                    error_low(n - 1)
                for s in range(HEADS):
                    wait_past(dve, S("prob_exp"), n)
                    wait_apart(dve, S("s_mm"), 2 * n + s // 2 + 1, S("passed_dve"))
                    ins = dve.tensor_tensor_reduce(
                        out=logit[:, s, :], in0=psum[3 + s // 2][:, (s % 2) * D:(s % 2 + 1) * D], in1=masks[:, mask, :],
                        scale=float(DH) ** -0.5, scalar=-3e38, op0=ALU.add, op1=ALU.max, accum_out=peak[:, s:s + 1])
                    if s % 2:
                        ins.then_inc(S("peak"), 1)
                dve.wait_ge(S("peak"), 2 * n + 2)
                dve.tensor_scalar(npeak[:], peak[:], -1.0, None, ALU.mult).then_inc(S("npeak"), 1)
                for g in range(2):
                    dve.wait_ge(S("z_mm"), 2 * n + g + 1)
                    wait_past(dve, S("h"), n)
                    dve.tensor_tensor(zb[:, g * CH:(g + 1) * CH], bank(5 + g), b1row[:, g * CH:(g + 1) * CH], ALU.add)\
                       .then_inc(S("zb"), 1)
                dve.wait_ge(S("prob_exp"), n + 1)
                wait_past(dve, S("prob"), n)
                dve.reciprocal(prec[:], psums[:]).then_inc(S("prec"), 1)
                if loads is not None:
                    normalise(n + 1, 1 - p, loads)
                if known(n, 1):
                    if isinstance(n, int) and n == 1:
                        dve.wait_ge(S("d_zero"), 1)
                    grad_z(n - 1)
                    gather_dW(n - 1, range(4))
                dve.wait_ge(S("xm_high"), n + 1)
                dve.tensor_tensor(xms[p][1][:], xm[:], xms[p][0][:].bitcast(F32), ALU.subtract)\
                   .then_inc(S("xm_low"), 1)
                if known(n, 1):
                    gather_dW(n - 1, range(4, 8))
                dve.wait_ge(S("probT_mm"), 2 * n + 1)
                wait_past(dve, S("o_mm"), n)
                dve.tensor_copy(flat(probT[:, 0:2, :, :]), bank(1)).then_inc(S("probT_lo"), 1)
                for g in range(2):
                    dve.wait_ge(S("hT_high"), 2 * n + g + 1)
                    wait_past(dve, S("pred_mm"), n)
                    dve.tensor_tensor(flat(hT[1][:, 4 * g:4 * g + 4, :]), bank(3 + g),
                                      flat(hT[0][:, 4 * g:4 * g + 4, :]).bitcast(F32), ALU.subtract)\
                       .then_inc(S("hT_low"), 1)
                dve.wait_ge(S("o_mm"), n + 1)
                wait_past(dve, S("swa_mm"), n)
                dve.tensor_copy(flat(oT[:]), bank(5, D)).then_inc(S("oT"), 1)
                if loads is not None:
                    turned_low(n + 1)
                dve.wait_ge(S("h_high"), n + 1)
                dve.tensor_tensor(hsp[p][1][:], h[:], hsp[p][0][:].bitcast(F32), ALU.subtract)\
                   .then_inc(S("h_low"), 1)
                dve.wait_ge(S("swa"), n + 1)
                wait_past(dve, S("e"), n)
                dve.tensor_tensor(pred[:], bank(7, D), b2row[:], ALU.add).then_inc(S("pred"), 1)
                dve.wait_ge(S("pred"), n + 1)
                wait_past(dve, S("eT_mm"), n)
                wait_past(dve, S("e_low"), n)
                wait_past(dve, S("e_sum"), n)
                if not known(n, 1):
                    dve.tensor_tensor(e[:], pred[:], swa[:], ALU.subtract).then_inc(S("e_raw"), 1)
                    dve.wait_ge(S("e_raw"), 1)
                    dve.memset(e[0:P - MEM, :], 0.0).then_inc(S("e"), 1)
                else:
                    dve.tensor_tensor(e[:], pred[:], swa[:], ALU.subtract).then_inc(S("e"), 1)

            turned_low(0)
            body(0, 0, 0, 1)
            body(1, 1, 1, 1)
            body(2, 0, 2, 2)
            with dve.Fori(1, TILES // 2 - 1) as i:
                body(i * 2 + 1, 1, 3, i + 1)
                body(i * 2 + 2, 0, 2, i + 2)
            body(LAST - 1, 1, 3, TILES // 2)
            body(LAST, 0, 2, None)
            error_low(LAST)
            grad_z(LAST)
            gather_dW(LAST, range(8))
            dve.wait_ge(S("small_in"), 64)
            dve.tensor_scalar(keep[:], alpha[:], -1.0, 1.0, ALU.mult, ALU.add)
            dve.tensor_scalar(step[:], theta[:], -1.0, None, ALU.mult).then_inc(S("rates"), 1)
            dve.wait_ge(S("rates"), 1)
            dve.wait_ge(S("dW"), 8 * LAST + 8)
            for i, (grad, pair) in enumerate(((dW2, w2n), (dW1T, w1T))):
                dve.tensor_scalar(grad[:], grad[:], step[:, 0:1], None, ALU.mult).then_inc(S("stepped"), 1)
                for part in range(2):
                    dve.wait_ge(S("stepped"), 3 * i + part + 1)
                    ins = dve.scalar_tensor_tensor(out=grad[:], in0=pair[part][:].bitcast(F32), scalar=keep[:, 0:1],
                                                   in1=grad[:], op0=ALU.mult, op1=ALU.add)
                    ins.then_inc(S("stepped") if part == 0 else S(("w2_new", "w1_new")[i]), 1)
                dve.wait_ge(S(("w2_new", "w1_new")[i]), 1)
                dve.memset(half[:, 0:1], 0.0).then_inc(S("stepped"), 1)
            for g in range(4):
                dve.wait_ge(S("w_high"), 4 + 1 + g + 1)
                dve.tensor_tensor(flat(w2T[1][:, 2 * g:2 * g + 2, :]), bank(g),
                                  flat(w2T[0][:, 2 * g:2 * g + 2, :]).bitcast(F32), ALU.subtract).then_inc(S("w_low"), 1)
            dve.tensor_tensor(flat(w1T[1][:]), flat(dW1T[:]), flat(w1T[0][:]).bitcast(F32), ALU.subtract)\
               .then_inc(S("w_low"), 1)
            dve.wait_ge(S("db_mm"), 1)
            dve.tensor_scalar(db[:], bank(4, HC + DC), step[:, 0:1], None, ALU.mult).then_inc(S("db"), 1)
            dve.wait_ge(S("db"), 1)
            dve.scalar_tensor_tensor(out=b1c[:], in0=b1c[:], scalar=keep[:, 0:1], in1=db[:, 0:HC],
                                     op0=ALU.mult, op1=ALU.add)
            dve.scalar_tensor_tensor(out=b2c[:], in0=b2c[:], scalar=keep[:, 0:1], in1=db[:, HC:HC + DC],
                                     op0=ALU.mult, op1=ALU.add).then_inc(S("b_new"), 1)
            dve.wait_ge(S("b_new"), 1)

        @block.tensor
        def _(pe):
            pe.wait_ge(S("cond_w"), 1)
            pe.wait_ge(S("wmod_in"), 48)
            for j in range(3):
                for k in range(DC):
                    ins = mm(bank(j), cond_w[:, k, :], wmod[j][:, k, :], k == 0, k == DC - 1)
            ins.then_inc(S("mod_mm"), 1)
            pe.wait_ge(S("mod_copied"), 1)
            pe.wait_ge(S("ident"), 1)

            def turn(out, src):
                return nc.tensor.transpose(out, src, ident[:])

            def turn_x(n):
                pe.wait_ge(S("xm"), n + 1)
                wait_past(pe, S("dW"), 8 * n - 10)
                if isinstance(n, int) and n == 1:
                    pe.wait_ge(S("zb"), 2)
                for k in range(DC):
                    ins = turn(psum[6][:, k * P:(k + 1) * P], xm[:, k * P:(k + 1) * P])
                ins.then_inc(S("xT_mm"), 1)

            def turn_error(m):
                pe.wait_ge(S("e"), m + 1)
                pe.wait_ge(S("probT_hi"), m + 1)
                for k in range(DC):
                    turn(psum[2][:, k * P:(k + 1) * P], e[:, k * P:(k + 1) * P])
                for k in range(DC):
                    ins = turn(psum[2][:, D + k * P:D + (k + 1) * P], swa[:, k * P:(k + 1) * P])
                ins.then_inc(S("eT_mm"), 1)

            def backward(m):
                pe.wait_ge(S("eT_low"), m + 1)
                if not known(m, 1):
                    pe.wait_ge(S("w_low"), 4)
                for g in range(2):
                    for k in range(DC):
                        ins = mm_split(nc, bank((7, 0)[g]), cut(eT, slice(None), k, slice(None)),
                                       cut(w2n, slice(None), k, slice(g * CH, (g + 1) * CH)), k == 0, k == DC - 1)
                    ins.then_inc(S("dh_mm"), 1)

            def gradient(m, p, tail=False):
                n = m + 1
                pe.wait_ge(S("e_low"), m + 1)
                pe.wait_ge(S("h_low"), m + 1)
                for j in range(4):
                    if j == 0:
                        pe.wait_ge(S("probT_lo" if tail else "v"), m + 1 if tail else n + 1)
                    elif j > 1 and not tail:
                        pe.wait_ge(S("peak"), 2 * n + j - 1)
                    mm_split(nc, bank(DW_BANK[j]), cut(es, slice(None), slice((j // 2) * P, (j // 2 + 1) * P)),
                             cut(hsp[p], slice(None), slice((j % 2) * CH, (j % 2 + 1) * CH)), True, True)\
                        .then_inc(S("dW_mm"), 1)
                pe.wait_ge(S("xm_low"), m + 1)
                for j in range(4, 8):
                    if j < 6 and not tail:
                        pe.wait_ge(S("zb"), 2 * n + j - 3)
                    g = j - 4
                    pe.wait_ge(S("dz_low"), 2 * m + g % 2 + 1)
                    if j == 6:
                        pe.wait_ge(S("dz"), 2 * m + 2)
                    mm_split(nc, bank(DW_BANK[j]), cut(xms[p], slice(None), slice((g // 2) * P, (g // 2 + 1) * P)),
                             cut(dzs, slice(None), slice((g % 2) * CH, (g % 2 + 1) * CH)), True, True)\
                        .then_inc(S("dW_mm"), 1)

            def body(n, p, more):
                first = not known(n, 1)
                if first:
                    pe.wait_ge(S("wqk_in"), 16)
                pe.wait_ge(S("xT"), n + 1)
                wait_past(pe, S("dW"), 8 * n - 8)
                for j in range(4):
                    for k in range(DC):
                        ins = mm(psum[0][:, j * P:(j + 1) * P], wqk[:, j // 2, k, (j % 2) * P:(j % 2 + 1) * P],
                                 xT[:, k, :], k == 0, k == DC - 1)
                ins.then_inc(S("qk_mm"), 1)
                wait_past(pe, S("probT_lo"), n)
                pe.wait_ge(S("xT_low"), n + 1)
                if first:
                    pe.wait_ge(S("w_low"), 2)
                for k in range(DC):
                    ins = mm_split(nc, bank(1, D), cut(xTs, slice(None), k, slice(None)),
                                   cut(wv, slice(None), k, slice(None)), k == 0, k == DC - 1)
                ins.then_inc(S("v_mm"), 1)
                if not first:
                    turn_error(n - 1)
                pe.wait_ge(S("qk"), n + 1)
                for b in range(2):
                    for c in range(DC):
                        ins = mm(psum[3 + b][:, c * D:(c + 1) * D], qT[b * DH:(b + 1) * DH, c, :],
                                 kT[b * DH:(b + 1) * DH, c, :, :], True, True)
                    ins.then_inc(S("s_mm"), 1)
                for g in range(2):
                    for k in range(DC):
                        ins = mm_split(nc, bank(5 + g), cut(xTs, slice(None), k, slice(None)),
                                       cut(w1T, slice(None), k, slice(g * CH, (g + 1) * CH)), k == 0, k == DC - 1)
                    ins.then_inc(S("z_mm"), 1)
                if not first:
                    backward(n - 1)
                    gradient(n - 1, 1 - p)
                pe.wait_ge(S("prob"), n + 1)
                for g in range(2):
                    wait_past(pe, S("dW"), 8 * n - 7 + g)
                    if first:
                        pe.wait_ge(S("v"), 1)
                    for b in range(4):
                        ins = turn(psum[1 + g][:, b * P:(b + 1) * P],
                                   prob[:, 2 * g + b // 2, (b % 2) * P:(b % 2 + 1) * P])
                    ins.then_inc(S("probT_mm"), 1)
                pe.wait_ge(S("h"), n + 1)
                for g in range(2):
                    wait_past(pe, S("dW"), 8 * n - 5 + g)
                    for b in range(4):
                        ins = turn(psum[3 + g][:, b * P:(b + 1) * P], h[:, (4 * g + b) * P:(4 * g + b + 1) * P])
                    ins.then_inc(S("hT_mm"), 1)
                if more:
                    turn_x(n + 1)
                pe.wait_ge(S("probT_lo"), n + 1)
                pe.wait_ge(S("probT_hi"), n + 1)
                pe.wait_ge(S("v"), n + 1)
                wait_past(pe, S("dW"), 8 * n - 3)
                for s in range(HEADS):
                    hd = HEAD_AT[s]
                    for t in range(2):
                        ins = mm(psum[5][(hd % 2) * DH:(hd % 2 + 1) * DH, (hd // 2) * P:(hd // 2 + 1) * P],
                                 v[:, t, hd * DH:(hd + 1) * DH], probT[:, s, t, :], t == 0, t == 1)
                ins.then_inc(S("o_mm"), 1)
                pe.wait_ge(S("hT_low"), 2 * n + 2)
                wait_past(pe, S("dW"), 8 * n - 1)
                for k in range(HC):
                    ins = mm_split(nc, bank(7, D), cut(hT, slice(None), k, slice(None)),
                                   cut(w2T, slice(None), k, slice(None)), k == 0, k == HC - 1)
                ins.then_inc(S("pred_mm"), 1)
                if first:
                    pe.wait_ge(S("wo_in"), 16)
                pe.wait_ge(S("oT"), n + 1)
                for k in range(DC):
                    ins = mm(psum[7][:, D:2 * D], oT[:, k, :], woT[:, k, :], k == 0, k == DC - 1)
                ins.then_inc(S("swa_mm"), 1)

            turn_x(0)
            body(0, 0, True)
            body(1, 1, True)
            body(2, 0, True)
            with pe.Fori(1, TILES // 2 - 1) as i:
                body(i * 2 + 1, 1, True)
                body(i * 2 + 2, 0, True)
            body(LAST - 1, 1, True)
            body(LAST, 0, False)
            turn_error(LAST)
            backward(LAST)
            gradient(LAST, 0, tail=True)
            pe.wait_ge(S("dz_sum"), LAST + 1)
            pe.wait_ge(S("e_sum"), LAST + 1)
            pe.wait_ge(S("dW"), 8 * LAST + 4)
            for j in range(HC):
                mm(psum[4][:, j:j + 1], dz_sum[:, j * P:(j + 1) * P], ones[:, 0:1], True, True)
            for j in range(DC):
                ins = mm(psum[4][:, HC + j:HC + j + 1], e_sum[:, j * P:(j + 1) * P], ones[:, 0:1], True, True)
            ins.then_inc(S("db_mm"), 1)
            pe.wait_ge(S("w2_new"), 1)
            for g in range(4):
                for b in range(4):
                    j, k = 2 * g + b // 2, b % 2
                    ins = turn(psum[g][:, b * P:(b + 1) * P], dW2[:, k, j * P:(j + 1) * P])
                ins.then_inc(S("w2T_mm"), 1)


def token_stage(nc, T, buf, psum, S):
    with ExitStack() as ctx:
        def sb(name, shape, dt=F32):
            return ctx.enter_context(nc.sbuf_tensor("b_" + name, shape, dt))

        def split(name, shape):
            return sb(name + "_high", shape, F32R), sb(name + "_low", shape, F32R)

        w1T, w2T, mod, ident, b1c, b2c = (buf[k] for k in ("w1T", "w2T", "mod", "ident", "b1c", "b2c"))
        linT = sb("linT", [P, 2, DC, D])
        wgT = sb("wgT", [P, DC, E])
        s1T = split("s1T", [P, DC, 2 * FFN])
        s2T = sb("s2T", [P, FC, D])
        before = sb("before", [P, P], BF16)
        every = sb("every", [P, P], BF16)
        slot_base = sb("slot_base", [P, E])
        token = sb("token", [P, TPC], I32)
        carry = sb("carry", [P, E])
        xT = sb("xT", [P, TPC, D])
        xTs = split("xT", [P, TPC, D])
        swaT = sb("swaT", [P, TPC, D])
        hidden = sb("hidden", [P, HC, CH])
        h2 = split("h2", [P, HC, CH])
        om = sb("om", [P, TPC, D])
        g1 = sb("g1", [P, TPC, D])
        g2 = sb("g2", [P, TPC, D])
        x = sb("x", [P, TPC, D])
        x2 = sb("x2", [P, TPC, D])
        stats = sb("stats", [P, TPC, 6])
        moments = sb("moments", [P, TPC, 2])
        rstd = sb("rstd", [P, TPC])
        half = sb("half", [P, TPC])
        hm = sb("hm", [P, TPC, D])
        hT = sb("hT", [P, DC, CH])
        hTs = split("hT", [P, DC, CH])
        lg = sb("lg", [P, TPC, E])
        lmax = sb("lmax", [P, TPC])
        gate = sb("gate", [P, TPC, E])
        gsum = sb("gsum", [P, TPC])
        grec = sb("grec", [P, TPC])
        top = sb("top", [P, TPC, TOPK])
        rest = sb("rest", [P, TPC, E])
        chosen = sb("chosen", [P, TPC, E])
        chosen_b = sb("chosen_b", [P, TPC, E], BF16)
        wsum = sb("wsum", [P, TPC])
        wrec = sb("wrec", [P, TPC])
        rank = sb("rank", [P, TPC, E])
        fits = sb("fits", [P, TPC, E])
        slot = sb("slot", [P, TPC, E])
        slot8 = sb("slot8", [P, TPC, TOPK])
        off = sb("off", [P, TPC, TOPK])
        index = sb("index", [P, TPC, TOPK], U32)
        picked = sb("picked", [P, TOPK, E])
        w8 = sb("w8", [P, TPC, TOPK])
        row = sb("row", [P, 2, TOPK, ROW])
        sil = [sb(f"sil{p}", [P, CH]) for p in range(2)]

        def bank(b, n=CH):
            return psum[b][:, 0:n]

        def mm(out, lhsT, rhs, first, last):
            return nc.tensor.matmul(out, lhsT, rhs, start=first, stop=last, skip_group_check=True)

        def wide(a, n):
            return a.unsqueeze(2).to_broadcast([P, TPC, n])

        def rows_of(a):
            return a.unsqueeze(1).to_broadcast([P, TPC, D])

        def block_of(a, k):
            return a[:, :, k * P:(k + 1) * P]

        def by_tile(a):
            return a.rearrange("p (t n) -> p t n", t=TPC)

        gT = hidden
        base = g2
        s1_raw = row[:].rearrange("p a b c -> p (a b c)")[:, 0:DC * 2 * FFN]

        x_rows = T["x"].rearrange("(c t p) d -> p (c t) d", p=P, t=TPC)
        xT_tiles = T["xT"].rearrange("(c t p) d -> p (c t) d", p=P, t=TPC)
        swaT_tiles = T["swaT"].rearrange("(c t p) d -> p (c t) d", p=P, t=TPC)
        out_rows = T["out"][0:TOKENS, :].rearrange("(c t p) d -> p (c t) d", p=P, t=TPC)
        BANK_Z = range(8)
        BANK_SH = [2, 3, 4, 5, 6, 7, 0, 1, 2, 3, 4, 5]

        block = ctx.enter_context(nc.Block())

        @block.sync
        def _(sp):
            def tiles(c):
                return bass.ds(c * TPC, TPC)

            def load_xT(c):
                wait_past(sp, S("xT_low"), c)
                sp.dma_start(xT[:], xT_tiles[:, tiles(c), :]).then_inc(S("xT_in"), 16)

            def load_swaT(c):
                wait_past(sp, S("parts"), c)
                sp.dma_start(swaT[:], swaT_tiles[:, tiles(c), :]).then_inc(S("swaT_in"), 16)

            def load(c):
                wait_past(sp, S("x2"), c)
                sp.dma_start(x[:], x_rows[:, tiles(c), :]).then_inc(S("x_in"), 16)

            def store(c):
                sp.wait_ge(S("base"), 2 * c)
                sp.dma_start(out_rows[:, tiles(c - 1), :], base[:]).then_inc(S("base_out"), 16)

            load_xT(0)
            sp.dma_start(s1_raw, T["s1T"].rearrange("p k n -> p (k n)")).then_inc(S("s1_in"), 16)
            load_swaT(0)
            sp.dma_start(linT[:], T["linT"]).then_inc(S("lin_in"), 16)
            sp.dma_start(wgT[:], T["wgT"]).then_inc(S("wg_in"), 16)
            sp.dma_start(s2T[:], T["s2T"]).then_inc(S("s2_in"), 16)
            load(0)
            load_xT(1)
            load_xT(2)
            load_swaT(1)
            load(1)
            with sp.Fori(1, CHUNKS - 2) as c:
                load_xT(c + 2)
                load_swaT(c + 1)
                store(c)
                load(c + 1)
            load_swaT(CHUNKS - 1)
            store(CHUNKS - 2)
            load(CHUNKS - 1)
            store(CHUNKS - 1)
            store(CHUNKS)
            sp.wait_ge(S("base_out"), 16 * CHUNKS)

        @block.gpsimd
        def _(pool):
            pool.memset(before[:], 1.0)
            pool.memset(every[:], 1.0)
            pool.memset(carry[:], 0.0).then_inc(S("set"), 1)
            pool.wait_ge(S("set"), 1)
            pool.affine_select(out=before[:], in_=before[:], compare_op=ALU.is_gt, fill=0.0, base=0,
                               pattern=[[1, P]], channel_multiplier=-1)
            pool.iota(slot_base[:], pattern=[[CAP, E]], base=1, channel_multiplier=0,
                      allow_small_or_imprecise_dtypes=True)
            pool.iota(token[:], pattern=[[P, TPC]], base=0, channel_multiplier=1).then_inc(S("route_const"), 1)

            def scatter(c):
                pool.wait_ge(S("index"), c)
                for t in range(TPC):
                    wait_apart(pool, S("row_part"), (c - 1) * TPC + t + 1, S("passed_pool"))
                    pool.tensor_copy(row[:, t % 2, :, D + 1:D + 2].bitcast(I32),
                                     token[:, t:t + 1].unsqueeze(1).to_broadcast([P, TOPK, 1])).then_inc(S("row"), 1)
                    wait_apart(pool, S("row"), (c - 1) * TPC + t + 1, S("passed_pool"))
                    for k in range(TOPK):
                        pool.indirect_dma_start(
                            out=T["slots"], out_offset=bass.IndirectOffsetOnAxis(ap=index[:, t, k:k + 1], axis=0),
                            in_=row[:, t % 2, k, :], in_offset=None,
                            bounds_check=last_slot, oob_is_err=False).then_inc(S(f"row_out{t % 2}"), 16)
                pool.tensor_scalar(token[:], token[:], float(CH), None, ALU.add).then_inc(S("token"), 1)
                pool.wait_ge(S("token"), c)

            last_slot = pool.to_reg(E * CAP - 1)
            scatter(1)
            with pool.Fori(2, CHUNKS + 1) as c:
                scatter(c)
            pool.wait_ge(S("row_out0"), CHUNKS * TPC // 2 * TOPK * 16)
            pool.wait_ge(S("row_out1"), CHUNKS * TPC // 2 * TOPK * 16)

        @block.scalar
        def _(act):
            def late(c):
                for g in range(2):
                    act.wait_ge(S("hT_mm"), 2 * c - 1 + g)
                    act.copy(hT[:, :, g * D:(g + 1) * D],
                             bank(g).rearrange("p (k t) -> p k t", k=DC)).then_inc(S("hT"), 1)
                act.wait_ge(S("hT"), 2 * c)
                act.copy(flat(hTs[0][:]), flat(hT[:])).then_inc(S("hT_high"), 1)
                act.wait_ge(S("lg"), c)
                act.activation(gate[:], lg[:], ACT.Exp).then_inc(S("gate_exp"), 1)

            def late_row(c, t):
                act.wait_ge(S("w8"), (c - 1) * TPC + t + 1)
                wait_past(act, S(f"row_out{t % 2}"), ((c - 1) * 2 + t // 2) * TOPK * 16)
                act.copy(row[:, t % 2, :, 0:D], hm[:, t, :].unsqueeze(1).to_broadcast([P, TOPK, D]))
                act.copy(row[:, t % 2, :, D:D + 1], w8[:, t, :].unsqueeze(2)).then_inc(S("row_part"), 1)

            def late_shared(c):
                for j in range(FC):
                    act.wait_ge(S("sh_mm"), (c - 1) * 2 * FC + 2 * j + 1)
                    wait_past(act, S("gT"), (c - 1) * FC + max(j - 1, 0))
                    act.activation(sil[j % 2][:], bank(BANK_SH[2 * j]), ACT.Silu).then_inc(S("sil"), 1)
                    if j in (1, 3):
                        late_row(c, j // 2)
                late_row(c, 2)
                late_row(c, 3)

            def x_high(c):
                act.wait_ge(S("xT_in"), 16 * (c + 1))
                wait_past(act, S("z_mm"), c * HC)
                act.copy(xTs[0][:], xT[:]).then_inc(S("xT_high"), 1)

            def body(c, after, more):
                for j in range(HC + 1):
                    if j < HC:
                        act.wait_ge(S("z_mm"), c * HC + j + 1)
                        wait_past(act, S("so_mm"), 2 * (c - 1))
                        act.activation(hidden[:, j, :], bank(BANK_Z[j]), ACT.Silu, bias=b1c[:, j:j + 1])\
                           .then_inc(S("h2"), 1)
                    if j > 0:
                        act.wait_ge(S("h2"), c * HC + j)
                        wait_past(act, S("om_mm"), 2 * c)
                        act.copy(h2[0][:, j - 1, :], hidden[:, j - 1, :]).then_inc(S("h2_high"), 1)
                if after:
                    late(c)
                if more:
                    x_high(c + 1)
                for g, (dst, banks) in enumerate(((g1, (5, 6)), (g2, (7, 0)))):
                    for m in range(DC):
                        act.wait_ge(S("lin_mm"), c * 4 + 2 * g + m + 1)
                        wait_past(act, S("mT_mm"), 2 * c)
                        if g == 1:
                            wait_past(act, S("base_out"), (c - 1) * 16)
                        act.activation(block_of(dst, m), by_tile(bank(banks[m])), ACT.Sigmoid)\
                           .then_inc(S("gated"), 1)
                if after:
                    late_shared(c)

            x_high(0)
            act.wait_ge(S("s1_in"), 16)
            act.copy(flat(s1T[0][:]), s1_raw).then_inc(S("s1_high"), 1)
            body(0, False, True)
            body(1, True, True)
            with act.Fori(2, CHUNKS - 1) as c:
                body(c, True, True)
            body(CHUNKS - 1, True, False)
            late(CHUNKS)
            late_shared(CHUNKS)

        @block.vector
        def _(dve):
            dve.wait_ge(S("route_const"), 1)

            def low(out, raw, high):
                return dve.tensor_tensor(out, raw, high.bitcast(F32), ALU.subtract)

            def x_low(c):
                dve.wait_ge(S("xT_high"), c + 1)
                low(xTs[1][:], xT[:], xTs[0][:]).then_inc(S("xT_low"), 1)

            def h2_low(c):
                for g in range(4):
                    dve.wait_ge(S("h2_high"), c * HC + 2 * g + 2)
                    part = slice(2 * g, 2 * g + 2)
                    low(flat(h2[1][:, part, :]), flat(hidden[:, part, :]), flat(h2[0][:, part, :]))\
                        .then_inc(S("h2_low"), 1)

            def route(c):
                lp = bank(2, TPC * E).rearrange("p (t e) -> p t e", t=TPC)
                dve.wait_ge(S("gate_mm"), c)
                dve.tensor_reduce(lmax[:], lp, AX, ALU.max).then_inc(S("lmax"), 1)
                dve.wait_ge(S("lmax"), c)
                dve.tensor_tensor(lg[:], lp, wide(lmax[:], E), ALU.subtract).then_inc(S("lg"), 1)
                dve.wait_ge(S("hT_high"), c)
                low(flat(hTs[1][:]), flat(hT[:]), flat(hTs[0][:])).then_inc(S("hT_low"), 1)
                dve.wait_ge(S("gate_exp"), c)
                dve.tensor_reduce(gsum[:], gate[:], AX, ALU.add).then_inc(S("gsum"), 1)
                dve.wait_ge(S("gsum"), c)
                dve.reciprocal(grec[:], gsum[:]).then_inc(S("grec"), 1)
                dve.wait_ge(S("grec"), c)
                dve.tensor_tensor(gate[:], gate[:], wide(grec[:], E), ALU.mult).then_inc(S("gate"), 1)
                wait_apart(dve, S("gate"), c, S("passed_dve"))
                for t in range(TPC):
                    ins = dve.max(top[:, t, :], gate[:, t, :])
                ins.then_inc(S("top"), 1)
                wait_apart(dve, S("top"), c, S("passed_dve"))
                for t in range(TPC):
                    dve.match_replace(out=rest[:, t, :], in_to_replace=top[:, t, :], in_values=gate[:, t, :],
                                      imm_value=-1.0)
                dve.tensor_reduce(wsum[:], top[:], AX, ALU.add).then_inc(S("rest"), 1)
                dve.wait_ge(S("rest"), c)
                dve.tensor_scalar(wsum[:], wsum[:], F32_EPS, None, ALU.max)
                dve.tensor_scalar(chosen_b[:], rest[:], 0.0, None, ALU.is_lt)
                dve.tensor_scalar(chosen[:], rest[:], 0.0, None, ALU.is_lt).then_inc(S("chosen"), 1)
                dve.wait_ge(S("chosen"), c)
                dve.reciprocal(wrec[:], wsum[:]).then_inc(S("wrec"), 1)
                dve.wait_ge(S("wrec"), c)
                dve.tensor_tensor(gate[:], gate[:], wide(wrec[:], E), ALU.mult).then_inc(S("weight"), 1)

            def slots_of(c):
                dve.wait_ge(S("rank_mm"), c)
                for t in range(TPC):
                    wait_past(dve, S("carry"), (c - 1) * TPC + t)
                    dve.tensor_tensor(rank[:, t, :], psum[1][:, D + t * E:D + (t + 1) * E], carry[:], ALU.add)\
                       .then_inc(S("rank"), 1)
                    dve.wait_ge(S("rank"), (c - 1) * TPC + t + 1)
                    dve.tensor_tensor(carry[:], carry[:], psum[1][:, t * E:(t + 1) * E], ALU.add)\
                       .then_inc(S("carry"), 1)
                dve.scalar_tensor_tensor(out=fits[:], in0=rank[:], scalar=float(CAP), in1=chosen[:],
                                         op0=ALU.is_lt, op1=ALU.mult)
                dve.tensor_tensor(slot[:], rank[:], slot_base[:].unsqueeze(1).to_broadcast([P, TPC, E]), ALU.add)\
                   .then_inc(S("fits"), 1)
                dve.wait_ge(S("fits"), c)
                dve.tensor_tensor(slot[:], slot[:], fits[:], ALU.mult).then_inc(S("slot"), 1)
                wait_apart(dve, S("slot"), c, S("passed_dve"))
                for t in range(TPC):
                    ins = dve.max(slot8[:, t, :], slot[:, t, :])
                ins.then_inc(S("slot8"), 1)
                dve.wait_ge(S("slot8"), c)
                dve.tensor_scalar(off[:], slot8[:], 1.0, float(OFF_LIST), ALU.is_lt, ALU.mult).then_inc(S("off"), 1)
                dve.wait_ge(S("off"), c)
                wait_past(dve, S("row_out0"), (c - 1) * 2 * TOPK * 16)
                wait_past(dve, S("row_out1"), (c - 1) * 2 * TOPK * 16)
                dve.scalar_tensor_tensor(out=index[:], in0=slot8[:], scalar=-1.0, in1=off[:], op0=ALU.add,
                                         op1=ALU.add).then_inc(S("index"), 1)

            def weights_of(c, t):
                if t == 0:
                    dve.wait_ge(S("weight"), c)
                    wait_past(dve, S("row_part"), (c - 1) * TPC)
                wait_past(dve, S("w8"), (c - 1) * TPC + t)
                for k in range(TOPK):
                    ins = dve.scalar_tensor_tensor(out=picked[:, k, :], in0=slot[:, t, :],
                                                   scalar=slot8[:, t, k:k + 1], in1=gate[:, t, :],
                                                   op0=ALU.is_equal, op1=ALU.mult, accum_out=w8[:, t, k:k + 1])
                ins.then_inc(S("w8"), 1)

            def merge(c):
                dve.wait_ge(S("gated"), 4 * c + 2)
                dve.tensor_tensor(g1[:], g1[:], swaT[:], ALU.mult)
                dve.wait_ge(S("gated"), 4 * c + 4)
                dve.tensor_tensor(g2[:], g2[:], om[:], ALU.mult).then_inc(S("parts"), 1)
                dve.wait_ge(S("parts"), c + 1)
                dve.tensor_tensor(g1[:], g1[:], g2[:], ALU.add).then_inc(S("merged"), 1)

            def shared(c):
                for j in range(FC):
                    if j < TPC:
                        weights_of(c, j)
                    dve.wait_ge(S("sil"), (c - 1) * FC + j + 1)
                    dve.wait_ge(S("sh_mm"), (c - 1) * 2 * FC + 2 * j + 2)
                    wait_past(dve, S("so_mm"), (c - 1) * 2)
                    dve.tensor_tensor(gT[:, j, :], bank(BANK_SH[2 * j + 1]), sil[j % 2][:], ALU.mult)\
                       .then_inc(S("gT"), 1)

            def base_rows(c, merges):
                dve.wait_ge(S("merged"), merges)
                for g in range(2):
                    dve.wait_ge(S("so_mm"), 2 * c - 1 + g)
                    wait_past(dve, S("base_out"), (c - 1) * 16)
                    dve.tensor_tensor(base[:, 2 * g:2 * g + 2, :], bank(6 + g).rearrange("p (t d) -> p t d", t=2),
                                      mod[:, 5, :].unsqueeze(1).to_broadcast([P, 2, D]), ALU.mult)\
                       .then_inc(S("base_raw"), 1)
                    dve.wait_ge(S("base_raw"), 2 * c - 1 + g)
                    dve.tensor_tensor(base[:, 2 * g:2 * g + 2, :], base[:, 2 * g:2 * g + 2, :],
                                      x2[:, 2 * g:2 * g + 2, :], ALU.add).then_inc(S("base"), 1)

            def residual(c):
                dve.wait_ge(S("x_in"), 16 * (c + 1))
                for g in range(2):
                    dve.wait_ge(S("mT_mm"), 2 * c + g + 1)
                    if g == 0:
                        wait_past(dve, S("base"), 2 * c)
                    dve.tensor_tensor(x2[:, 2 * g:2 * g + 2, :], bank(2 + g).rearrange("p (t d) -> p t d", t=2),
                                      mod[:, 2, :].unsqueeze(1).to_broadcast([P, 2, D]), ALU.mult)\
                       .then_inc(S("x2_raw"), 1)
                dve.wait_ge(S("x2_raw"), 2 * c + 2)
                dve.tensor_tensor(x2[:], x2[:], x[:], ALU.add).then_inc(S("x2"), 1)
                dve.wait_ge(S("x2"), c + 1)
                for t in range(TPC):
                    ins = dve.bn_stats(stats[:, t, :], x2[:, t, :])
                ins.then_inc(S("stats"), 1)
                wait_apart(dve, S("stats"), c + 1, S("passed_dve"))
                for t in range(TPC):
                    ins = dve.bn_aggr(moments[:, t, :], stats[:, t, :])
                ins.then_inc(S("moments"), 1)
                dve.wait_ge(S("moments"), c + 1)
                inverse_sqrt(dve, S("rstd"), c, rstd[:], moments[:, :, 1], half[:])
                wait_past(dve, S("hT_mm"), 2 * c)
                wait_past(dve, S("row_part"), c * TPC)
                for t in range(TPC):
                    ins = dve.tensor_scalar(hm[:, t, :], x2[:, t, :], moments[:, t, 0:1], rstd[:, t:t + 1],
                                            ALU.subtract, ALU.mult)
                ins.then_inc(S("hn"), 1)
                dve.wait_ge(S("hn"), c + 1)
                dve.tensor_tensor(hm[:], hm[:], rows_of(mod[:, 4, :]), ALU.mult).then_inc(S("hscaled"), 1)
                dve.wait_ge(S("hscaled"), c + 1)
                dve.tensor_tensor(hm[:], hm[:], rows_of(mod[:, 3, :]), ALU.add).then_inc(S("hm"), 1)

            def body(c, after, more):
                h2_low(c)
                if after:
                    route(c)
                for m in range(DC):
                    dve.wait_ge(S("om_mm"), 2 * c + m + 1)
                    wait_past(dve, S("parts"), c)
                    dve.tensor_scalar(block_of(om, m), by_tile(bank(3 + m)), b2c[:, m:m + 1], None, ALU.add)\
                       .then_inc(S("om"), 1)
                if after:
                    slots_of(c)
                    shared(c)
                merge(c)
                if more:
                    x_low(c + 1)
                if after:
                    base_rows(c, c + 1)
                residual(c)

            x_low(0)
            dve.wait_ge(S("s1_high"), 1)
            low(flat(s1T[1][:]), s1_raw, flat(s1T[0][:])).then_inc(S("s1_low"), 1)
            body(0, False, True)
            body(1, True, True)
            with dve.Fori(2, CHUNKS - 1) as c:
                body(c, True, True)
            body(CHUNKS - 1, True, False)
            route(CHUNKS)
            slots_of(CHUNKS)
            shared(CHUNKS)
            base_rows(CHUNKS, CHUNKS)

        @block.tensor
        def _(pe):
            def turn(out, src):
                return nc.tensor.transpose(out, src, ident[:])

            def gates(c):
                pe.wait_ge(S("hm"), c)
                for g in range(2):
                    for b in range(4):
                        k, t = b // 2, 2 * g + b % 2
                        ins = turn(psum[g][:, b * P:(b + 1) * P], hm[:, t, k * P:(k + 1) * P])
                    ins.then_inc(S("hT_mm"), 1)
                pe.wait_ge(S("hT"), 2 * c)
                for t in range(TPC):
                    for k in range(DC):
                        ins = mm(psum[2][:, t * E:(t + 1) * E], hT[:, k, t * P:(t + 1) * P], wgT[:, k, :],
                                 k == 0, k == DC - 1)
                ins.then_inc(S("gate_mm"), 1)

            def ranks(c):
                pe.wait_ge(S("chosen"), c)
                flat = chosen_b[:].rearrange("p t e -> p (t e)")
                mm(psum[1][:, 0:TPC * E], every[:], flat, True, True)
                mm(psum[1][:, D:D + TPC * E], before[:], flat, True, True).then_inc(S("rank_mm"), 1)

            def shared(c, tail):
                for i in range(2 * FC):
                    j, part = i // 2, i % 2
                    if i == 0:
                        pe.wait_ge(S("lg"), c)
                        pe.wait_ge(S("hT_low"), c)
                    if not tail:
                        if i == 1:
                            pe.wait_ge(S("om"), 2 * c + 2)
                        if i in (3, 4, 5, 6):
                            pe.wait_ge(S("gated"), 4 * c + i - 2)
                    if i == 7:
                        pe.wait_ge(S("carry"), c * TPC)
                    if i >= 8:
                        pe.wait_ge(S("gT"), (c - 1) * FC + (i - 8) // 2 + 1)
                    col = (FC + j if part == 0 else j) * P
                    for k in range(DC):
                        ins = mm_split(nc, bank(BANK_SH[i]), cut(s1T, slice(None), k, slice(col, col + P)),
                                       cut(hTs, slice(None), k, slice(None)), k == 0, k == DC - 1)
                    ins.then_inc(S("sh_mm"), 1)
                for g in range(2):
                    for t in range(2):
                        for k in range(FC):
                            if g == 0 and t == 0:
                                pe.wait_ge(S("gT"), (c - 1) * FC + max(k, 2) + 1)
                            ins = mm(psum[6 + g][:, t * D:(t + 1) * D], gT[:, k, (2 * g + t) * P:(2 * g + t + 1) * P],
                                     s2T[:, k, :], k == 0, k == FC - 1)
                    ins.then_inc(S("so_mm"), 1)

            def body(c, after):
                pe.wait_ge(S("xT_low"), c + 1)
                for j in range(HC):
                    if j in (2, 3):
                        wait_past(pe, S("x2_raw"), 2 * c - 3 + j)
                    if j == 6 and after:
                        wait_past(pe, S("base_raw"), 2 * c - 2)
                    for k in range(DC):
                        ins = mm_split(nc, bank(BANK_Z[j]), cut(w1T, slice(None), k, slice(j * P, (j + 1) * P)),
                                       [block_of(a, k) for a in xTs], k == 0, k == DC - 1)
                    ins.then_inc(S("z_mm"), 1)
                pe.wait_ge(S("h2"), c * HC + 3)
                if after:
                    gates(c)
                pe.wait_ge(S("h2"), c * HC + 5)
                for m in range(DC):
                    for k in range(HC):
                        if m == 0 and k % 2 == 0:
                            pe.wait_ge(S("h2_low"), c * 4 + k // 2 + 1)
                        ins = mm_split(nc, bank(3 + m), cut(w2T, slice(None), k, slice(m * P, (m + 1) * P)),
                                       cut(h2, slice(None), k, slice(None)), k == 0, k == HC - 1)
                    ins.then_inc(S("om_mm"), 1)
                pe.wait_ge(S("swaT_in"), 16 * (c + 1))
                for m in range(DC):
                    for k in range(DC):
                        ins = mm(bank(5 + m), linT[:, 0, k, m * P:(m + 1) * P], block_of(swaT, k),
                                 k == 0, k == DC - 1)
                    ins.then_inc(S("lin_mm"), 1)
                pe.wait_ge(S("om"), 2 * c + 2)
                for m in range(DC):
                    for k in range(DC):
                        ins = mm(bank((7, 0)[m]), linT[:, 1, k, m * P:(m + 1) * P], block_of(om, k), k == 0, k == DC - 1)
                    ins.then_inc(S("lin_mm"), 1)
                if after:
                    ranks(c)
                    shared(c, False)
                pe.wait_ge(S("merged"), c + 1)
                for g in range(2):
                    for b in range(4):
                        t, k = 2 * g + b // 2, b % 2
                        ins = turn(psum[2 + g][:, b * P:(b + 1) * P], g1[:, t, k * P:(k + 1) * P])
                    ins.then_inc(S("mT_mm"), 1)

            pe.wait_ge(S("lin_in"), 16)
            pe.wait_ge(S("wg_in"), 16)
            pe.wait_ge(S("s1_low"), 1)
            pe.wait_ge(S("s2_in"), 16)
            body(0, False)
            body(1, True)
            with pe.Fori(2, CHUNKS) as c:
                body(c, True)
            gates(CHUNKS)
            ranks(CHUNKS)
            shared(CHUNKS, True)


def expert_stage(nc, T, buf, psum, S):
    with ExitStack() as ctx:
        def sb(name, shape, dt=F32):
            return ctx.enter_context(nc.sbuf_tensor("c_" + name, shape, dt))

        mod, ident = buf["mod"], buf["ident"]
        w1 = [sb(f"w1_{p}", [P, DC, 2 * FFN]) for p in range(2)]
        w2 = [sb(f"w2_{p}", [P, FC, D]) for p in range(2)]
        xa = [sb(f"xa{q}", [P, ROW]) for q in range(4)]
        xb = [sb(f"xb{q}", [CAP_B, ROW]) for q in range(4)]
        xT = [sb(f"xT{p}", [P, DC, CAP]) for p in range(2)]
        sil = sb("sil", [P, FC, CAP])
        gT = [sb(f"gT{p}", [P, FC, CAP]) for p in range(2)]
        yT = sb("yT", [P, DC, CAP])
        ya = sb("ya", [P, D])
        yb = sb("yb", [CAP_B, D])
        H = FC // 2
        Y_BANK = (5, 7)

        def mm(out, lhsT, rhs, first, last):
            return nc.tensor.matmul(out, lhsT, rhs, start=first, stop=last, skip_group_check=True)

        def experts(eng, step):
            for n in range(4):
                step(n, n, 1, n // 2 + 1)
            with eng.Fori(1, E // 4) as i:
                for q in range(4):
                    step(i * 4 + q, q, i + 1, i * 2 + q // 2 + 1)

        block = ctx.enter_context(nc.Block())

        @block.sync
        def _(sp):
            def load_w2(n, p):
                wait_past(sp, S("y_mm"), n - 1)
                sp.dma_start(w2[p][:], T["e2T"][bass.ds(n, 1)].rearrange("a p k f -> p (a k) f"))\
                  .then_inc(S(f"w2_in{p}"), 16)

            def step(n, q, rows_in, weights_in):
                p = q % 2
                wait_past(sp, S("added"), (n - 3) * 32)
                sp.dma_start(xa[q][:], T["slots"][bass.ds(n * CAP, P), :]).then_inc(S(f"x_in{q}"), 16)
                sp.dma_start(xb[q][:], T["slots"][bass.ds(n * CAP + P, CAP_B), :]).then_inc(S(f"x_in{q}"), 16)
                wait_past(sp, S("h_mm"), (n - 1) * 4)
                sp.dma_start(w1[p][:], T["e1T"][bass.ds(n, 1)].rearrange("a p k f -> p (a k) f"))\
                  .then_inc(S(f"w1_in{p}"), 16)
                if not isinstance(n, int) or n >= 1:
                    load_w2(n - 1, 1 - p)

            experts(sp, step)
            load_w2(E - 1, 1)

        @block.scalar
        def _(act):
            def y_cols(n):
                for m in range(DC):
                    act.wait_ge(S("y_mm"), n + 1)
                    wait_past(act, S("yR_mm"), n)
                    ins = act.copy(yT[:, m, :], psum[Y_BANK[m]][:, 0:CAP])
                ins.then_inc(S("yT"), 1)

            def step(n, q, rows_in, weights_in):
                p = q % 2
                act.wait_ge(S("xT_mm"), n + 1)
                wait_past(act, S("h_mm"), (n - 1) * 4)
                act.copy(flat(xT[p][:]), psum[0][:, 0:DC * CAP]).then_inc(S("xT"), 1)
                if not isinstance(n, int) or n >= 1:
                    y_cols(n - 1)
                for g in range(2):
                    act.wait_ge(S("h_mm"), 4 * n + 2 * g + 1)
                    wait_past(act, S("gT"), 2 * n - 1 + g)
                    act.activation(flat(sil[:, g * H:(g + 1) * H, :]), psum[1 + 2 * g][:, 0:H * CAP], ACT.Silu)\
                       .then_inc(S("sil"), 1)

            experts(act, step)
            y_cols(E - 1)

        @block.vector
        def _(dve):
            def y_rows(n, q):
                dve.wait_ge(S("yR_mm"), n + 1)
                wait_past(dve, S("added"), n * 32)
                dve.scalar_tensor_tensor(out=ya[:], in0=psum[6][:, 0:D], scalar=xa[q][:, D:D + 1], in1=mod[:, 5, :],
                                         op0=ALU.mult, op1=ALU.mult)
                dve.scalar_tensor_tensor(out=yb[:], in0=psum[6][0:CAP_B, D:2 * D], scalar=xb[q][:, D:D + 1],
                                         in1=mod[0:CAP_B, 5, :], op0=ALU.mult, op1=ALU.mult).then_inc(S("y"), 1)

            def step(n, q, rows_in, weights_in):
                p = q % 2
                for g in range(2):
                    dve.wait_ge(S("sil"), 2 * n + g + 1)
                    dve.wait_ge(S("h_mm"), 4 * n + 2 * g + 2)
                    wait_past(dve, S("y_mm"), n - 1)
                    dve.tensor_tensor(flat(gT[p][:, g * H:(g + 1) * H, :]), psum[2 + 2 * g][:, 0:H * CAP],
                                      flat(sil[:, g * H:(g + 1) * H, :]), ALU.mult).then_inc(S("gT"), 1)
                if not isinstance(n, int) or n >= 1:
                    y_rows(n - 1, (q - 1) % 4)

            experts(dve, step)
            y_rows(E - 1, 3)

        @block.gpsimd
        def _(pool):
            last_row = pool.to_reg(TOKENS + CAP - 1)

            def step(n, q, rows_in, weights_in):
                wait_past(pool, S("added"), n * 32)
                wait_apart(pool, S("y"), n + 1, S("passed_pool"))
                for y, x in ((ya, xa[q]), (yb, xb[q])):
                    pool.indirect_dma_start(
                        out=T["out"], out_offset=bass.IndirectOffsetOnAxis(ap=x[:, D + 1:D + 2].bitcast(U32), axis=0),
                        in_=y[:], in_offset=None, bounds_check=last_row, oob_is_err=True,
                        compute_op=ALU.add).then_inc(S("added"), 16)

            experts(pool, step)
            pool.wait_ge(S("added"), E * 32)

        @block.tensor
        def _(pe):
            def turn_x(n, q, rows_in):
                pe.wait_ge(S(f"x_in{q}"), rows_in * 32)
                wait_past(pe, S("xT"), n)
                for k in range(DC):
                    nc.tensor.transpose(psum[0][:, k * CAP:k * CAP + P], xa[q][:, k * P:(k + 1) * P], ident[:])
                    ins = nc.tensor.transpose(psum[0][:, k * CAP + P:(k + 1) * CAP], xb[q][:, k * P:(k + 1) * P],
                                              ident[0:CAP_B, 0:CAP_B])
                ins.then_inc(S("xT_mm"), 1)

            def up(n, p, weights_in):
                pe.wait_ge(S(f"w1_in{p}"), weights_in * 16)
                pe.wait_ge(S("xT"), n + 1)
                for g in range(2):
                    for part in range(2):
                        wait_past(pe, S("sil" if part == 0 else "gT"), 2 * n - 1 + g)
                        for j in range(H):
                            col = ((FC if part == 0 else 0) + g * H + j) * P
                            for k in range(DC):
                                ins = mm(psum[1 + 2 * g + part][:, j * CAP:(j + 1) * CAP], w1[p][:, k, col:col + P],
                                         xT[p][:, k, :], k == 0, k == DC - 1)
                        ins.then_inc(S("h_mm"), 1)

            def down(n, p, weights_in):
                pe.wait_ge(S(f"w2_in{p}"), weights_in * 16)
                wait_past(pe, S("yT"), n)
                for g in range(2):
                    pe.wait_ge(S("gT"), 2 * n + g + 1)
                    for m in range(DC):
                        for k in range(g * H, (g + 1) * H):
                            ins = mm(psum[Y_BANK[m]][:, 0:CAP], w2[p][:, k, m * P:(m + 1) * P], gT[p][:, k, :],
                                     k == 0, k == FC - 1)
                ins.then_inc(S("y_mm"), 1)

            def turn_y(n):
                pe.wait_ge(S("yT"), n + 1)
                wait_past(pe, S("y"), n)
                for k in range(DC):
                    nc.tensor.transpose(psum[6][:, k * P:(k + 1) * P], yT[:, k, 0:P], ident[:])
                    ins = nc.tensor.transpose(psum[6][0:CAP_B, D + k * P:D + (k + 1) * P], yT[:, k, P:CAP], ident[:])
                ins.then_inc(S("yR_mm"), 1)

            def step(n, q, rows_in, weights_in):
                p = q % 2
                late = not isinstance(n, int) or n >= 1
                turn_x(n, q, rows_in)
                if late:
                    down(n - 1, 1 - p, weights_in - (1 - p))
                up(n, p, weights_in)
                if late:
                    turn_y(n - 1)

            experts(pe, step)
            down(E - 1, 1, E // 2)
            turn_y(E - 1)


def build(nc, T):
    def run(stage, prefix, buf):
        sems = Sems(nc, prefix)
        stage(nc, T, buf, psum, sems)
        sems.clear()

    with ExitStack() as ctx:
        psum = [ctx.enter_context(nc.psum_tensor(f"bank{b}", [P, CH], F32)) for b in range(8)]
        with ExitStack() as inner:
            buf = shared_buffers(nc, ctx, inner)
            run(memory_stage, "a_", buf)
            run(token_stage, "b_", buf)
        run(expert_stage, "c_", buf)


def kernel(**inputs):
    import numpy as np
    import concourse.bacc as bacc
    from concourse.bass_utils import run_bass_kernel_spmd

    a = {k: np.asarray(v) for k, v in inputs.items()}

    def split(w):
        k, n = w.shape
        return np.ascontiguousarray(w.reshape(k // P, P, n).transpose(1, 0, 2))

    w = {k[len("L0_"):]: v for k, v in a.items()}
    e1, e2 = w["ffn_expert_w1"], w["ffn_expert_w2"]
    arrays = {
        "x": w["attn_x"].reshape(TOKENS, D),
        "mem": w["attn_mem"],
        "wqkT": np.ascontiguousarray(np.stack([split(w["attn_wq"].T), split(w["attn_wk"].T)], axis=1)),
        "wvT": split(w["attn_wv"].T),
        "woT": split(w["attn_wo"].T),
        "w1T": split(w["attn_w1"].T),
        "w2T": split(w["attn_w2"].T),
        "w2n": split(w["attn_w2"]),
        "b1row": np.ascontiguousarray(np.broadcast_to(w["attn_b1"][None, :], (P, HID))),
        "b2row": np.ascontiguousarray(np.broadcast_to(w["attn_b2"][None, :], (P, D))),
        "b1c": np.ascontiguousarray(w["attn_b1"].reshape(HC, P).T),
        "b2c": np.ascontiguousarray(w["attn_b2"].reshape(DC, P).T),
        "alpha": np.ascontiguousarray(np.broadcast_to(w["attn_alpha"].reshape(1, 1), (P, 1))),
        "theta": np.ascontiguousarray(np.broadcast_to(w["attn_theta"].reshape(1, 1), (P, 1))),
        "linT": np.ascontiguousarray(np.stack([split(w["attn_lin1"].T), split(w["attn_lin2"].T)], axis=1)),
        "wgT": split(w["ffn_wg"].T),
        "s1T": split(w["ffn_shared_w1"].T),
        "s2T": split(w["ffn_shared_w2"].T),
        "e1T": np.ascontiguousarray(e1.reshape(E, 2 * FFN, DC, P).transpose(0, 3, 2, 1)),
        "e2T": np.ascontiguousarray(e2.reshape(E, D, FC, P).transpose(0, 3, 2, 1)),
        "c": np.ascontiguousarray(w["c"].reshape(DC, P).T),
        "wmod": split(w["wmod"]),
    }
    nc = bacc.Bacc("TRN2", target_bir_lowering=False, num_devices=1)
    T = {k: nc.dram_tensor("in_" + k, v.shape, mybir.dt.from_np(v.dtype), kind="ExternalInput").ap()
         for k, v in arrays.items()}
    T["out"] = nc.dram_tensor("out_rows", (TOKENS + CAP, D), F32, kind="ExternalOutput").ap()
    T["xT"] = nc.dram_tensor("xT_tiles", (TOKENS, D), F32, kind="Internal").ap()
    T["swaT"] = nc.dram_tensor("swaT_tiles", (TOKENS, D), F32, kind="Internal").ap()
    T["slots"] = nc.dram_tensor("slots", (E * CAP, ROW), F32, kind="Internal").ap()
    build(nc, T)
    r = run_bass_kernel_spmd(nc, [{"in_" + k: v for k, v in arrays.items()}], core_ids=[0])
    return r.results[0]["out_rows"][:TOKENS].reshape(1, TOKENS, D)
```

```python
from contextlib import ExitStack

import concourse.bass as bass
from concourse import mybir

F32 = mybir.dt.float32
F32R = mybir.dt.float32r
BF16 = mybir.dt.bfloat16
I32 = mybir.dt.int32
U32 = mybir.dt.uint32
ALU = mybir.AluOpType
ACT = mybir.ActivationFunctionType
AX = mybir.AxisListType.X

P = 128
D = 256
DC = D // P
HID = 1024
HC = HID // P
HEADS = 4
DH = D // HEADS
MEM = 64
TOKENS = 4096
TILES = TOKENS // P
CH = 512
TPC = CH // P
CHUNKS = TOKENS // CH
E = 64
TOPK = 8
FFN = 768
FC = FFN // P
CAP = 160
CAP_B = CAP - P
ROW = D + 2
NEG = -1e30
EPS = 1e-5
F32_EPS = 1.1920929e-07
OFF_LIST = 20000
HEAD_AT = [0, 2, 1, 3]


def wait_past(engine, sem, value):
    if isinstance(value, int) and value <= 0:
        return
    engine.wait_ge(sem, value)


def wait_apart(engine, sem, value, passed):
    engine.wait_ge(sem, value)
    engine.sem_inc(passed, 1)


def flat(a):
    names = "abcd"[:len(a.shape) - 1]
    return a.rearrange(f"p {' '.join(names)} -> p ({' '.join(names)})")


def mm_split(nc, out, w, x, first, last):
    pairs = ((w[0], x[0]), (w[0], x[1]), (w[1], x[0]))
    for i, (a, b) in enumerate(pairs):
        ins = nc.tensor.matmul(out, a, b, start=first and i == 0, stop=last and i == 2, skip_group_check=True)
    return ins


class Sems:

    def __init__(self, nc, prefix):
        self.nc, self.prefix, self.made = nc, prefix, {}

    def __call__(self, name):
        if name not in self.made:
            self.made[name] = self.nc.alloc_semaphore(self.prefix + name)
        return self.made[name]

    def clear(self):
        self.nc.clear_and_free_semaphores(list(self.made.values()))
        self.nc.all_engine_barrier()


RSQRT_STEPS = 3
RSQRT_OPS = 3 + 3 * RSQRT_STEPS


def inverse_sqrt(dve, done, calls, y, var, t):
    ops = [
        lambda: dve.tensor_scalar(var, var, EPS, None, ALU.add),
        lambda: dve.tensor_scalar(t.bitcast(I32), var.bitcast(I32), 1, None, ALU.logical_shift_right),
        lambda: dve.tensor_scalar(y.bitcast(I32), t.bitcast(I32), -1.0, float(0x5F3759DF), ALU.mult, ALU.add),
    ] + [
        lambda: dve.tensor_tensor(t, y, y, ALU.mult),
        lambda: dve.scalar_tensor_tensor(out=t, in0=t, scalar=-0.5, in1=var, op0=ALU.mult, op1=ALU.mult),
        lambda: dve.scalar_tensor_tensor(out=y, in0=t, scalar=1.5, in1=y, op0=ALU.add, op1=ALU.mult),
    ] * RSQRT_STEPS
    for k, op in enumerate(ops):
        op().then_inc(done, 1)
        dve.wait_ge(done, calls * RSQRT_OPS + k + 1)


def shared_buffers(nc, ctx, inner):
    def sb(where, name, shape, dt=F32):
        return where.enter_context(nc.sbuf_tensor(name, shape, dt))
    return {
        "mod": sb(ctx, "mod", [P, 6, D]),
        "ident": sb(ctx, "ident", [P, P]),
        "early": sb(ctx, "early", [P, HC * CH]),
        "w1T": [sb(inner, f"w1T_{part}", [P, DC, HID], F32R) for part in ("high", "low")],
        "w2T": [sb(inner, f"w2T_{part}", [P, HC, D], F32R) for part in ("high", "low")],
        "b1c": sb(inner, "b1c", [P, HC]),
        "b2c": sb(inner, "b2c", [P, DC]),
    }


def cut(pair, *at):
    return tuple(t[at] for t in pair)


def memory_stage(nc, T, buf, psum, S):
    with ExitStack() as ctx:
        def sb(name, shape, dt=F32):
            return ctx.enter_context(nc.sbuf_tensor("a_" + name, shape, dt))

        def split(name, shape):
            return sb(name + "_high", shape, F32R), sb(name + "_low", shape, F32R)

        w1T, w2T, mod, ident, b1c, b2c = (buf[k] for k in ("w1T", "w2T", "mod", "ident", "b1c", "b2c"))
        wqk = sb("wqk", [P, 2, DC, D])
        wv = split("wv", [P, DC, D])
        woT = sb("woT", [P, DC, D])
        w2n = split("w2n", [P, DC, HID])
        b1row = sb("b1row", [P, HID])
        b2row = sb("b2row", [P, D])
        alpha = sb("alpha", [P, 1])
        theta = sb("theta", [P, 1])
        keep = sb("keep", [P, 1])
        step = sb("step", [P, 1])
        cond = sb("cond", [P, DC])
        cond_s = sb("cond_s", [P, DC])
        cond_w = sb("cond_w", [P, DC, P])
        ones = sb("ones", [P, P])
        masks = sb("masks", [P, 4, 2 * P])
        fill = sb("fill", [P, 2, ROW])
        slot_id = sb("slot_id", [P, 2], I32)
        dW1T = sb("dW1T", [P, DC, HID])
        dW2 = sb("dW2", [P, DC, HID])
        dz_sum = sb("dz_sum", [P, HID])
        e_sum = sb("e_sum", [P, D])
        db = sb("db", [P, HC + DC])
        again = [buf["early"][:, p * HID:(p + 1) * HID] for p in range(2)]
        stats = sb("stats", [P, TILES, 6])
        moments = sb("moments", [P, TILES, 2])
        rstd = sb("rstd", [P, TILES])
        half = sb("half", [P, TILES])
        x_in = [sb(f"x_in{p}", [P, D]) for p in range(2)]
        xn = sb("xn", [P, D])
        xm = sb("xm", [P, D])
        xms = [split(f"xm{p}", [P, D]) for p in range(2)]
        xT = sb("xT", [P, DC, P])
        xTs = split("xT", [P, DC, P])
        qT = split("qT", [P, DC, P])
        kT = split("kT", [P, DC, 2, P])
        v = sb("v", [P, 2, D])
        logit = sb("logit", [P, HEADS, 2 * P])
        peak = sb("peak", [P, HEADS])
        npeak = sb("npeak", [P, HEADS])
        psums = sb("psums", [P, HEADS])
        prec = sb("prec", [P, HEADS])
        table = sb("table", [P, 1])
        prob = sb("prob", [P, HEADS, 2 * P])
        probT = sb("probT", [P, HEADS, 2, P])
        oT = sb("oT", [P, DC, P])
        swa = sb("swa", [P, D])
        swaT = sb("swaT", [P, DC, P])
        zb, sg = (buf["early"][:, p * HID:(p + 1) * HID] for p in (2, 3))
        h = sb("h", [P, HID])
        hsp = [split(f"h{p}", [P, HID]) for p in range(2)]
        gp = sb("gp", [P, HID])
        hT = split("hT", [P, HC, P])
        pred = sb("pred", [P, D])
        e = sb("e", [P, D])
        es = split("e", [P, D])
        eT = split("eT", [P, DC, P])
        dz = sb("dz", [P, HID])
        dzs = split("dz", [P, HID])
        wmod = [t[:].rearrange("p a b -> p (a b)").rearrange("p (k n) -> p k n", k=DC) for t in (logit, prob)]
        wmod.append(probT[:].rearrange("p a b c -> p (a b c)").rearrange("p (k n) -> p k n", k=DC))
        w2n_raw = sb("w2n_raw", [P, DC, HID])
        wv_raw = h[:, 0:DC * D].rearrange("p (k n) -> p k n", k=DC)
        clamp = h[:, 2 * D:4 * D].rearrange("p (k n) -> p k n", k=2)
        x_pre = [a[:].rearrange("p (t d) -> p t d", t=TPC) for a in (again[0], again[1], dz, gp, dz_sum)]
        PRE = len(x_pre)

        def bank(b, n=CH):
            return psum[b][:, 0:n]

        def mm(out, lhsT, rhs, first, last):
            return nc.tensor.matmul(out, lhsT, rhs, start=first, stop=last, skip_group_check=True)

        LAST = TILES
        DW_BANK = (1, 2, 3, 4, 5, 6, 7, 0)
        slots = T["slots"].rearrange("(e r) d -> r e d", e=E)
        CLEARED = E // (TILES // 2)

        def known(n, least):
            return not isinstance(n, int) or n >= least

        x_rows = T["x"]
        x_chunks = T["x"].rearrange("(c t p) d -> c p t d", p=P, t=TPC)
        block = ctx.enter_context(nc.Block())

        @block.sync
        def _(sp):
            sp.dma_start(cond[:], T["c"]).then_inc(S("cond_in"), 16)
            sp.dma_start(x_in[0][P - MEM:P, :], T["mem"]).then_inc(S("mem_in"), 16)
            for j in range(3):
                sp.dma_start(wmod[j], T["wmod"][:, :, j * CH:(j + 1) * CH]).then_inc(S("wmod_in"), 16)

            def load_chunks(chunks):
                for c in chunks:
                    wait_past(sp, S("stats"), c - PRE + 1)
                    sp.dma_start(x_pre[c % PRE], x_chunks[c]).then_inc(S(f"x_pre{c}"), 16)

            load_chunks(range(0, 3))
            sp.dma_start(wqk[:], T["wqkT"]).then_inc(S("wqk_in"), 16)
            sp.dma_start(wv_raw, T["wvT"]).then_inc(S("wv_in"), 16)
            sp.dma_start(dW1T[:], T["w1T"]).then_inc(S("w1_in"), 16)
            sp.dma_start(b1row[:], T["b1row"]).then_inc(S("b1row_in"), 16)
            sp.dma_start(dW2[:].rearrange("p k n -> p (k n)"), T["w2T"].rearrange("p k n -> p (k n)"))\
              .then_inc(S("w2T_in"), 16)
            sp.dma_start(b2row[:], T["b2row"]).then_inc(S("b1row_in"), 16)
            sp.dma_start(woT[:], T["woT"]).then_inc(S("wo_in"), 16)
            sp.dma_start(w2n_raw[:], T["w2n"]).then_inc(S("w2n_in"), 16)
            sp.dma_start(x_in[1][:], x_rows[0:P, :]).then_inc(S("x_in1"), 16)
            load_chunks(range(3, CHUNKS))
            sp.wait_ge(S("stats"), CHUNKS)
            for k in range(DC):
                sp.dma_start(again[k][:], T["w1T"][:, k, :]).then_inc(S("w1_again"), 16)
            for name, into in (("b2c", b2c), ("b1c", b1c), ("alpha", alpha), ("theta", theta)):
                sp.dma_start(into[:], T[name]).then_inc(S("small_in"), 16)

            def step(n, p):
                sp.wait_ge(S("xn"), n) if known(n, 1) else sp.wait_ge(S("xm"), 1)
                sp.dma_start(x_in[p][:], x_rows[bass.ds((n + 1) * P, P), :]).then_inc(S(f"x_in{p}"), 16)
                keep_xT(n)
                keep_swaT(n - 1)

            def keep_xT(n):
                if known(n, 1):
                    sp.wait_ge(S("xT"), n + 1)
                    sp.dma_start(T["xT"][bass.ds((n - 1) * P, P), :], flat(xT[:])).then_inc(S("xT_out"), 16)

            def keep_swaT(n):
                if known(n, 1):
                    sp.wait_ge(S("swaT"), n + 1)
                    sp.dma_start(T["swaT"][bass.ds((n - 1) * P, P), :], flat(swaT[:])).then_inc(S("swaT_out"), 16)

            def clear_slots(i):
                part = bass.ds(i * CLEARED, CLEARED)
                for half, rows in enumerate((P, CAP_B)):
                    sp.dma_start(slots[half * P:half * P + rows, part, :],
                                 fill[0:rows, half, :].unsqueeze(1).to_broadcast([rows, CLEARED, ROW]))\
                        .then_inc(S("slots_out"), 16)

            step(0, 0)
            step(1, 1)
            step(2, 0)
            sp.wait_ge(S("fill"), 1)
            for half, rows in enumerate((P, CAP_B)):
                sp.dma_start(T["out"][TOKENS + half * P:TOKENS + half * P + rows, :], fill[0:rows, half, 0:D])\
                    .then_inc(S("spare_out"), 16)
            clear_slots(0)
            with sp.Fori(1, TILES // 2 - 1) as i:
                step(i * 2 + 1, 1)
                clear_slots(i)
                step(i * 2 + 2, 0)
            clear_slots(TILES // 2 - 1)
            for n in (LAST - 1, LAST):
                keep_xT(n)
                keep_swaT(n - 1)
            keep_swaT(LAST)
            sp.wait_ge(S("slots_out"), 2 * 16 * E // CLEARED)
            sp.wait_ge(S("spare_out"), 32)
            sp.wait_ge(S("xT_out"), 16 * TILES)
            sp.wait_ge(S("swaT_out"), 16 * TILES)

        @block.gpsimd
        def _(pool):
            pool.memset(ident[:], 0.0)
            pool.memset(ones[:], 1.0).then_inc(S("ones"), 1)
            pool.memset(x_in[0][0:P - MEM, :], 0.0)
            pool.memset(v[:, 1, :], 0.0)
            pool.memset(e_sum[:], 0.0)
            pool.memset(fill[:], 0.0)
            pool.memset(masks[:], 0.0).then_inc(S("zeroed"), 1)
            pool.wait_ge(S("zeroed"), 1)
            for part in kT:
                ins = pool.tensor_copy(part[:, :, 1, :], masks[:, 0, :].rearrange("p (c t) -> p c t", c=DC))
            ins.then_inc(S("kv_zero"), 1)
            pool.wait_ge(S("kv_zero"), 1)
            pool.affine_select(out=ident[:], in_=ident[:], compare_op=ALU.not_equal, fill=1.0, base=0,
                               pattern=[[-1, P]], channel_multiplier=1).then_inc(S("ident"), 1)
            for m, own in ((0, 0), (1, 1), (2, 0), (3, 1)):
                prev = 1 - own
                a = masks[:, m, own * P:(own + 1) * P]
                pool.affine_select(out=a, in_=a, compare_op=ALU.is_ge, fill=NEG, base=0,
                                   pattern=[[-1, P]], channel_multiplier=1)
                b = masks[:, m, prev * P:(prev + 1) * P]
                pool.affine_select(out=b, in_=b, compare_op=ALU.is_gt, fill=NEG, base=0,
                                   pattern=[[1, P]], channel_multiplier=-1).then_inc(S("banded"), 1)
            pool.wait_ge(S("banded"), 4)
            pool.memset(masks[:, 0, P:2 * P], NEG)
            pool.memset(masks[:, 0, 0:P - MEM], NEG)
            pool.memset(masks[:, 1, 0:P - MEM], NEG).then_inc(S("masks"), 1)
            pool.iota(slot_id[:, 0:1], pattern=[[0, 1]], base=TOKENS, channel_multiplier=1)
            pool.iota(slot_id[:, 1:2], pattern=[[0, 1]], base=TOKENS + P, channel_multiplier=1).then_inc(S("slot_id"), 1)
            pool.wait_ge(S("slot_id"), 1)
            pool.tensor_copy(fill[:, :, D + 1:D + 2].bitcast(I32), slot_id[:].unsqueeze(2)).then_inc(S("fill"), 1)
            pool.wait_ge(S("mem_in"), 16)
            pool.tensor_copy(xm[:], x_in[0][:]).then_inc(S("xm"), 1)

            def modulate(n):
                pool.wait_ge(S("xn"), n)
                pool.wait_ge(S("xT_mm"), n)
                pool.wait_ge(S("xm_low"), n)
                pool.tensor_tensor(xm[:], xn[:], mod[:, 1, :], ALU.mult).then_inc(S("xm_scaled"), 1)
                pool.wait_ge(S("xm_scaled"), n)
                pool.tensor_tensor(xm[:], xm[:], mod[:, 0, :], ALU.add).then_inc(S("xm"), 1)

            for i, (name, raw, pair) in enumerate((("w2T_low", dW2, w2T), ("w2n_low", w2n_raw, w2n))):
                pool.wait_ge(S("w_high"), i + 3)
                pool.tensor_tensor(flat(pair[1][:]), flat(raw[:]), flat(pair[0][:]).bitcast(F32), ALU.subtract)\
                    .then_inc(S(name), 1)
            pool.wait_ge(S("mod"), 1)

            def sums(m):
                pool.wait_ge(S("dz"), 2 * m + 2)
                wait_past(pool, S("dz_sum"), m)
                pool.tensor_tensor(dz_sum[:], dz_sum[:], dz[:], ALU.add).then_inc(S("dz_sum"), 1)

            def body(n, p, more):
                pool.wait_ge(S("xm_high"), n + 1)
                wait_past(pool, S("dW_mm"), 8 * n - 8)
                pool.tensor_tensor(xms[p][1][:], xm[:], xms[p][0][:].bitcast(F32), ALU.subtract)\
                    .then_inc(S("xm_low"), 1)
                pool.wait_ge(S("prec"), n + 1)
                pool.tensor_tensor(prob[:], prob[:], prec[:].unsqueeze(2).to_broadcast([P, HEADS, 2 * P]),
                                   ALU.mult).then_inc(S("prob"), 1)
                pool.wait_ge(S("sg"), n + 1)
                wait_past(pool, S("hT_mm"), 2 * n)
                wait_past(pool, S("h_low"), n)
                pool.tensor_tensor(h[:], zb[:], sg[:], ALU.mult).then_inc(S("h"), 1)
                if more:
                    modulate(n + 1)
                wait_past(pool, S("dz"), 2 * n)
                pool.wait_ge(S("h"), n + 1)
                pool.tensor_tensor(gp[:], h[:], sg[:], ALU.mult).then_inc(S("h_sg"), 1)
                pool.wait_ge(S("h_sg"), n + 1)
                pool.tensor_tensor(sg[:], h[:], sg[:], ALU.add).then_inc(S("h_plus"), 1)
                pool.wait_ge(S("h_plus"), n + 1)
                pool.tensor_tensor(gp[:], sg[:], gp[:], ALU.subtract).then_inc(S("gp"), 1)
                if known(n, 1):
                    sums(n - 1)
                pool.wait_ge(S("e"), n + 1)
                wait_past(pool, S("e_sum"), n)
                pool.tensor_tensor(e_sum[:], e_sum[:], e[:], ALU.add).then_inc(S("e_sum"), 1)

            body(0, 0, True)
            pool.memset(dz_sum[:], 0.0)
            pool.wait_ge(S("w_low"), 2)
            pool.wait_ge(S("w2T_low"), 1)
            pool.memset(dW1T[:], 0.0)
            pool.memset(dW2[:], 0.0).then_inc(S("d_zero"), 1)
            body(1, 1, True)
            body(2, 0, True)
            with pool.Fori(1, TILES // 2 - 1) as i:
                body(i * 2 + 1, 1, True)
                body(i * 2 + 2, 0, True)
            body(LAST - 1, 1, True)
            body(LAST, 0, False)
            sums(LAST)

        @block.scalar
        def _(act):
            act.wait_ge(S("cond_in"), 16)
            act.activation(cond_s[:], cond[:], ACT.Sigmoid).then_inc(S("cond_s"), 1)

            def weight_high(name, raw, high):
                act.wait_ge(S(name + "_in"), 16)
                act.copy(flat(high[:]), flat(raw)).then_inc(S("w_high"), 1)

            def turned(n):
                act.wait_ge(S("xT_mm"), n + 1)
                wait_past(act, S("qk_mm"), n)
                wait_past(act, S("xT_out"), (n - 1) * 16)
                act.copy(flat(xT[:]), bank(6, D)).then_inc(S("xT"), 1)
                wait_past(act, S("z_mm"), 2 * n)
                act.copy(flat(xTs[0][:]), bank(6, D)).then_inc(S("xT_high"), 1)

            def error_high(m):
                act.wait_ge(S("e"), m + 1)
                wait_past(act, S("dW_mm"), 8 * m)
                act.copy(es[0][:], e[:]).then_inc(S("e_high"), 1)
                act.wait_ge(S("eT_mm"), m + 1)
                wait_past(act, S("dh_mm"), 2 * m)
                act.copy(flat(eT[0][:]), bank(2, D)).then_inc(S("eT_high"), 1)
                wait_past(act, S("swaT_out"), (m - 1) * 16)
                act.copy(flat(swaT[:]), psum[2][:, D:2 * D]).then_inc(S("swaT"), 1)

            def dz_high(m):
                wait_past(act, S("dW_mm"), 8 * m)
                for g in range(2):
                    act.wait_ge(S("dz"), 2 * m + g + 1)
                    act.copy(dzs[0][:, g * CH:(g + 1) * CH], dz[:, g * CH:(g + 1) * CH]).then_inc(S("dz_high"), 1)

            def body(n, p, more):
                act.wait_ge(S("qk_mm"), n + 1)
                wait_past(act, S("s_mm"), 2 * n)
                if not known(n, 1):
                    act.wait_ge(S("kv_zero"), 1)
                act.copy(flat(qT[0][:]), bank(0, D))
                act.copy(kT[0][:, :, p, :], psum[0][:, D:2 * D].rearrange("p (c t) -> p c t", c=DC))\
                   .then_inc(S("qk_high"), 1)
                act.wait_ge(S("v_mm"), n + 1)
                wait_past(act, S("o_mm"), n)
                act.copy(v[:, p, :], bank(1, D)).then_inc(S("v"), 1)
                if known(n, 1):
                    error_high(n - 1)
                act.wait_ge(S("xm"), n + 1)
                wait_past(act, S("dW_mm"), 8 * n - 8)
                act.copy(xms[p][0][:], xm[:]).then_inc(S("xm_high"), 1)
                if not known(n, 1):
                    act.wait_ge(S("ones"), 1)
                act.activation(table[:], ones[:, 0:1], ACT.Exp)
                act.wait_ge(S("npeak"), n + 1)
                wait_past(act, S("probT_mm"), 2 * n)
                for s in range(HEADS):
                    ins = act.activation(prob[:, s, :], logit[:, s, :], ACT.Exp, bias=npeak[:, s:s + 1],
                                         accum_out=psums[:, s:s + 1])
                ins.then_inc(S("prob_exp"), 1)
                act.wait_ge(S("zb"), 2 * n + 2)
                wait_past(act, S("gp"), n)
                act.activation(sg[:], zb[:], ACT.Sigmoid).then_inc(S("sg"), 1)
                if known(n, 1):
                    dz_high(n - 1)
                act.wait_ge(S("h"), n + 1)
                act.copy(hsp[p][0][:], h[:]).then_inc(S("h_high"), 1)
                act.wait_ge(S("probT_mm"), 2 * n + 2)
                wait_past(act, S("o_mm"), n)
                act.copy(flat(probT[:, 2:4, :, :]), bank(2)).then_inc(S("probT_hi"), 1)
                for g in range(2):
                    act.wait_ge(S("hT_mm"), 2 * n + g + 1)
                    wait_past(act, S("pred_mm"), n)
                    act.copy(flat(hT[0][:, 4 * g:4 * g + 4, :]), bank(3 + g)).then_inc(S("hT_high"), 1)
                if more:
                    turned(n + 1)
                act.wait_ge(S("swa_mm"), n + 1)
                wait_past(act, S("eT_mm"), n)
                wait_past(act, S("e"), n)
                act.copy(swa[:], psum[7][:, D:2 * D]).then_inc(S("swa"), 1)

            weight_high("wv", wv_raw, wv[0])
            weight_high("w1", dW1T[:], w1T[0])
            turned(0)
            weight_high("w2T", dW2[:], w2T[0])
            weight_high("w2n", w2n_raw[:], w2n[0])
            body(0, 0, True)
            body(1, 1, True)
            body(2, 0, True)
            with act.Fori(1, TILES // 2 - 1) as i:
                body(i * 2 + 1, 1, True)
                body(i * 2 + 2, 0, True)
            body(LAST - 1, 1, True)
            body(LAST, 0, False)
            error_high(LAST)
            dz_high(LAST)
            act.wait_ge(S("rates"), 1)
            for i, grad in enumerate((dW2, dW1T)):
                act.wait_ge(S("dW"), 8 * LAST + 4 * (i + 1))
                act.activation(flat(grad[:]), flat(grad[:]), ACT.Copy, scale=step[:, 0:1]).then_inc(S("stepped"), 1)
            for g in range(4):
                if g == 2:
                    for k in range(DC):
                        act.wait_ge(S("w1_new"), k + 1)
                        act.copy(w1T[0][:, k, :], dW1T[:, k, :]).then_inc(S("w_high"), 1)
                act.wait_ge(S("w2T_mm"), g + 1)
                act.copy(flat(w2T[0][:, 2 * g:2 * g + 2, :]), bank(g)).then_inc(S("w_high"), 1)

        @block.vector
        def _(dve):
            def weight_low(i, raw, pair):
                dve.wait_ge(S("w_high"), i)
                dve.tensor_tensor(flat(pair[1][:]), flat(raw), flat(pair[0][:]).bitcast(F32), ALU.subtract)\
                   .then_inc(S("w_low"), 1)

            def statistics(chunks):
                for c in chunks:
                    dve.wait_ge(S(f"x_pre{c}"), 16)
                    for t in range(TPC):
                        ins = dve.bn_stats(stats[:, c * TPC + t, :], x_pre[c % PRE][:, t, :])
                    ins.then_inc(S("stats"), 1)

            dve.wait_ge(S("cond_s"), 1)
            dve.tensor_tensor(cond_s[:], cond_s[:], cond[:], ALU.mult).then_inc(S("cond_silu"), 1)
            dve.wait_ge(S("cond_silu"), 1)
            dve.wait_ge(S("ones"), 1)
            for k in range(DC):
                ins = dve.tensor_scalar(cond_w[:, k, :], ones[:], cond_s[:, k:k + 1], None, ALU.mult)
            ins.then_inc(S("cond_w"), 1)
            statistics(range(0, 3))
            weight_low(1, wv_raw, wv)
            dve.wait_ge(S("mod_mm"), 1)
            for j in range(3):
                ins = dve.tensor_copy(flat(mod[:, 2 * j:2 * j + 2, :]), bank(j))
            ins.then_inc(S("mod_copied"), 1)
            weight_low(2, dW1T[:], w1T)
            dve.wait_ge(S("mod_copied"), 1)
            for j in (1, 4):
                dve.tensor_scalar(mod[:, j, :], mod[:, j, :], 1.0, None, ALU.add)
            for j, g in enumerate((2, 5)):
                dve.scalar_tensor_tensor(out=clamp[:, j, :], in0=mod[:, g, :], scalar=-1.0, in1=mod[:, g, :],
                                         op0=ALU.mult, op1=ALU.max).then_inc(S("clamped"), 1)
                dve.wait_ge(S("clamped"), 3 * j + 1)
                dve.tensor_scalar(clamp[:, j, :], clamp[:, j, :], 0.25, None, ALU.max)
                dve.tensor_scalar(mod[:, g, :], mod[:, g, :], 0.0, 2.0, ALU.is_ge, ALU.mult).then_inc(S("clamped"), 1)
                dve.wait_ge(S("clamped"), 3 * j + 2)
                dve.scalar_tensor_tensor(out=mod[:, g, :], in0=mod[:, g, :], scalar=-1.0, in1=clamp[:, j, :],
                                         op0=ALU.add, op1=ALU.mult).then_inc(S("clamped"), 1)
            dve.wait_ge(S("clamped"), 6)
            dve.memset(peak[:], 0.0).then_inc(S("mod"), 1)

            def deviations():
                dve.wait_ge(S("stats"), CHUNKS)
                for t in range(TILES):
                    ins = dve.bn_aggr(moments[:, t, :], stats[:, t, :])
                ins.then_inc(S("moments"), 1)
                dve.wait_ge(S("moments"), 1)
                inverse_sqrt(dve, S("rstd"), 0, rstd[:], moments[:, :, 1], half[:])

            dve.wait_ge(S("mod"), 1)
            dve.wait_ge(S("b1row_in"), 32)
            dve.wait_ge(S("masks"), 1)

            def normalise(n, p, loads):
                dve.wait_ge(S(f"x_in{p}"), loads * 16)
                wait_past(dve, S("xm_scaled"), n - 1)
                m = n - 1
                dve.tensor_scalar(xn[:], x_in[p][:], moments[:, bass.ds(m, 1), 0], rstd[:, bass.ds(m, 1)],
                                  ALU.subtract, ALU.mult).then_inc(S("xn"), 1)

            def turned_low(n):
                dve.wait_ge(S("xT_high"), n + 1)
                wait_past(dve, S("z_mm"), 2 * n)
                dve.tensor_tensor(flat(xTs[1][:]), bank(6, D), flat(xTs[0][:]).bitcast(F32), ALU.subtract)\
                   .then_inc(S("xT_low"), 1)

            def error_low(m):
                dve.wait_ge(S("e_high"), m + 1)
                wait_past(dve, S("dW_mm"), 8 * m)
                dve.tensor_tensor(es[1][:], e[:], es[0][:].bitcast(F32), ALU.subtract).then_inc(S("e_low"), 1)
                dve.wait_ge(S("eT_high"), m + 1)
                wait_past(dve, S("dh_mm"), 2 * m)
                dve.wait_ge(S("swaT"), m + 1)
                dve.tensor_tensor(flat(eT[1][:]), bank(2, D), flat(eT[0][:]).bitcast(F32), ALU.subtract)\
                   .then_inc(S("eT_low"), 1)

            def grad_z(m):
                dve.wait_ge(S("gp"), m + 1)
                wait_past(dve, S("dW_mm"), 8 * m)
                wait_past(dve, S("dz_sum"), m)
                for g in range(2):
                    dve.wait_ge(S("dh_mm"), 2 * m + g + 1)
                    dve.tensor_tensor(dz[:, g * CH:(g + 1) * CH], bank((7, 0)[g]), gp[:, g * CH:(g + 1) * CH],
                                      ALU.mult).then_inc(S("dz"), 1)
                for g in range(2):
                    dve.wait_ge(S("dz_high"), 2 * m + g + 1)
                    c = slice(g * CH, (g + 1) * CH)
                    dve.tensor_tensor(dzs[1][:, c], dz[:, c], dzs[0][:, c].bitcast(F32), ALU.subtract)\
                       .then_inc(S("dz_low"), 1)

            def gather_dW(m, js):
                for j in js:
                    into = dW2 if j < 4 else dW1T
                    part = into[:, (j % 4) // 2, (j % 2) * CH:(j % 2 + 1) * CH]
                    dve.wait_ge(S("dW_mm"), 8 * m + j + 1)
                    wait_past(dve, S("dW"), 8 * m + j - 7)
                    dve.tensor_tensor(part, part, bank(DW_BANK[j]), ALU.add).then_inc(S("dW"), 1)

            def body(n, p, mask, loads):
                dve.wait_ge(S("qk_high"), n + 1)
                dve.tensor_tensor(flat(qT[1][:]), bank(0, D), flat(qT[0][:]).bitcast(F32), ALU.subtract)
                dve.tensor_tensor(kT[1][:, :, p, :], psum[0][:, D:2 * D].rearrange("p (c t) -> p c t", c=DC),
                                  kT[0][:, :, p, :].bitcast(F32), ALU.subtract).then_inc(S("qk"), 1)
                if known(n, 1):
                    error_low(n - 1)
                else:
                    statistics(range(3, 4))
                for s in range(HEADS):
                    wait_past(dve, S("prob_exp"), n)
                    wait_apart(dve, S("s_mm"), 2 * n + s // 2 + 1, S("passed_dve"))
                    ins = dve.tensor_tensor_reduce(
                        out=logit[:, s, :], in0=psum[3 + s // 2][:, (s % 2) * D:(s % 2 + 1) * D], in1=masks[:, mask, :],
                        scale=float(DH) ** -0.5, scalar=-3e38, op0=ALU.add, op1=ALU.max, accum_out=peak[:, s:s + 1])
                    if s % 2:
                        ins.then_inc(S("peak"), 1)
                dve.wait_ge(S("peak"), 2 * n + 2)
                dve.tensor_scalar(npeak[:], peak[:], -1.0, None, ALU.mult).then_inc(S("npeak"), 1)
                if not known(n, 1):
                    statistics(range(4, 6))
                for g in range(2):
                    dve.wait_ge(S("z_mm"), 2 * n + g + 1)
                    wait_past(dve, S("h"), n)
                    dve.tensor_tensor(zb[:, g * CH:(g + 1) * CH], bank(5 + g), b1row[:, g * CH:(g + 1) * CH], ALU.add)\
                       .then_inc(S("zb"), 1)
                dve.wait_ge(S("prob_exp"), n + 1)
                wait_past(dve, S("prob"), n)
                dve.reciprocal(prec[:], psums[:]).then_inc(S("prec"), 1)
                if not known(n, 1):
                    statistics(range(6, CHUNKS))
                    deviations()
                if loads is not None:
                    normalise(n + 1, 1 - p, loads)
                if known(n, 1):
                    if isinstance(n, int) and n == 1:
                        dve.wait_ge(S("d_zero"), 1)
                    grad_z(n - 1)
                if known(n, 1):
                    gather_dW(n - 1, range(6))
                dve.wait_ge(S("probT_mm"), 2 * n + 1)
                wait_past(dve, S("o_mm"), n)
                dve.tensor_copy(flat(probT[:, 0:2, :, :]), bank(1)).then_inc(S("probT_lo"), 1)
                if known(n, 1):
                    gather_dW(n - 1, range(6, 7))
                for g in range(2):
                    dve.wait_ge(S("hT_high"), 2 * n + g + 1)
                    wait_past(dve, S("pred_mm"), n)
                    dve.tensor_tensor(flat(hT[1][:, 4 * g:4 * g + 4, :]), bank(3 + g),
                                      flat(hT[0][:, 4 * g:4 * g + 4, :]).bitcast(F32), ALU.subtract)\
                       .then_inc(S("hT_low"), 1)
                if known(n, 1):
                    gather_dW(n - 1, range(7, 8))
                dve.wait_ge(S("o_mm"), n + 1)
                wait_past(dve, S("swa_mm"), n)
                dve.tensor_copy(flat(oT[:]), bank(5, D)).then_inc(S("oT"), 1)
                if loads is not None:
                    turned_low(n + 1)
                dve.wait_ge(S("h_high"), n + 1)
                dve.tensor_tensor(hsp[p][1][:], h[:], hsp[p][0][:].bitcast(F32), ALU.subtract)\
                   .then_inc(S("h_low"), 1)
                dve.wait_ge(S("swa"), n + 1)
                wait_past(dve, S("e"), n)
                dve.tensor_tensor(pred[:], bank(7, D), b2row[:], ALU.add).then_inc(S("pred"), 1)
                dve.wait_ge(S("pred"), n + 1)
                wait_past(dve, S("eT_mm"), n)
                wait_past(dve, S("e_low"), n)
                wait_past(dve, S("e_sum"), n)
                if not known(n, 1):
                    dve.tensor_tensor(e[:], pred[:], swa[:], ALU.subtract).then_inc(S("e_raw"), 1)
                    dve.wait_ge(S("e_raw"), 1)
                    dve.memset(e[0:P - MEM, :], 0.0).then_inc(S("e"), 1)
                else:
                    dve.tensor_tensor(e[:], pred[:], swa[:], ALU.subtract).then_inc(S("e"), 1)

            turned_low(0)
            body(0, 0, 0, 1)
            body(1, 1, 1, 1)
            body(2, 0, 2, 2)
            with dve.Fori(1, TILES // 2 - 1) as i:
                body(i * 2 + 1, 1, 3, i + 1)
                body(i * 2 + 2, 0, 2, i + 2)
            body(LAST - 1, 1, 3, TILES // 2)
            body(LAST, 0, 2, None)
            dve.wait_ge(S("small_in"), 64)
            dve.tensor_scalar(keep[:], alpha[:], -1.0, 1.0, ALU.mult, ALU.add)
            dve.tensor_scalar(step[:], theta[:], -1.0, None, ALU.mult).then_inc(S("rates"), 1)
            error_low(LAST)
            grad_z(LAST)
            gather_dW(LAST, range(8))
            dve.wait_ge(S("rates"), 1)
            dve.wait_ge(S("stepped"), 1)
            dve.scalar_tensor_tensor(out=dW2[:], in0=w2n_raw[:], scalar=keep[:, 0:1], in1=dW2[:],
                                     op0=ALU.mult, op1=ALU.add).then_inc(S("w2_new"), 1)
            dve.wait_ge(S("stepped"), 2)
            dve.wait_ge(S("w1_again"), 32)
            for k in range(DC):
                dve.scalar_tensor_tensor(out=dW1T[:, k, :], in0=again[k][:], scalar=keep[:, 0:1],
                                         in1=dW1T[:, k, :], op0=ALU.mult, op1=ALU.add).then_inc(S("w1_new"), 1)
            dve.wait_ge(S("db_mm"), 1)
            dve.tensor_scalar(db[:], bank(4, HC + DC), step[:, 0:1], None, ALU.mult).then_inc(S("db"), 1)
            dve.wait_ge(S("db"), 1)
            dve.scalar_tensor_tensor(out=b1c[:], in0=b1c[:], scalar=keep[:, 0:1], in1=db[:, 0:HC],
                                     op0=ALU.mult, op1=ALU.add)
            dve.scalar_tensor_tensor(out=b2c[:], in0=b2c[:], scalar=keep[:, 0:1], in1=db[:, HC:HC + DC],
                                     op0=ALU.mult, op1=ALU.add).then_inc(S("b_new"), 1)
            for g in range(4):
                if g == 2:
                    for k in range(DC):
                        dve.wait_ge(S("w_high"), 4 + g + k + 1)
                        dve.wait_ge(S("w1_new"), DC)
                        dve.tensor_tensor(w1T[1][:, k, :], dW1T[:, k, :], w1T[0][:, k, :].bitcast(F32), ALU.subtract)\
                           .then_inc(S("w_low"), 1)
                dve.wait_ge(S("w_high"), 4 + g + 1 + (DC if g >= 2 else 0))
                dve.tensor_tensor(flat(w2T[1][:, 2 * g:2 * g + 2, :]), bank(g),
                                  flat(w2T[0][:, 2 * g:2 * g + 2, :]).bitcast(F32), ALU.subtract).then_inc(S("w_low"), 1)
            dve.wait_ge(S("b_new"), 1)

        @block.tensor
        def _(pe):
            pe.wait_ge(S("cond_w"), 1)
            pe.wait_ge(S("wmod_in"), 48)
            for j in range(3):
                for k in range(DC):
                    ins = mm(bank(j), cond_w[:, k, :], wmod[j][:, k, :], k == 0, k == DC - 1)
            ins.then_inc(S("mod_mm"), 1)
            pe.wait_ge(S("mod_copied"), 1)
            pe.wait_ge(S("ident"), 1)

            def turn(out, src):
                return nc.tensor.transpose(out, src, ident[:])

            def turn_x(n):
                pe.wait_ge(S("xm"), n + 1)
                wait_past(pe, S("dW"), 8 * n - 10)
                if isinstance(n, int) and n == 1:
                    pe.wait_ge(S("zb"), 2)
                for k in range(DC):
                    ins = turn(psum[6][:, k * P:(k + 1) * P], xm[:, k * P:(k + 1) * P])
                ins.then_inc(S("xT_mm"), 1)

            def turn_error(m):
                pe.wait_ge(S("e"), m + 1)
                pe.wait_ge(S("probT_hi"), m + 1)
                for k in range(DC):
                    turn(psum[2][:, k * P:(k + 1) * P], e[:, k * P:(k + 1) * P])
                for k in range(DC):
                    ins = turn(psum[2][:, D + k * P:D + (k + 1) * P], swa[:, k * P:(k + 1) * P])
                ins.then_inc(S("eT_mm"), 1)

            def backward(m):
                pe.wait_ge(S("eT_low"), m + 1)
                if not known(m, 1):
                    pe.wait_ge(S("w2n_low"), 1)
                for g in range(2):
                    for k in range(DC):
                        ins = mm_split(nc, bank((7, 0)[g]), cut(eT, slice(None), k, slice(None)),
                                       cut(w2n, slice(None), k, slice(g * CH, (g + 1) * CH)), k == 0, k == DC - 1)
                    ins.then_inc(S("dh_mm"), 1)

            def gradient(m, p, tail=False):
                n = m + 1
                pe.wait_ge(S("e_low"), m + 1)
                pe.wait_ge(S("h_low"), m + 1)
                for j in range(4):
                    if j == 0:
                        pe.wait_ge(S("probT_lo" if tail else "v"), m + 1 if tail else n + 1)
                    elif j > 1 and not tail:
                        pe.wait_ge(S("peak"), 2 * n + j - 1)
                    mm_split(nc, bank(DW_BANK[j]), cut(es, slice(None), slice((j // 2) * P, (j // 2 + 1) * P)),
                             cut(hsp[p], slice(None), slice((j % 2) * CH, (j % 2 + 1) * CH)), True, True)\
                        .then_inc(S("dW_mm"), 1)
                pe.wait_ge(S("xm_low"), m + 1)
                for j in range(4, 8):
                    if j < 6 and not tail:
                        pe.wait_ge(S("zb"), 2 * n + j - 3)
                    g = j - 4
                    pe.wait_ge(S("dz_low"), 2 * m + g % 2 + 1)
                    if j == 6:
                        pe.wait_ge(S("dz"), 2 * m + 2)
                    mm_split(nc, bank(DW_BANK[j]), cut(xms[p], slice(None), slice((g // 2) * P, (g // 2 + 1) * P)),
                             cut(dzs, slice(None), slice((g % 2) * CH, (g % 2 + 1) * CH)), True, True)\
                        .then_inc(S("dW_mm"), 1)

            def hidden_layer(n, g, ks):
                for k in ks:
                    ins = mm_split(nc, bank(5 + g), cut(xTs, slice(None), k, slice(None)),
                                   cut(w1T, slice(None), k, slice(g * CH, (g + 1) * CH)), k == 0, k == DC - 1)
                if ks[-1] == DC - 1:
                    ins.then_inc(S("z_mm"), 1)

            def body(n, p, more):
                first = not known(n, 1)
                if first:
                    pe.wait_ge(S("wqk_in"), 16)
                pe.wait_ge(S("xT"), n + 1)
                wait_past(pe, S("dW"), 8 * n - 8)
                for j in range(4):
                    for k in range(DC):
                        ins = mm(psum[0][:, j * P:(j + 1) * P], wqk[:, j // 2, k, (j % 2) * P:(j % 2 + 1) * P],
                                 xT[:, k, :], k == 0, k == DC - 1)
                ins.then_inc(S("qk_mm"), 1)
                wait_past(pe, S("probT_lo"), n)
                pe.wait_ge(S("xT_low"), n + 1)
                if first:
                    pe.wait_ge(S("w_low"), 2)
                for k in range(DC):
                    ins = mm_split(nc, bank(1, D), cut(xTs, slice(None), k, slice(None)),
                                   cut(wv, slice(None), k, slice(None)), k == 0, k == DC - 1)
                ins.then_inc(S("v_mm"), 1)
                if not first:
                    turn_error(n - 1)
                hidden_layer(n, 0, (0,))
                pe.wait_ge(S("qk"), n + 1)
                for b in range(2):
                    rows = slice(b * DH, (b + 1) * DH)
                    for c in range(DC):
                        ins = mm_split(nc, psum[3 + b][:, c * D:(c + 1) * D], cut(qT, rows, c, slice(None)),
                                       cut(kT, rows, c, slice(None), slice(None)), True, True)
                    ins.then_inc(S("s_mm"), 1)
                hidden_layer(n, 0, (1,))
                hidden_layer(n, 1, (0, 1))
                if not first:
                    backward(n - 1)
                    gradient(n - 1, 1 - p)
                pe.wait_ge(S("prob"), n + 1)
                for g in range(2):
                    wait_past(pe, S("dW"), 8 * n - 7 + g)
                    if first:
                        pe.wait_ge(S("v"), 1)
                    for b in range(4):
                        ins = turn(psum[1 + g][:, b * P:(b + 1) * P],
                                   prob[:, 2 * g + b // 2, (b % 2) * P:(b % 2 + 1) * P])
                    ins.then_inc(S("probT_mm"), 1)
                pe.wait_ge(S("h"), n + 1)
                for g in range(2):
                    wait_past(pe, S("dW"), 8 * n - 5 + g)
                    for b in range(4):
                        ins = turn(psum[3 + g][:, b * P:(b + 1) * P], h[:, (4 * g + b) * P:(4 * g + b + 1) * P])
                    ins.then_inc(S("hT_mm"), 1)
                if more:
                    turn_x(n + 1)
                pe.wait_ge(S("probT_lo"), n + 1)
                pe.wait_ge(S("probT_hi"), n + 1)
                pe.wait_ge(S("v"), n + 1)
                wait_past(pe, S("dW"), 8 * n - 3)
                for s in range(HEADS):
                    hd = HEAD_AT[s]
                    for t in range(2):
                        ins = mm(psum[5][(hd % 2) * DH:(hd % 2 + 1) * DH, (hd // 2) * P:(hd // 2 + 1) * P],
                                 v[:, t, hd * DH:(hd + 1) * DH], probT[:, s, t, :], t == 0, t == 1)
                ins.then_inc(S("o_mm"), 1)
                wait_past(pe, S("dW"), 8 * n - 1)
                if first:
                    pe.wait_ge(S("w2T_low"), 1)
                for k in range(HC):
                    if k % 4 == 0:
                        pe.wait_ge(S("hT_low"), 2 * n + k // 4 + 1)
                    ins = mm_split(nc, bank(7, D), cut(hT, slice(None), k, slice(None)),
                                   cut(w2T, slice(None), k, slice(None)), k == 0, k == HC - 1)
                ins.then_inc(S("pred_mm"), 1)
                if first:
                    pe.wait_ge(S("wo_in"), 16)
                pe.wait_ge(S("oT"), n + 1)
                for k in range(DC):
                    ins = mm(psum[7][:, D:2 * D], oT[:, k, :], woT[:, k, :], k == 0, k == DC - 1)
                ins.then_inc(S("swa_mm"), 1)

            turn_x(0)
            body(0, 0, True)
            body(1, 1, True)
            body(2, 0, True)
            with pe.Fori(1, TILES // 2 - 1) as i:
                body(i * 2 + 1, 1, True)
                body(i * 2 + 2, 0, True)
            body(LAST - 1, 1, True)
            body(LAST, 0, False)
            turn_error(LAST)
            backward(LAST)
            gradient(LAST, 0, tail=True)
            pe.wait_ge(S("dz_sum"), LAST + 1)
            pe.wait_ge(S("e_sum"), LAST + 1)
            pe.wait_ge(S("dW"), 8 * LAST + 4)
            for j in range(HC):
                mm(psum[4][:, j:j + 1], dz_sum[:, j * P:(j + 1) * P], ones[:, 0:1], True, True)
            for j in range(DC):
                ins = mm(psum[4][:, HC + j:HC + j + 1], e_sum[:, j * P:(j + 1) * P], ones[:, 0:1], True, True)
            ins.then_inc(S("db_mm"), 1)
            pe.wait_ge(S("w2_new"), 1)
            for g in range(4):
                for b in range(4):
                    j, k = 2 * g + b // 2, b % 2
                    ins = turn(psum[g][:, b * P:(b + 1) * P], dW2[:, k, j * P:(j + 1) * P])
                ins.then_inc(S("w2T_mm"), 1)


def token_stage(nc, T, buf, psum, S):
    with ExitStack() as ctx:
        def sb(name, shape, dt=F32):
            return ctx.enter_context(nc.sbuf_tensor("b_" + name, shape, dt))

        def split(name, shape):
            return sb(name + "_high", shape, F32R), sb(name + "_low", shape, F32R)

        w1T, w2T, mod, ident, b1c, b2c = (buf[k] for k in ("w1T", "w2T", "mod", "ident", "b1c", "b2c"))
        linT = sb("linT", [P, 2, DC, D])
        wgT = sb("wgT", [P, DC, E])
        s1T = split("s1T", [P, DC, 2 * FFN])
        s2T = split("s2T", [P, FC, D])
        before = sb("before", [P, P], BF16)
        every = sb("every", [P, P], BF16)
        slot_base = sb("slot_base", [P, E])
        token = sb("token", [P, TPC], I32)
        carry = sb("carry", [P, E])
        xT = sb("xT", [P, TPC, D])
        xTs = split("xT", [P, TPC, D])
        swaT = sb("swaT", [P, TPC, D])
        hidden = buf["early"][:].rearrange("p (j n) -> p j n", j=HC)
        h2 = split("h2", [P, HC, CH])
        om = sb("om", [P, TPC, D])
        g1 = sb("g1", [P, TPC, D])
        g2 = sb("g2", [P, TPC, D])
        x = sb("x", [P, TPC, D])
        x2 = sb("x2", [P, TPC, D])
        stats = sb("stats", [P, TPC, 6])
        moments = sb("moments", [P, TPC, 2])
        rstd = sb("rstd", [P, TPC])
        half = sb("half", [P, TPC])
        hm = sb("hm", [P, TPC, D])
        hT = sb("hT", [P, DC, CH])
        hTs = split("hT", [P, DC, CH])
        lg = sb("lg", [P, TPC, E])
        lmax = sb("lmax", [P, TPC])
        gate = sb("gate", [P, TPC, E])
        gsum = sb("gsum", [P, TPC])
        grec = sb("grec", [P, TPC])
        top = sb("top", [P, TPC, TOPK])
        rest = sb("rest", [P, TPC, E])
        chosen = sb("chosen", [P, TPC, E])
        chosen_b = sb("chosen_b", [P, TPC, E], BF16)
        wsum = sb("wsum", [P, TPC])
        wrec = sb("wrec", [P, TPC])
        rank = sb("rank", [P, TPC, E])
        fits = sb("fits", [P, TPC, E])
        slot = sb("slot", [P, TPC, E])
        slot8 = sb("slot8", [P, TPC, TOPK])
        off = sb("off", [P, TPC, TOPK])
        index = sb("index", [P, TPC, TOPK], U32)
        picked = sb("picked", [P, TOPK, E])
        w8 = sb("w8", [P, TPC, TOPK])
        row = sb("row", [P, 2, TOPK, ROW])

        def bank(b, n=CH):
            return psum[b][:, 0:n]

        def mm(out, lhsT, rhs, first, last):
            return nc.tensor.matmul(out, lhsT, rhs, start=first, stop=last, skip_group_check=True)

        def wide(a, n):
            return a.unsqueeze(2).to_broadcast([P, TPC, n])

        def rows_of(a):
            return a.unsqueeze(1).to_broadcast([P, TPC, D])

        def block_of(a, k):
            return a[:, :, k * P:(k + 1) * P]

        def by_tile(a):
            return a.rearrange("p (t n) -> p t n", t=TPC)

        gT, sil, gTs = hidden, [hidden[:, FC + p, :] for p in range(2)], h2
        x2_last, hm_last = xT, swaT
        s2_raw = hidden[:, 0:FC // 2, :].rearrange("p j n -> p (j n)")
        base = g2
        s1_raw = row[:].rearrange("p a b c -> p (a b c)")[:, 0:DC * 2 * FFN]

        x_rows = T["x"].rearrange("(c t p) d -> p (c t) d", p=P, t=TPC)
        xT_tiles = T["xT"].rearrange("(c t p) d -> p (c t) d", p=P, t=TPC)
        swaT_tiles = T["swaT"].rearrange("(c t p) d -> p (c t) d", p=P, t=TPC)
        out_rows = T["out"][0:TOKENS, :].rearrange("(c t p) d -> p (c t) d", p=P, t=TPC)
        BANK_Z = range(8)
        BANK_SH = [2, 3, 4, 5, 6, 7, 0, 1, 2, 3, 4, 5]

        block = ctx.enter_context(nc.Block())

        @block.sync
        def _(sp):
            def tiles(c):
                return bass.ds(c * TPC, TPC)

            def load_xT(c):
                wait_past(sp, S("xT_low"), c)
                sp.dma_start(xT[:], xT_tiles[:, tiles(c), :]).then_inc(S("xT_in"), 16)

            def load_swaT(c):
                wait_past(sp, S("parts"), c)
                sp.dma_start(swaT[:], swaT_tiles[:, tiles(c), :]).then_inc(S("swaT_in"), 16)

            def load(c):
                wait_past(sp, S("x2"), c)
                sp.dma_start(x[:], x_rows[:, tiles(c), :]).then_inc(S("x_in"), 16)

            def store(c):
                sp.wait_ge(S("base"), 2 * c)
                sp.dma_start(out_rows[:, tiles(c - 1), :], base[:]).then_inc(S("base_out"), 16)

            load_xT(0)
            sp.dma_start(s1_raw, T["s1T"].rearrange("p k n -> p (k n)")).then_inc(S("s1_in"), 16)
            load_swaT(0)
            sp.dma_start(linT[:], T["linT"]).then_inc(S("lin_in"), 16)
            sp.dma_start(wgT[:], T["wgT"]).then_inc(S("wg_in"), 16)
            load(0)
            load_xT(1)
            sp.wait_ge(S("h2_low"), 4)
            sp.dma_start(s2_raw, T["s2T"].rearrange("p k n -> p (k n)")).then_inc(S("s2_in"), 16)
            load_xT(2)
            load_swaT(1)
            load(1)
            with sp.Fori(1, CHUNKS - 2) as c:
                load_xT(c + 2)
                load_swaT(c + 1)
                store(c)
                load(c + 1)
            load_swaT(CHUNKS - 1)
            store(CHUNKS - 2)
            load(CHUNKS - 1)
            store(CHUNKS - 1)
            sp.wait_ge(S("gT_low"), CHUNKS * FC)
            sp.dma_start(buf["early"][:, 0:DC * 2 * FFN], T["e1T"][0].rearrange("p k f -> p (k f)"))\
              .then_inc(S("w1_first"), 16)
            store(CHUNKS)
            sp.wait_ge(S("base_out"), 16 * CHUNKS)
            sp.wait_ge(S("w1_first"), 16)

        @block.gpsimd
        def _(pool):
            pool.memset(before[:], 1.0)
            pool.memset(every[:], 1.0)
            pool.memset(carry[:], 0.0).then_inc(S("set"), 1)
            pool.wait_ge(S("set"), 1)
            pool.affine_select(out=before[:], in_=before[:], compare_op=ALU.is_gt, fill=0.0, base=0,
                               pattern=[[1, P]], channel_multiplier=-1)
            pool.iota(slot_base[:], pattern=[[CAP, E]], base=1, channel_multiplier=0,
                      allow_small_or_imprecise_dtypes=True)
            pool.iota(token[:], pattern=[[P, TPC]], base=0, channel_multiplier=1).then_inc(S("route_const"), 1)

            def scatter(c):
                pool.wait_ge(S("index"), c)
                for t in range(TPC):
                    wait_apart(pool, S("row_part"), (c - 1) * TPC + t + 1, S("passed_pool"))
                    pool.tensor_copy(row[:, t % 2, :, D + 1:D + 2].bitcast(I32),
                                     token[:, t:t + 1].unsqueeze(1).to_broadcast([P, TOPK, 1])).then_inc(S("row"), 1)
                    wait_apart(pool, S("row"), (c - 1) * TPC + t + 1, S("passed_pool"))
                    for k in range(TOPK):
                        pool.indirect_dma_start(
                            out=T["slots"], out_offset=bass.IndirectOffsetOnAxis(ap=index[:, t, k:k + 1], axis=0),
                            in_=row[:, t % 2, k, :], in_offset=None,
                            bounds_check=last_slot, oob_is_err=False).then_inc(S(f"row_out{t % 2}"), 16)
                pool.tensor_scalar(token[:], token[:], float(CH), None, ALU.add).then_inc(S("token"), 1)
                pool.wait_ge(S("token"), c)

            last_slot = pool.to_reg(E * CAP - 1)
            scatter(1)
            with pool.Fori(2, CHUNKS + 1) as c:
                scatter(c)
            pool.wait_ge(S("row_out0"), CHUNKS * TPC // 2 * TOPK * 16)
            pool.wait_ge(S("row_out1"), CHUNKS * TPC // 2 * TOPK * 16)

        @block.scalar
        def _(act):
            def late(c):
                for g in range(2):
                    act.wait_ge(S("hT_mm"), 2 * c - 1 + g)
                    act.copy(hT[:, :, g * D:(g + 1) * D],
                             bank(g).rearrange("p (k t) -> p k t", k=DC)).then_inc(S("hT"), 1)
                act.wait_ge(S("hT"), 2 * c)
                act.copy(flat(hTs[0][:]), flat(hT[:])).then_inc(S("hT_high"), 1)
                act.wait_ge(S("lg"), c)
                act.activation(gate[:], lg[:], ACT.Exp).then_inc(S("gate_exp"), 1)

            def late_row(c, t, hm):
                act.wait_ge(S("w8"), (c - 1) * TPC + t + 1)
                wait_past(act, S(f"row_out{t % 2}"), ((c - 1) * 2 + t // 2) * TOPK * 16)
                act.copy(row[:, t % 2, :, 0:D], hm[:, t, :].unsqueeze(1).to_broadcast([P, TOPK, D]))
                act.copy(row[:, t % 2, :, D:D + 1], w8[:, t, :].unsqueeze(2)).then_inc(S("row_part"), 1)

            def late_shared(c, hm):
                def high(j):
                    act.wait_ge(S("gT"), (c - 1) * FC + j + 1)
                    act.copy(gTs[0][:, j, :], gT[:, j, :]).then_inc(S("gT_high"), 1)

                for j in range(FC):
                    act.wait_ge(S("sh_mm"), (c - 1) * 2 * FC + 2 * j + 1)
                    wait_past(act, S("gT"), (c - 1) * FC + max(j - 1, 0))
                    act.activation(sil[j % 2], bank(BANK_SH[2 * j]), ACT.Silu).then_inc(S("sil"), 1)
                    if j > 0:
                        high(j - 1)
                    if j in (0, 2):
                        late_row(c, j // 2, hm)
                high(FC - 1)
                late_row(c, 2, hm)
                late_row(c, 3, hm)

            def x_high(c):
                act.wait_ge(S("xT_in"), 16 * (c + 1))
                wait_past(act, S("z_mm"), c * HC)
                act.copy(xTs[0][:], xT[:]).then_inc(S("xT_high"), 1)

            def body(c, after, more):
                for j in range(HC + 1):
                    if j < HC:
                        act.wait_ge(S("z_mm"), c * HC + j + 1)
                        wait_past(act, S("so_mm"), 2 * (c - 1))
                        act.activation(hidden[:, j, :], bank(BANK_Z[j]), ACT.Silu, bias=b1c[:, j:j + 1])\
                           .then_inc(S("h2"), 1)
                    if j > 0:
                        act.wait_ge(S("h2"), c * HC + j)
                        wait_past(act, S("om_mm"), 2 * c)
                        act.copy(h2[0][:, j - 1, :], hidden[:, j - 1, :]).then_inc(S("h2_high"), 1)
                if after:
                    late(c)
                if not after:
                    act.wait_ge(S("s1_in"), 16)
                    act.copy(flat(s1T[0][:]), s1_raw).then_inc(S("s1_high"), 1)
                if more:
                    x_high(c + 1)
                for g, (dst, banks) in enumerate(((g1, (5, 6)), (g2, (7, 0)))):
                    for m in range(DC):
                        act.wait_ge(S("lin_mm"), c * 4 + 2 * g + m + 1)
                        wait_past(act, S("mT_mm"), 2 * c)
                        if g == 1:
                            wait_past(act, S("base_out"), (c - 1) * 16)
                        act.activation(block_of(dst, m), by_tile(bank(banks[m])), ACT.Sigmoid)\
                           .then_inc(S("gated"), 1)
                if after:
                    late_shared(c, hm)

            x_high(0)
            body(0, False, True)
            act.wait_ge(S("s2_in"), 16)
            act.copy(flat(s2T[0][:]), s2_raw).then_inc(S("s2_high"), 1)
            act.wait_ge(S("s2_low"), 1)
            body(1, True, True)
            with act.Fori(2, CHUNKS - 1) as c:
                body(c, True, True)
            body(CHUNKS - 1, True, False)
            late(CHUNKS)
            late_shared(CHUNKS, hm_last)

        @block.vector
        def _(dve):
            dve.wait_ge(S("route_const"), 1)

            def low(out, raw, high):
                return dve.tensor_tensor(out, raw, high.bitcast(F32), ALU.subtract)

            def x_low(c):
                dve.wait_ge(S("xT_high"), c + 1)
                low(xTs[1][:], xT[:], xTs[0][:]).then_inc(S("xT_low"), 1)

            def h2_low(c):
                for g in range(4):
                    dve.wait_ge(S("h2_high"), c * HC + 2 * g + 2)
                    part = slice(2 * g, 2 * g + 2)
                    low(flat(h2[1][:, part, :]), flat(hidden[:, part, :]), flat(h2[0][:, part, :]))\
                        .then_inc(S("h2_low"), 1)

            def route(c):
                lp = bank(2, TPC * E).rearrange("p (t e) -> p t e", t=TPC)
                dve.wait_ge(S("gate_mm"), c)
                dve.tensor_reduce(lmax[:], lp, AX, ALU.max).then_inc(S("lmax"), 1)
                dve.wait_ge(S("lmax"), c)
                dve.tensor_tensor(lg[:], lp, wide(lmax[:], E), ALU.subtract).then_inc(S("lg"), 1)
                dve.wait_ge(S("hT_high"), c)
                low(flat(hTs[1][:]), flat(hT[:]), flat(hTs[0][:])).then_inc(S("hT_low"), 1)
                dve.wait_ge(S("gate_exp"), c)
                dve.tensor_reduce(gsum[:], gate[:], AX, ALU.add).then_inc(S("gsum"), 1)
                dve.wait_ge(S("gsum"), c)
                dve.reciprocal(grec[:], gsum[:]).then_inc(S("grec"), 1)
                dve.wait_ge(S("grec"), c)
                dve.tensor_tensor(gate[:], gate[:], wide(grec[:], E), ALU.mult).then_inc(S("gate"), 1)
                wait_apart(dve, S("gate"), c, S("passed_dve"))
                for t in range(TPC):
                    ins = dve.max(top[:, t, :], gate[:, t, :])
                ins.then_inc(S("top"), 1)
                wait_apart(dve, S("top"), c, S("passed_dve"))
                for t in range(TPC):
                    dve.match_replace(out=rest[:, t, :], in_to_replace=top[:, t, :], in_values=gate[:, t, :],
                                      imm_value=-1.0)
                dve.tensor_reduce(wsum[:], top[:], AX, ALU.add).then_inc(S("rest"), 1)
                dve.wait_ge(S("rest"), c)
                dve.tensor_scalar(wsum[:], wsum[:], F32_EPS, None, ALU.max)
                dve.tensor_scalar(chosen_b[:], rest[:], 0.0, None, ALU.is_lt)
                dve.tensor_scalar(chosen[:], rest[:], 0.0, None, ALU.is_lt).then_inc(S("chosen"), 1)
                dve.wait_ge(S("chosen"), c)
                dve.reciprocal(wrec[:], wsum[:]).then_inc(S("wrec"), 1)
                dve.wait_ge(S("wrec"), c)
                dve.tensor_tensor(gate[:], gate[:], wide(wrec[:], E), ALU.mult).then_inc(S("weight"), 1)

            def slots_of(c):
                dve.wait_ge(S("rank_mm"), c)
                for t in range(TPC):
                    wait_past(dve, S("carry"), (c - 1) * TPC + t)
                    dve.tensor_tensor(rank[:, t, :], psum[1][:, D + t * E:D + (t + 1) * E], carry[:], ALU.add)\
                       .then_inc(S("rank"), 1)
                    dve.wait_ge(S("rank"), (c - 1) * TPC + t + 1)
                    dve.tensor_tensor(carry[:], carry[:], psum[1][:, t * E:(t + 1) * E], ALU.add)\
                       .then_inc(S("carry"), 1)
                dve.scalar_tensor_tensor(out=fits[:], in0=rank[:], scalar=float(CAP), in1=chosen[:],
                                         op0=ALU.is_lt, op1=ALU.mult)
                dve.tensor_tensor(slot[:], rank[:], slot_base[:].unsqueeze(1).to_broadcast([P, TPC, E]), ALU.add)\
                   .then_inc(S("fits"), 1)
                dve.wait_ge(S("fits"), c)
                dve.tensor_tensor(slot[:], slot[:], fits[:], ALU.mult).then_inc(S("slot"), 1)
                wait_apart(dve, S("slot"), c, S("passed_dve"))
                for t in range(TPC):
                    ins = dve.max(slot8[:, t, :], slot[:, t, :])
                ins.then_inc(S("slot8"), 1)
                dve.wait_ge(S("slot8"), c)
                dve.tensor_scalar(off[:], slot8[:], 1.0, float(OFF_LIST), ALU.is_lt, ALU.mult).then_inc(S("off"), 1)
                dve.wait_ge(S("off"), c)
                wait_past(dve, S("row_out0"), (c - 1) * 2 * TOPK * 16)
                wait_past(dve, S("row_out1"), (c - 1) * 2 * TOPK * 16)
                dve.scalar_tensor_tensor(out=index[:], in0=slot8[:], scalar=-1.0, in1=off[:], op0=ALU.add,
                                         op1=ALU.add).then_inc(S("index"), 1)

            def weights_of(c, t):
                if t == 0:
                    dve.wait_ge(S("weight"), c)
                    wait_past(dve, S("row_part"), (c - 1) * TPC)
                wait_past(dve, S("w8"), (c - 1) * TPC + t)
                for k in range(TOPK):
                    ins = dve.scalar_tensor_tensor(out=picked[:, k, :], in0=slot[:, t, :],
                                                   scalar=slot8[:, t, k:k + 1], in1=gate[:, t, :],
                                                   op0=ALU.is_equal, op1=ALU.mult, accum_out=w8[:, t, k:k + 1])
                ins.then_inc(S("w8"), 1)

            def merge(c):
                dve.wait_ge(S("gated"), 4 * c + 2)
                dve.tensor_tensor(g1[:], g1[:], swaT[:], ALU.mult)
                dve.wait_ge(S("gated"), 4 * c + 4)
                dve.tensor_tensor(g2[:], g2[:], om[:], ALU.mult).then_inc(S("parts"), 1)
                dve.wait_ge(S("parts"), c + 1)
                dve.tensor_tensor(g1[:], g1[:], g2[:], ALU.add).then_inc(S("merged"), 1)

            def gT_low(c, j):
                dve.wait_ge(S("gT_high"), (c - 1) * FC + j + 1)
                low(gTs[1][:, j, :], gT[:, j, :], gTs[0][:, j, :]).then_inc(S("gT_low"), 1)

            def shared(c, weights):
                for j in range(FC):
                    if j in weights:
                        weights_of(c, j)
                    dve.wait_ge(S("sil"), (c - 1) * FC + j + 1)
                    dve.wait_ge(S("sh_mm"), (c - 1) * 2 * FC + 2 * j + 2)
                    wait_past(dve, S("so_mm"), (c - 1) * 2)
                    dve.tensor_tensor(gT[:, j, :], bank(BANK_SH[2 * j + 1]), sil[j % 2], ALU.mult)\
                       .then_inc(S("gT"), 1)
                    if j > 0:
                        gT_low(c, j - 1)
                gT_low(c, FC - 1)

            def base_rows(c, merges, x2):
                dve.wait_ge(S("merged"), merges)
                for g in range(2):
                    dve.wait_ge(S("so_mm"), 2 * c - 1 + g)
                    wait_past(dve, S("base_out"), (c - 1) * 16)
                    dve.tensor_tensor(base[:, 2 * g:2 * g + 2, :], bank(6 + g).rearrange("p (t d) -> p t d", t=2),
                                      mod[:, 5, :].unsqueeze(1).to_broadcast([P, 2, D]), ALU.mult)\
                       .then_inc(S("base_raw"), 1)
                    dve.wait_ge(S("base_raw"), 2 * c - 1 + g)
                    dve.tensor_tensor(base[:, 2 * g:2 * g + 2, :], base[:, 2 * g:2 * g + 2, :],
                                      x2[:, 2 * g:2 * g + 2, :], ALU.add).then_inc(S("base"), 1)

            def residual(c, x2, hm, last):
                dve.wait_ge(S("x_in"), 16 * (c + 1))
                for g in range(2):
                    dve.wait_ge(S("mT_mm"), 2 * c + g + 1)
                    if g == 0 and not last:
                        wait_past(dve, S("base"), 2 * c)
                    dve.tensor_tensor(x2[:, 2 * g:2 * g + 2, :], bank(2 + g).rearrange("p (t d) -> p t d", t=2),
                                      mod[:, 2, :].unsqueeze(1).to_broadcast([P, 2, D]), ALU.mult)\
                       .then_inc(S("x2_raw"), 1)
                dve.wait_ge(S("x2_raw"), 2 * c + 2)
                dve.tensor_tensor(x2[:], x2[:], x[:], ALU.add).then_inc(S("x2"), 1)
                dve.wait_ge(S("x2"), c + 1)
                for t in range(TPC):
                    ins = dve.bn_stats(stats[:, t, :], x2[:, t, :])
                ins.then_inc(S("stats"), 1)
                wait_apart(dve, S("stats"), c + 1, S("passed_dve"))
                for t in range(TPC):
                    ins = dve.bn_aggr(moments[:, t, :], stats[:, t, :])
                ins.then_inc(S("moments"), 1)
                dve.wait_ge(S("moments"), c + 1)
                inverse_sqrt(dve, S("rstd"), c, rstd[:], moments[:, :, 1], half[:])
                if not last:
                    wait_past(dve, S("hT_mm"), 2 * c)
                    wait_past(dve, S("row_part"), c * TPC)
                for t in range(TPC):
                    ins = dve.tensor_scalar(hm[:, t, :], x2[:, t, :], moments[:, t, 0:1], rstd[:, t:t + 1],
                                            ALU.subtract, ALU.mult)
                ins.then_inc(S("hn"), 1)
                dve.wait_ge(S("hn"), c + 1)
                dve.tensor_tensor(hm[:], hm[:], rows_of(mod[:, 4, :]), ALU.mult).then_inc(S("hscaled"), 1)
                dve.wait_ge(S("hscaled"), c + 1)
                dve.tensor_tensor(hm[:], hm[:], rows_of(mod[:, 3, :]), ALU.add).then_inc(S("hm"), 1)

            def body(c, after, more):
                h2_low(c)
                if after:
                    route(c)
                for m in range(DC):
                    dve.wait_ge(S("om_mm"), 2 * c + m + 1)
                    wait_past(dve, S("parts"), c)
                    dve.tensor_scalar(block_of(om, m), by_tile(bank(3 + m)), b2c[:, m:m + 1], None, ALU.add)\
                       .then_inc(S("om"), 1)
                if after:
                    slots_of(c)
                if after and more:
                    shared(c, range(TPC))
                elif after:
                    weights_of(c, 0)
                else:
                    dve.wait_ge(S("s1_high"), 1)
                    low(flat(s1T[1][:]), s1_raw, flat(s1T[0][:])).then_inc(S("s1_low"), 1)
                merge(c)
                if not after:
                    dve.wait_ge(S("s2_high"), 1)
                    low(flat(s2T[1][:]), s2_raw, flat(s2T[0][:])).then_inc(S("s2_low"), 1)
                if more:
                    x_low(c + 1)
                if more:
                    if after:
                        base_rows(c, c + 1, x2)
                    residual(c, x2, hm, False)
                else:
                    weights_of(c, 1)
                    residual(c, x2_last, hm_last, True)
                    shared(c, (2, 3))
                    base_rows(c, c + 1, x2)

            x_low(0)
            body(0, False, True)
            body(1, True, True)
            with dve.Fori(2, CHUNKS - 1) as c:
                body(c, True, True)
            body(CHUNKS - 1, True, False)
            route(CHUNKS)
            slots_of(CHUNKS)
            shared(CHUNKS, range(TPC))
            base_rows(CHUNKS, CHUNKS, x2_last)

        @block.tensor
        def _(pe):
            def turn(out, src):
                return nc.tensor.transpose(out, src, ident[:])

            def turn_rows(c, hm):
                pe.wait_ge(S("hm"), c)
                for g in range(2):
                    for b in range(4):
                        k, t = b // 2, 2 * g + b % 2
                        ins = turn(psum[g][:, b * P:(b + 1) * P], hm[:, t, k * P:(k + 1) * P])
                    ins.then_inc(S("hT_mm"), 1)

            def gates(c):
                pe.wait_ge(S("hT"), 2 * c)
                for t in range(TPC):
                    for k in range(DC):
                        ins = mm(psum[2][:, t * E:(t + 1) * E], hT[:, k, t * P:(t + 1) * P], wgT[:, k, :],
                                 k == 0, k == DC - 1)
                ins.then_inc(S("gate_mm"), 1)

            def ranks(c):
                pe.wait_ge(S("chosen"), c)
                flat = chosen_b[:].rearrange("p t e -> p (t e)")
                mm(psum[1][:, 0:TPC * E], every[:], flat, True, True)
                mm(psum[1][:, D:D + TPC * E], before[:], flat, True, True).then_inc(S("rank_mm"), 1)

            def shared(c, tail, last=False):
                for i in range(2 * FC):
                    j, part = i // 2, i % 2
                    if last and i < 2:
                        pe.wait_ge(S("x2_raw"), 2 * c + i + 1)
                    if i == 0:
                        pe.wait_ge(S("lg"), c)
                        pe.wait_ge(S("hT_low"), c)
                    if not tail:
                        if i == 1:
                            pe.wait_ge(S("om"), 2 * c + 2)
                        if i in (3, 4, 5, 6):
                            pe.wait_ge(S("gated"), 4 * c + i - 2)
                    if i == 7:
                        pe.wait_ge(S("carry"), c * TPC)
                    if i >= 8:
                        pe.wait_ge(S("gT"), (c - 1) * FC + (i - 8) // 2 + 1)
                    col = (FC + j if part == 0 else j) * P
                    for k in range(DC):
                        ins = mm_split(nc, bank(BANK_SH[i]), cut(s1T, slice(None), k, slice(col, col + P)),
                                       cut(hTs, slice(None), k, slice(None)), k == 0, k == DC - 1)
                    ins.then_inc(S("sh_mm"), 1)
                for g in range(2):
                    for t in range(2):
                        for k in range(FC):
                            if g == 0 and t == 0:
                                pe.wait_ge(S("gT_low"), (c - 1) * FC + max(k, 2) + 1)
                            ins = mm_split(nc, psum[6 + g][:, t * D:(t + 1) * D],
                                           cut(gTs, slice(None), k, slice((2 * g + t) * P, (2 * g + t + 1) * P)),
                                           cut(s2T, slice(None), k, slice(None)), k == 0, k == FC - 1)
                    ins.then_inc(S("so_mm"), 1)

            def gate_of_attention(c, m):
                for k in range(DC):
                    ins = mm(bank(5 + m), linT[:, 0, k, m * P:(m + 1) * P], block_of(swaT, k), k == 0, k == DC - 1)
                ins.then_inc(S("lin_mm"), 1)

            def body(c, after, last=False):
                pe.wait_ge(S("xT_low"), c + 1)
                for j in range(HC):
                    if j in (2, 3):
                        wait_past(pe, S("x2_raw"), 2 * c - 3 + j)
                    if j == 6 and after:
                        wait_past(pe, S("base_raw"), 2 * c - 2)
                    for k in range(DC):
                        ins = mm_split(nc, bank(BANK_Z[j]), cut(w1T, slice(None), k, slice(j * P, (j + 1) * P)),
                                       [block_of(a, k) for a in xTs], k == 0, k == DC - 1)
                    ins.then_inc(S("z_mm"), 1)
                if not after:
                    pe.wait_ge(S("lin_in"), 16)
                pe.wait_ge(S("swaT_in"), 16 * (c + 1))
                pe.wait_ge(S("h2"), c * HC + 6)
                gate_of_attention(c, 0)
                if after:
                    turn_rows(c, hm)
                pe.wait_ge(S("h2"), c * HC + 7)
                gate_of_attention(c, 1)
                if after:
                    gates(c)
                pe.wait_ge(S("h2"), c * HC + 5)
                for m in range(DC):
                    for k in range(HC):
                        if m == 0 and k % 2 == 0:
                            pe.wait_ge(S("h2_low"), c * 4 + k // 2 + 1)
                        ins = mm_split(nc, bank(3 + m), cut(w2T, slice(None), k, slice(m * P, (m + 1) * P)),
                                       cut(h2, slice(None), k, slice(None)), k == 0, k == HC - 1)
                    ins.then_inc(S("om_mm"), 1)
                if after:
                    ranks(c)
                for k in range(DC):
                    pe.wait_ge(S("om"), 2 * c + k + 1)
                    for m in range(DC):
                        ins = mm(bank((7, 0)[m]), linT[:, 1, k, m * P:(m + 1) * P], block_of(om, k), k == 0, k == DC - 1)
                        if k == DC - 1:
                            ins.then_inc(S("lin_mm"), 1)
                if after and not last:
                    shared(c, False)
                if last:
                    pe.wait_ge(S("lg"), c)
                pe.wait_ge(S("merged"), c + 1)
                for g in range(2):
                    for b in range(4):
                        t, k = 2 * g + b // 2, b % 2
                        ins = turn(psum[2 + g][:, b * P:(b + 1) * P], g1[:, t, k * P:(k + 1) * P])
                    ins.then_inc(S("mT_mm"), 1)
                if last:
                    shared(c, False, last=True)

            body(0, False)
            pe.wait_ge(S("wg_in"), 16)
            pe.wait_ge(S("s1_low"), 1)
            pe.wait_ge(S("s2_low"), 1)
            body(1, True)
            with pe.Fori(2, CHUNKS - 1) as c:
                body(c, True)
            body(CHUNKS - 1, True, last=True)
            turn_rows(CHUNKS, hm_last)
            gates(CHUNKS)
            ranks(CHUNKS)
            shared(CHUNKS, True)


def expert_stage(nc, T, buf, psum, S):
    with ExitStack() as ctx:
        def sb(name, shape, dt=F32):
            return ctx.enter_context(nc.sbuf_tensor("c_" + name, shape, dt))

        mod, ident = buf["mod"], buf["ident"]
        w1 = [buf["early"][:, 0:DC * 2 * FFN].rearrange("p (k f) -> p k f", k=DC), sb("w1_1", [P, DC, 2 * FFN])]
        w2 = [sb(f"w2_{p}", [P, FC, D]) for p in range(2)]
        xa = [sb(f"xa{q}", [P, ROW]) for q in range(4)]
        xb = [sb(f"xb{q}", [CAP_B, ROW]) for q in range(4)]
        xT = [sb(f"xT{p}", [P, DC, CAP]) for p in range(2)]
        sil = sb("sil", [P, FC, CAP])
        gT = [sb(f"gT{p}", [P, FC, CAP]) for p in range(2)]
        yT = sb("yT", [P, DC, CAP])
        ya = sb("ya", [P, D])
        yb = sb("yb", [CAP_B, D])
        H = FC // 2
        Y_BANK = (5, 7)

        def mm(out, lhsT, rhs, first, last):
            return nc.tensor.matmul(out, lhsT, rhs, start=first, stop=last, skip_group_check=True)

        def experts(eng, step):
            for n in range(4):
                step(n, n, 1, n // 2 + 1)
            with eng.Fori(1, E // 4) as i:
                for q in range(4):
                    step(i * 4 + q, q, i + 1, i * 2 + q // 2 + 1)

        block = ctx.enter_context(nc.Block())

        @block.sync
        def _(sp):
            def load_w2(n, p):
                wait_past(sp, S("y_mm"), n - 1)
                sp.dma_start(w2[p][:], T["e2T"][bass.ds(n, 1)].rearrange("a p k f -> p (a k) f"))\
                  .then_inc(S(f"w2_in{p}"), 16)

            def step(n, q, rows_in, weights_in):
                p = q % 2
                wait_past(sp, S("added"), (n - 3) * 32)
                sp.dma_start(xa[q][:], T["slots"][bass.ds(n * CAP, P), :]).then_inc(S(f"x_in{q}"), 16)
                sp.dma_start(xb[q][:], T["slots"][bass.ds(n * CAP + P, CAP_B), :]).then_inc(S(f"x_in{q}"), 16)
                if not isinstance(n, int) or n >= 1:
                    wait_past(sp, S("h_mm"), (n - 1) * 4)
                    sp.dma_start(w1[p][:], T["e1T"][bass.ds(n, 1)].rearrange("a p k f -> p (a k) f"))\
                      .then_inc(S(f"w1_in{p}"), 16)
                if not isinstance(n, int) or n >= 1:
                    load_w2(n - 1, 1 - p)

            experts(sp, step)
            load_w2(E - 1, 1)

        @block.scalar
        def _(act):
            def y_cols(n):
                for m in range(DC):
                    act.wait_ge(S("y_mm"), n + 1)
                    wait_past(act, S("yR_mm"), n)
                    ins = act.copy(yT[:, m, :], psum[Y_BANK[m]][:, 0:CAP])
                ins.then_inc(S("yT"), 1)

            def step(n, q, rows_in, weights_in):
                p = q % 2
                act.wait_ge(S("xT_mm"), n + 1)
                wait_past(act, S("h_mm"), (n - 1) * 4)
                act.copy(flat(xT[p][:]), psum[0][:, 0:DC * CAP]).then_inc(S("xT"), 1)
                if not isinstance(n, int) or n >= 1:
                    y_cols(n - 1)
                for g in range(2):
                    act.wait_ge(S("h_mm"), 4 * n + 2 * g + 1)
                    wait_past(act, S("gT"), 2 * n - 1 + g)
                    act.activation(flat(sil[:, g * H:(g + 1) * H, :]), psum[1 + 2 * g][:, 0:H * CAP], ACT.Silu)\
                       .then_inc(S("sil"), 1)

            experts(act, step)
            y_cols(E - 1)

        @block.vector
        def _(dve):
            def y_rows(n, q):
                dve.wait_ge(S("yR_mm"), n + 1)
                wait_past(dve, S("added"), n * 32)
                dve.scalar_tensor_tensor(out=ya[:], in0=psum[6][:, 0:D], scalar=xa[q][:, D:D + 1], in1=mod[:, 5, :],
                                         op0=ALU.mult, op1=ALU.mult)
                dve.scalar_tensor_tensor(out=yb[:], in0=psum[6][0:CAP_B, D:2 * D], scalar=xb[q][:, D:D + 1],
                                         in1=mod[0:CAP_B, 5, :], op0=ALU.mult, op1=ALU.mult).then_inc(S("y"), 1)

            def step(n, q, rows_in, weights_in):
                p = q % 2
                for g in range(2):
                    dve.wait_ge(S("sil"), 2 * n + g + 1)
                    dve.wait_ge(S("h_mm"), 4 * n + 2 * g + 2)
                    wait_past(dve, S("y_mm"), n - 1)
                    dve.tensor_tensor(flat(gT[p][:, g * H:(g + 1) * H, :]), psum[2 + 2 * g][:, 0:H * CAP],
                                      flat(sil[:, g * H:(g + 1) * H, :]), ALU.mult).then_inc(S("gT"), 1)
                if not isinstance(n, int) or n >= 1:
                    y_rows(n - 1, (q - 1) % 4)

            experts(dve, step)
            y_rows(E - 1, 3)

        @block.gpsimd
        def _(pool):
            last_row = pool.to_reg(TOKENS + CAP - 1)

            def step(n, q, rows_in, weights_in):
                wait_past(pool, S("added"), n * 32)
                wait_apart(pool, S("y"), n + 1, S("passed_pool"))
                for y, x in ((ya, xa[q]), (yb, xb[q])):
                    pool.indirect_dma_start(
                        out=T["out"], out_offset=bass.IndirectOffsetOnAxis(ap=x[:, D + 1:D + 2].bitcast(U32), axis=0),
                        in_=y[:], in_offset=None, bounds_check=last_row, oob_is_err=True,
                        compute_op=ALU.add).then_inc(S("added"), 16)

            experts(pool, step)
            pool.wait_ge(S("added"), E * 32)

        @block.tensor
        def _(pe):
            def turn_x(n, q, rows_in):
                pe.wait_ge(S(f"x_in{q}"), rows_in * 32)
                wait_past(pe, S("xT"), n)
                for k in range(DC):
                    nc.tensor.transpose(psum[0][:, k * CAP:k * CAP + P], xa[q][:, k * P:(k + 1) * P], ident[:])
                    ins = nc.tensor.transpose(psum[0][:, k * CAP + P:(k + 1) * CAP], xb[q][:, k * P:(k + 1) * P],
                                              ident[0:CAP_B, 0:CAP_B])
                ins.then_inc(S("xT_mm"), 1)

            def up(n, p, weights_in):
                wait_past(pe, S(f"w1_in{p}"), (weights_in - (1 - p)) * 16)
                pe.wait_ge(S("xT"), n + 1)
                for g in range(2):
                    for part in range(2):
                        wait_past(pe, S("sil" if part == 0 else "gT"), 2 * n - 1 + g)
                        for j in range(H):
                            col = ((FC if part == 0 else 0) + g * H + j) * P
                            for k in range(DC):
                                ins = mm(psum[1 + 2 * g + part][:, j * CAP:(j + 1) * CAP], w1[p][:, k, col:col + P],
                                         xT[p][:, k, :], k == 0, k == DC - 1)
                        ins.then_inc(S("h_mm"), 1)

            def down(n, p, weights_in):
                pe.wait_ge(S(f"w2_in{p}"), weights_in * 16)
                wait_past(pe, S("yT"), n)
                for g in range(2):
                    pe.wait_ge(S("gT"), 2 * n + g + 1)
                    for m in range(DC):
                        for k in range(g * H, (g + 1) * H):
                            ins = mm(psum[Y_BANK[m]][:, 0:CAP], w2[p][:, k, m * P:(m + 1) * P], gT[p][:, k, :],
                                     k == 0, k == FC - 1)
                ins.then_inc(S("y_mm"), 1)

            def turn_y(n):
                pe.wait_ge(S("yT"), n + 1)
                wait_past(pe, S("y"), n)
                for k in range(DC):
                    nc.tensor.transpose(psum[6][:, k * P:(k + 1) * P], yT[:, k, 0:P], ident[:])
                    ins = nc.tensor.transpose(psum[6][0:CAP_B, D + k * P:D + (k + 1) * P], yT[:, k, P:CAP], ident[:])
                ins.then_inc(S("yR_mm"), 1)

            def step(n, q, rows_in, weights_in):
                p = q % 2
                late = not isinstance(n, int) or n >= 1
                turn_x(n, q, rows_in)
                if late:
                    down(n - 1, 1 - p, weights_in - (1 - p))
                up(n, p, weights_in)
                if late:
                    turn_y(n - 1)

            experts(pe, step)
            down(E - 1, 1, E // 2)
            turn_y(E - 1)


def build(nc, T):
    def run(stage, prefix, buf):
        sems = Sems(nc, prefix)
        stage(nc, T, buf, psum, sems)
        sems.clear()

    with ExitStack() as ctx:
        psum = [ctx.enter_context(nc.psum_tensor(f"bank{b}", [P, CH], F32)) for b in range(8)]
        with ExitStack() as inner:
            buf = shared_buffers(nc, ctx, inner)
            run(memory_stage, "a_", buf)
            run(token_stage, "b_", buf)
        run(expert_stage, "c_", buf)


def kernel(**inputs):
    import numpy as np
    import concourse.bacc as bacc
    from concourse.bass_utils import run_bass_kernel_spmd

    a = {k: np.asarray(v) for k, v in inputs.items()}

    def split(w):
        k, n = w.shape
        return np.ascontiguousarray(w.reshape(k // P, P, n).transpose(1, 0, 2))

    w = {k[len("L0_"):]: v for k, v in a.items()}
    e1, e2 = w["ffn_expert_w1"], w["ffn_expert_w2"]
    arrays = {
        "x": w["attn_x"].reshape(TOKENS, D),
        "mem": w["attn_mem"],
        "wqkT": np.ascontiguousarray(np.stack([split(w["attn_wq"].T), split(w["attn_wk"].T)], axis=1)),
        "wvT": split(w["attn_wv"].T),
        "woT": split(w["attn_wo"].T),
        "w1T": split(w["attn_w1"].T),
        "w2T": split(w["attn_w2"].T),
        "w2n": split(w["attn_w2"]),
        "b1row": np.ascontiguousarray(np.broadcast_to(w["attn_b1"][None, :], (P, HID))),
        "b2row": np.ascontiguousarray(np.broadcast_to(w["attn_b2"][None, :], (P, D))),
        "b1c": np.ascontiguousarray(w["attn_b1"].reshape(HC, P).T),
        "b2c": np.ascontiguousarray(w["attn_b2"].reshape(DC, P).T),
        "alpha": np.ascontiguousarray(np.broadcast_to(w["attn_alpha"].reshape(1, 1), (P, 1))),
        "theta": np.ascontiguousarray(np.broadcast_to(w["attn_theta"].reshape(1, 1), (P, 1))),
        "linT": np.ascontiguousarray(np.stack([split(w["attn_lin1"].T), split(w["attn_lin2"].T)], axis=1)),
        "wgT": split(w["ffn_wg"].T),
        "s1T": split(w["ffn_shared_w1"].T),
        "s2T": split(w["ffn_shared_w2"].T),
        "e1T": np.ascontiguousarray(e1.reshape(E, 2 * FFN, DC, P).transpose(0, 3, 2, 1)),
        "e2T": np.ascontiguousarray(e2.reshape(E, D, FC, P).transpose(0, 3, 2, 1)),
        "c": np.ascontiguousarray(w["c"].reshape(DC, P).T),
        "wmod": split(w["wmod"]),
    }
    nc = bacc.Bacc("TRN2", target_bir_lowering=False, num_devices=1)
    T = {k: nc.dram_tensor("in_" + k, v.shape, mybir.dt.from_np(v.dtype), kind="ExternalInput").ap()
         for k, v in arrays.items()}
    T["out"] = nc.dram_tensor("out_rows", (TOKENS + CAP, D), F32, kind="ExternalOutput").ap()
    T["xT"] = nc.dram_tensor("xT_tiles", (TOKENS, D), F32, kind="Internal").ap()
    T["swaT"] = nc.dram_tensor("swaT_tiles", (TOKENS, D), F32, kind="Internal").ap()
    T["slots"] = nc.dram_tensor("slots", (E * CAP, ROW), F32, kind="Internal").ap()
    build(nc, T)
    r = run_bass_kernel_spmd(nc, [{"in_" + k: v for k, v in arrays.items()}], core_ids=[0])
    return r.results[0]["out_rows"][:TOKENS].reshape(1, TOKENS, D)
```
